# Optimizing a Trainium2 kernel written in Bass

```python
import numpy as np
import jax
import jax.numpy as jnp

def _softmax(x, axis=-1):
    return jax.nn.softmax(x, axis=axis)

def _gelu(x):
    return jax.nn.gelu(x, approximate=True)

def _silu(x):
    return jax.nn.silu(x)

def _sigmoid(x):
    return jax.nn.sigmoid(x)

def _layernorm(x, axis=-1, eps=1e-05):
    m = jnp.mean(x, axis=axis, keepdims=True)
    v = jnp.var(x, axis=axis, keepdims=True)
    return (x - m) / jnp.sqrt(v + eps)

def _scatter_add(tgt, idx, src, axis=0):
    return tgt.at[idx].add(src)

def _segment_sum(src, seg, n):
    return jax.ops.segment_sum(src, seg, n)
kernel_name = 'mk_sandwich_d1_jaxref_r8_d1d55c'

def setup_inputs(seed: int=0):
    np.random.seed(seed)
    _w = jnp.asarray

    def _L0_attn_setup():
        import math
        import jax, jax.numpy as jnp
        import numpy as np
        D_MODEL = 128
        N_HEADS = 16
        D_K = D_MODEL // N_HEADS
        D_C = 32
        B, S = (2, 256)
        key = jax.random.key(seed)
        ks = jax.random.split(key, 7)
        sd = lambda fan_in: 1.0 / math.sqrt(fan_in)
        return {'x': jax.random.normal(ks[0], (B, S, D_MODEL), dtype=jnp.float32), 'W_dq': jax.random.uniform(ks[1], (D_MODEL, D_C), minval=-sd(D_MODEL), maxval=sd(D_MODEL), dtype=jnp.float32), 'W_uq': jax.random.uniform(ks[2], (D_C, N_HEADS * D_K), minval=-sd(D_C), maxval=sd(D_C), dtype=jnp.float32), 'W_dkv': jax.random.uniform(ks[3], (D_MODEL, D_C), minval=-sd(D_MODEL), maxval=sd(D_MODEL), dtype=jnp.float32), 'W_uk': jax.random.uniform(ks[4], (D_C, N_HEADS * D_K), minval=-sd(D_C), maxval=sd(D_C), dtype=jnp.float32), 'W_uv': jax.random.uniform(ks[5], (D_C, N_HEADS * D_K), minval=-sd(D_C), maxval=sd(D_C), dtype=jnp.float32), 'W_o': jax.random.uniform(ks[6], (N_HEADS * D_K, D_MODEL), minval=-sd(N_HEADS * D_K), maxval=sd(N_HEADS * D_K), dtype=jnp.float32)}
    _L0_attn_in = _L0_attn_setup()

    def _L0_ffn_setup():
        import jax, jax.numpy as jnp
        import numpy as np
        DIM = 128
        DEPTH = 2
        HEADS = 8
        DIM_HEAD = 64
        WINDOW = 64
        INNER = HEADS * DIM_HEAD
        HID = int(DIM * 4 * 2 / 3)
        B, N = (2, 1024)
        QK_SCALE = 8.0

        def shift_token(t):
            t1, t2 = jnp.split(t, 2, axis=-1)
            t2 = jnp.pad(t2, ((0, 0), (1, 0), (0, 0)))[:, :-1]
            return jnp.concatenate([t1, t2], axis=-1)

        def l2norm(t):
            return t / jnp.clip(jnp.linalg.norm(t, axis=-1, keepdims=True), 1e-12)

        def rotate_half(x):
            x1, x2 = jnp.split(x, 2, axis=-1)
            return jnp.concatenate([-x2, x1], axis=-1)

        def rotary_xpos(q, k):
            n = q.shape[-2]
            half_idx = jnp.arange(0, DIM_HEAD, 2, dtype=jnp.float32)
            inv_freq = 1.0 / 10000.0 ** (half_idx / DIM_HEAD)
            t = jnp.arange(n, dtype=jnp.float32)
            freqs = t[:, None] * inv_freq[None, :]
            freqs = jnp.concatenate([freqs, freqs], axis=-1)
            base = (half_idx + 0.4 * DIM_HEAD) / (1.4 * DIM_HEAD)
            power = (t - n // 2) / float(WINDOW // 2)
            scale = base[None, :] ** power[:, None]
            scale = jnp.concatenate([scale, scale], axis=-1)
            cos, sin = (jnp.cos(freqs), jnp.sin(freqs))
            q = q * cos * scale + rotate_half(q) * sin * scale
            k = k * cos / scale + rotate_half(k) * sin / scale
            return (q, k)

        def local_attention(q, k, v):
            b, h, n, d = q.shape
            w = n // WINDOW
            bq = q.reshape(b, h, w, WINDOW, d) * QK_SCALE
            bk = k.reshape(b, h, w, WINDOW, d)
            bv = v.reshape(b, h, w, WINDOW, d)

            def look_around(t):
                p = jnp.pad(t, ((0, 0), (0, 0), (1, 0), (0, 0), (0, 0)))
                return jnp.concatenate([p[:, :, :w], p[:, :, 1:]], axis=3)
            bk, bv = (look_around(bk), look_around(bv))
            bt = jnp.arange(n).reshape(w, WINDOW)
            btp = jnp.pad(bt, ((1, 0), (0, 0)), constant_values=-1)
            btk = jnp.concatenate([btp[:w], btp[1:]], axis=1)
            sim = jnp.einsum('bhwid,bhwjd->bhwij', bq, bk)
            i = bt[:, :, None]
            j = btk[:, None, :]
            mask = (i < j) | (i > j + WINDOW) | (j == -1)
            sim = jnp.where(mask, -jnp.finfo(sim.dtype).max, sim)
            attn = jax.nn.softmax(sim, axis=-1)
            out = jnp.einsum('bhwij,bhwjd->bhwid', attn, bv)
            return out.reshape(b, h, n, d)

        def _layer(x, wqkv, qs, ksc, wo, lg, lb, w1, b1, w2, b2):
            b, n, _ = x.shape
            h = shift_token(x)
            qkv = h @ wqkv
            q, k, v = jnp.split(qkv, 3, axis=-1)
            to_heads = lambda t: t.reshape(b, n, HEADS, DIM_HEAD).transpose(0, 2, 1, 3)
            q, k, v = (to_heads(q), to_heads(k), to_heads(v))
            q = l2norm(q) * qs
            k = l2norm(k) * ksc
            q, k = rotary_xpos(q, k)
            o = local_attention(q, k, v)
            o = o.transpose(0, 2, 1, 3).reshape(b, n, INNER)
            x = x + o @ wo
            h = shift_token(x)
            mu = h.mean(-1, keepdims=True)
            var = h.var(-1, keepdims=True)
            h = (h - mu) / jnp.sqrt(var + 1e-05) * lg + lb
            h = h @ w1 + b1
            a, g = jnp.split(h, 2, axis=-1)
            h = a * jax.nn.gelu(g, approximate=False)
            x = x + h @ w2 + b2
            return x
        key = jax.random.key(seed)
        ks = jax.random.split(key, 6)
        return {'x': jax.random.normal(ks[0], (B, N, DIM), jnp.float32), 'wqkv': jax.random.normal(ks[1], (DEPTH, DIM, 3 * INNER), jnp.float32) * 0.02, 'q_scale': jnp.ones((DEPTH, DIM_HEAD), jnp.float32), 'k_scale': jnp.ones((DEPTH, DIM_HEAD), jnp.float32), 'wo': jax.random.normal(ks[2], (DEPTH, INNER, DIM), jnp.float32) * 0.02, 'ln_g': jnp.ones((DEPTH, DIM), jnp.float32), 'ln_b': jnp.zeros((DEPTH, DIM), jnp.float32), 'w1': jax.random.normal(ks[3], (DEPTH, DIM, 2 * HID), jnp.float32) * 0.02, 'b1': jnp.zeros((DEPTH, 2 * HID), jnp.float32), 'w2': jax.random.normal(ks[4], (DEPTH, HID, DIM), jnp.float32) * 0.02, 'b2': jnp.zeros((DEPTH, DIM), jnp.float32)}
    _L0_ffn_in = _L0_ffn_setup()
    _d = {'L0_attn_x': _L0_attn_in['x'], 'L0_attn_W_dq': _L0_attn_in['W_dq'], 'L0_attn_W_uq': _L0_attn_in['W_uq'], 'L0_attn_W_dkv': _L0_attn_in['W_dkv'], 'L0_attn_W_uk': _L0_attn_in['W_uk'], 'L0_attn_W_uv': _L0_attn_in['W_uv'], 'L0_attn_W_o': _L0_attn_in['W_o'], 'L0_ffn_wqkv': _L0_ffn_in['wqkv'], 'L0_ffn_q_scale': _L0_ffn_in['q_scale'], 'L0_ffn_k_scale': _L0_ffn_in['k_scale'], 'L0_ffn_wo': _L0_ffn_in['wo'], 'L0_ffn_ln_g': _L0_ffn_in['ln_g'], 'L0_ffn_ln_b': _L0_ffn_in['ln_b'], 'L0_ffn_w1': _L0_ffn_in['w1'], 'L0_ffn_b1': _L0_ffn_in['b1'], 'L0_ffn_w2': _L0_ffn_in['w2'], 'L0_ffn_b2': _L0_ffn_in['b2']}
    _x0 = _d['L0_attn_x']
    _d['L0_attn_x'] = jax.random.normal(jax.random.fold_in(jax.random.key(seed), 1), (4, 1024, 128), dtype=_x0.dtype)
    del _x0
    return _d

def reference(L0_attn_x, L0_attn_W_dq, L0_attn_W_uq, L0_attn_W_dkv, L0_attn_W_uk, L0_attn_W_uv, L0_attn_W_o, L0_ffn_wqkv, L0_ffn_q_scale, L0_ffn_k_scale, L0_ffn_wo, L0_ffn_ln_g, L0_ffn_ln_b, L0_ffn_w1, L0_ffn_b1, L0_ffn_w2, L0_ffn_b2):

    def _L0_attn_ref(x, W_dq, W_uq, W_dkv, W_uk, W_uv, W_o):
        import math
        import jax, jax.numpy as jnp
        import numpy as np
        D_MODEL = 128
        N_HEADS = 16
        D_K = D_MODEL // N_HEADS
        D_C = 32
        B, S = (2, 256)
        Bx, Sx, _ = x.shape
        c_q = x @ W_dq
        Q = (c_q @ W_uq).reshape(Bx, Sx, N_HEADS, D_K)
        c_kv = x @ W_dkv
        K = (c_kv @ W_uk).reshape(Bx, Sx, N_HEADS, D_K)
        V = (c_kv @ W_uv).reshape(Bx, Sx, N_HEADS, D_K)
        scores = jnp.einsum('bqhd,bkhd->bhqk', Q, K) / math.sqrt(D_K)
        causal = jnp.tril(jnp.ones((Sx, Sx), dtype=bool))
        scores = jnp.where(causal, scores, -jnp.inf)
        attn = jax.nn.softmax(scores, axis=-1)
        out = jnp.einsum('bhqk,bkhd->bqhd', attn, V).reshape(Bx, Sx, N_HEADS * D_K)
        return out @ W_o

    def _L0_ffn_ref(x, wqkv, q_scale, k_scale, wo, ln_g, ln_b, w1, b1, w2, b2):
        import jax, jax.numpy as jnp
        import numpy as np
        DIM = 128
        DEPTH = 2
        HEADS = 8
        DIM_HEAD = 64
        WINDOW = 64
        INNER = HEADS * DIM_HEAD
        HID = int(DIM * 4 * 2 / 3)
        B, N = (2, 1024)
        QK_SCALE = 8.0

        def shift_token(t):
            t1, t2 = jnp.split(t, 2, axis=-1)
            t2 = jnp.pad(t2, ((0, 0), (1, 0), (0, 0)))[:, :-1]
            return jnp.concatenate([t1, t2], axis=-1)

        def l2norm(t):
            return t / jnp.clip(jnp.linalg.norm(t, axis=-1, keepdims=True), 1e-12)

        def rotate_half(x):
            x1, x2 = jnp.split(x, 2, axis=-1)
            return jnp.concatenate([-x2, x1], axis=-1)

        def rotary_xpos(q, k):
            n = q.shape[-2]
            half_idx = jnp.arange(0, DIM_HEAD, 2, dtype=jnp.float32)
            inv_freq = 1.0 / 10000.0 ** (half_idx / DIM_HEAD)
            t = jnp.arange(n, dtype=jnp.float32)
            freqs = t[:, None] * inv_freq[None, :]
            freqs = jnp.concatenate([freqs, freqs], axis=-1)
            base = (half_idx + 0.4 * DIM_HEAD) / (1.4 * DIM_HEAD)
            power = (t - n // 2) / float(WINDOW // 2)
            scale = base[None, :] ** power[:, None]
            scale = jnp.concatenate([scale, scale], axis=-1)
            cos, sin = (jnp.cos(freqs), jnp.sin(freqs))
            q = q * cos * scale + rotate_half(q) * sin * scale
            k = k * cos / scale + rotate_half(k) * sin / scale
            return (q, k)

        def local_attention(q, k, v):
            b, h, n, d = q.shape
            w = n // WINDOW
            bq = q.reshape(b, h, w, WINDOW, d) * QK_SCALE
            bk = k.reshape(b, h, w, WINDOW, d)
            bv = v.reshape(b, h, w, WINDOW, d)

            def look_around(t):
                p = jnp.pad(t, ((0, 0), (0, 0), (1, 0), (0, 0), (0, 0)))
                return jnp.concatenate([p[:, :, :w], p[:, :, 1:]], axis=3)
            bk, bv = (look_around(bk), look_around(bv))
            bt = jnp.arange(n).reshape(w, WINDOW)
            btp = jnp.pad(bt, ((1, 0), (0, 0)), constant_values=-1)
            btk = jnp.concatenate([btp[:w], btp[1:]], axis=1)
            sim = jnp.einsum('bhwid,bhwjd->bhwij', bq, bk)
            i = bt[:, :, None]
            j = btk[:, None, :]
            mask = (i < j) | (i > j + WINDOW) | (j == -1)
            sim = jnp.where(mask, -jnp.finfo(sim.dtype).max, sim)
            attn = jax.nn.softmax(sim, axis=-1)
            out = jnp.einsum('bhwij,bhwjd->bhwid', attn, bv)
            return out.reshape(b, h, n, d)

        def _layer(x, wqkv, qs, ksc, wo, lg, lb, w1, b1, w2, b2):
            b, n, _ = x.shape
            h = shift_token(x)
            qkv = h @ wqkv
            q, k, v = jnp.split(qkv, 3, axis=-1)
            to_heads = lambda t: t.reshape(b, n, HEADS, DIM_HEAD).transpose(0, 2, 1, 3)
            q, k, v = (to_heads(q), to_heads(k), to_heads(v))
            q = l2norm(q) * qs
            k = l2norm(k) * ksc
            q, k = rotary_xpos(q, k)
            o = local_attention(q, k, v)
            o = o.transpose(0, 2, 1, 3).reshape(b, n, INNER)
            x = x + o @ wo
            h = shift_token(x)
            mu = h.mean(-1, keepdims=True)
            var = h.var(-1, keepdims=True)
            h = (h - mu) / jnp.sqrt(var + 1e-05) * lg + lb
            h = h @ w1 + b1
            a, g = jnp.split(h, 2, axis=-1)
            h = a * jax.nn.gelu(g, approximate=False)
            x = x + h @ w2 + b2
            return x
        for l in range(DEPTH):
            x = _layer(x, wqkv[l], q_scale[l], k_scale[l], wo[l], ln_g[l], ln_b[l], w1[l], b1[l], w2[l], b2[l])
        return x
    x = L0_attn_x
    x = x + _layernorm(_L0_attn_ref(_layernorm(x, axis=-1), L0_attn_W_dq, L0_attn_W_uq, L0_attn_W_dkv, L0_attn_W_uk, L0_attn_W_uv, L0_attn_W_o), axis=-1)
    x = x + _layernorm(_L0_ffn_ref(_layernorm(x, axis=-1), L0_ffn_wqkv, L0_ffn_q_scale, L0_ffn_k_scale, L0_ffn_wo, L0_ffn_ln_g, L0_ffn_ln_b, L0_ffn_w1, L0_ffn_b1, L0_ffn_w2, L0_ffn_b2), axis=-1)
    return x

_drawn_inputs = setup_inputs


def setup_inputs(seed=0):
    import zlib

    import numpy as np

    out = dict(_drawn_inputs(seed))
    spreads = {'L0_ffn_q_scale': (1.0, 0.6),
     'L0_ffn_k_scale': (1.0, 0.6),
     'L0_ffn_ln_g': (1.0, 0.6),
     'L0_ffn_ln_b': (0.0, 0.8),
     'L0_ffn_b1': (0.0, 0.8),
     'L0_ffn_b2': (0.0, 0.8)}
    factors = {'L0_ffn_w1': 7.511, 'L0_ffn_w2': 7.395}
    for name, (base, spread) in spreads.items():
        noise = np.random.default_rng([zlib.crc32(name.encode()), seed]).standard_normal(out[name].shape)
        drawn = base * np.exp(spread * noise) if base else spread * noise
        out[name] = jnp.asarray(drawn.astype(out[name].dtype))
    for name, factor in factors.items():
        out[name] = (out[name] * factor).astype(out[name].dtype)
    return out
```

```python
from contextlib import ExitStack

import numpy as np
import concourse.bass as bass
from concourse import mybir

F32 = mybir.dt.float32
BF16 = mybir.dt.bfloat16
ALU = mybir.AluOpType
ACT = mybir.ActivationFunctionType
AX = mybir.AxisListType

B, S, D = 4, 1024, 128
P = 128
NT = B * S // P
TB = S // P
NCH = NT // 4
NH, DK, DC = 16, 8, 32
HG = 4
NG = NH // HG
NPAIR = 9
ROWS = NPAIR * DK
KROWS = 96
NM = 3 * HG
VA = DK + 1
VPAD = 32 - VA
SCALE0 = float(1.0 / np.sqrt(np.float32(DK)))
NEG = -1e30
EPS = 1e-5
DEPTH, HEADS, DH, WIN = 2, 8, 64, 64
INNER = HEADS * DH
QK_SCALE = 8.0
KEYS = 3 * WIN
HID = int(D * 4 * 2 / 3)
HC = 114
HCS = [HC, HC, HID - 2 * HC]


def ge(eng, sem, count):
    if isinstance(count, int) and count <= 0:
        return
    eng.wait_ge(sem, count)


def carry_wait(dve, sb):
    dve.memset(sb["spare"], 0.0)


def project(nc, io, sb):
    with ExitStack() as ctx:
        def tile(name, shape, dt=F32):
            return ctx.enter_context(nc.sbuf_tensor(name, shape, dt))

        def sem(name):
            return ctx.enter_context(nc.semaphore(name))

        stats = tile("p_stats", [P, 2, 4, 6])
        mv = tile("p_mv", [P, 2, 4, 2])
        rstd = tile("p_rstd", [P, 2, 4])
        ve = tile("p_ve", [P, 2, 4])
        xn = tile("p_xn", [P, 2, 4, D])
        xnT = tile("p_xnT", [P, 2, 512])
        cT = tile("p_cT", [2 * DC, 2, 512])
        rem = tile("p_rem", [P, 2, 2, 512])
        parts = tile("p_parts", [P, 2, 2, 3, 512], BF16)
        psT = ctx.enter_context(nc.psum_tensor("p_psT", [P, 2, 512], F32))
        psC = ctx.enter_context(nc.psum_tensor("p_psC", [P, 2, 512], F32))
        psQK = ctx.enter_context(nc.psum_tensor("p_psQK", [P, 2, 512], F32))
        psV = ctx.enter_context(nc.psum_tensor("p_psV", [P, 512], F32))

        x_first, x_rest, w_in = sem("x_first"), sem("x_rest"), sem("w_in")
        stats_done, mean_done, var_done, rstd_done = sem("stats_done"), sem("mean_done"), sem("var_done"), sem("rstd_done")
        xn_done, xnT_done, xnT_copied = sem("xn_done"), sem("xnT_done"), sem("xnT_copied")
        c_done, c_copied = sem("c_done"), sem("c_copied")
        qk_done, v_done, v_copied = sem("qk_done"), sem("v_done"), sem("v_copied")
        hi_done, rem1_done, mid_done, parts_done = sem("hi_done"), sem("rem1_done"), sem("mid_done"), sem("parts_done")
        parts_out = [sem("parts_out0"), sem("parts_out1")]
        ones_set = sem("ones_set")

        block = ctx.enter_context(nc.Block())
        x_v = io["x"].rearrange("b (t p) c -> p (b t) c", p=P)

        @block.sync
        def _(sp):
            sp.dma_start(sb["x"][:, 0:4, :], x_v[:, 0:4, :]).then_inc(x_first, 16)
            sp.dma_start(sb["x"][:, 4:NT, :], x_v[:, 4:NT, :]).then_inc(x_rest, 16)
            with sp.Fori(0, NCH // 2) as pair:
                for par in range(2):
                    c = pair * 2 + par
                    sp.wait_ge(parts_done, 2 * c + 2)
                    for w, name in ((0, "q_parts"), (1, "k_parts")):
                        for a in range(3):
                            sp.dma_start(io[name][pair, :, a, :, 512 * par:512 * par + 512],
                                         parts[:, par, w, a, :]).then_inc(parts_out[par], 16)
            for par in range(2):
                sp.wait_ge(parts_out[par], 16 * 6 * (NCH // 2))

        @block.scalar
        def _(act):
            loads = [(sb["ident"], io["c_ident"]), (sb["w_down"][:, 0:DC], io["W_dq"]), (sb["w_down"][:, DC:2 * DC], io["W_dkv"]),
                     (sb["w_uq"][0:DC, :], io["W_uq"]), (sb["w_ukv"][DC:2 * DC, 0:D], io["W_uk"]),
                     (sb["w_ukv"][DC:2 * DC, D:2 * D], io["W_uv"])]
            for dst, src in loads:
                act.dma_start(dst, src).then_inc(w_in, 16)

            def copy_xnT(c, par):
                act.wait_ge(xnT_done, c + 1)
                ge(act, c_done, c - 1)
                act.activation(xnT[:, par, :], psT[:, par, :], ACT.Copy).then_inc(xnT_copied, 1)

            def copy_c(c, par):
                act.wait_ge(c_done, c + 1)
                ge(act, v_done, c - 1)
                act.activation(cT[:, par, :], psC[0:2 * DC, par, :], ACT.Copy).then_inc(c_copied, 1)

            def copy_v(c, par):
                act.wait_ge(v_done, c + 1)
                for g in range(NG):
                    src = psV[:, :].rearrange("p (t g j d) -> p g t j d", t=4, g=NG, j=HG)[:, g]
                    dst = sb["v_all"][:, g, bass.ts(c, 4), :].rearrange("p t (j a) -> p t j a", a=VA)[:, :, :, 0:DK]
                    i = act.activation(dst, src, ACT.Copy)
                i.then_inc(v_copied, 1)

            act.wait_ge(ones_set, 3)
            copy_xnT(0, 0)
            copy_c(0, 0)
            copy_v(0, 0)
            copy_xnT(1, 1)
            copy_c(1, 1)
            copy_v(1, 1)
            with act.Fori(1, NCH // 2) as pair:
                for par in range(2):
                    copy_xnT(pair * 2 + par, par)
                    copy_c(pair * 2 + par, par)
                    copy_v(pair * 2 + par, par)

        @block.gpsimd
        def _(pool):
            pool.memset(sb["mhalf"], -0.5).then_inc(ones_set, 1)
            pool.memset(sb["eps"], EPS).then_inc(ones_set, 1)

            def powers(c, par):
                pool.wait_ge(mean_done, c + 1)
                ge(pool, xn_done, c - 1)
                pool.tensor_tensor(ve[:, par, :], mv[:, par, :, 1], sb["eps"][:, 0:4], ALU.add).then_inc(var_done, 1)
                pool.wait_ge(var_done, c + 1)
                pool.tensor_tensor(rstd[:, par, :], ve[:, par, :], sb["mhalf"][:, 0:4], ALU.pow).then_inc(rstd_done, 1)

            pool.wait_ge(ones_set, 3)
            powers(0, 0)
            powers(1, 1)
            with pool.Fori(1, NCH // 2) as pair:
                for par in range(2):
                    powers(pair * 2 + par, par)

        @block.vector
        def _(dve):
            dve.memset(sb["v_all"][:, :, :, :], 1.0).then_inc(ones_set, 1)

            def mean(c, par):
                for t in range(4):
                    i = dve.bn_stats(stats[:, par, t, :], sb["x"][:, c * 4 + t, :])
                i.then_inc(stats_done, 1)
                dve.wait_ge(stats_done, c + 1)
                ge(dve, xn_done, c - 1)
                ge(dve, rstd_done, c - 1)
                carry_wait(dve, sb)
                for t in range(4):
                    i = dve.bn_aggr(mv[:, par, t, :], stats[:, par, t, :])
                i.then_inc(mean_done, 1)

            def norm(c, par):
                dve.wait_ge(rstd_done, c + 1)
                ge(dve, xnT_done, c - 1)
                for t in range(4):
                    i = dve.tensor_scalar(xn[:, par, t, :], sb["x"][:, c * 4 + t, :], mv[:, par, t, 0:1],
                                          rstd[:, par, t:t + 1], ALU.subtract, ALU.mult)
                i.then_inc(xn_done, 1)

            def cut(c, par):
                if not isinstance(c, int) or c >= 2:
                    dve.wait_ge(parts_out[par], (c - par) * (8 * 6))
                for w in range(2):
                    dve.wait_ge(qk_done, 2 * c + w + 1)
                    dve.tensor_copy(parts[:, par, w, 0, :], psQK[:, w, :]).then_inc(hi_done, 1)
                    dve.wait_ge(hi_done, 2 * c + w + 1)
                    dve.tensor_tensor(rem[:, par, w, :], psQK[:, w, :], parts[:, par, w, 0, :], ALU.subtract).then_inc(rem1_done, 1)
                    dve.wait_ge(rem1_done, 2 * c + w + 1)
                    dve.tensor_copy(parts[:, par, w, 1, :], rem[:, par, w, :]).then_inc(mid_done, 1)
                    dve.wait_ge(mid_done, 2 * c + w + 1)
                    dve.tensor_tensor(parts[:, par, w, 2, :], rem[:, par, w, :], parts[:, par, w, 1, :], ALU.subtract).then_inc(parts_done, 1)

            dve.wait_ge(x_first, 16)
            mean(0, 0)
            dve.wait_ge(x_rest, 16)
            norm(0, 0)
            mean(1, 1)
            cut(0, 0)
            norm(1, 1)
            mean(2, 0)
            cut(1, 1)
            with dve.Fori(1, NCH // 2 - 1) as pair:
                for par in range(2):
                    c = pair * 2 + par
                    norm(c, par)
                    mean(c + 1, 1 - par)
                    cut(c, par)
            norm(NCH - 2, 0)
            mean(NCH - 1, 1)
            cut(NCH - 2, 0)
            norm(NCH - 1, 1)
            cut(NCH - 1, 1)

        @block.tensor
        def _(pe):
            pe.wait_ge(w_in, 16 * 6)

            def transposes(c, par):
                pe.wait_ge(xn_done, c + 1)
                ge(pe, xnT_copied, c - 1)
                for t in range(4):
                    i = pe.transpose(psT[:, par, t * P:(t + 1) * P], xn[:, par, t, :], sb["ident"])
                i.then_inc(xnT_done, 1)

            def latents(c, par):
                pe.wait_ge(xnT_copied, c + 1)
                ge(pe, c_copied, c - 1)
                pe.matmul(psC[0:2 * DC, par, :], sb["w_down"], xnT[:, par, :], start=True, stop=True).then_inc(c_done, 1)

            def heads(c, par):
                pe.wait_ge(c_copied, c + 1)
                ge(pe, rem1_done, 2 * c - 1)
                pe.matmul(psQK[:, 0, :], sb["w_uq"][0:DC, :], cT[0:DC, par, :], start=True, stop=True).then_inc(qk_done, 1)
                ge(pe, rem1_done, 2 * c)
                pe.matmul(psQK[:, 1, :], sb["w_ukv"][DC:2 * DC, 0:D], cT[DC:2 * DC, par, :], start=True, stop=True).then_inc(qk_done, 1)
                ge(pe, v_copied, c)
                for t in range(4):
                    i = pe.matmul(psV[:, t * P:(t + 1) * P], cT[DC:2 * DC, par, t * P:(t + 1) * P],
                                  sb["w_ukv"][DC:2 * DC, D:2 * D], start=True, stop=True)
                i.then_inc(v_done, 1)

            for c in range(2):
                transposes(c, c)
                latents(c, c)
                heads(c, c)
            with pe.Fori(1, NCH // 2) as pair:
                for par in range(2):
                    c = pair * 2 + par
                    transposes(c, par)
                    latents(c, par)
                    heads(c, par)


MAX_UNITS = [(i, j, kc) for i in range(TB) for j in range(HG) for kc in range(i // 4 + 1)]
EXP_GROUPS = [(qc, kt) for qc in range(2) for kt in range(4 * qc + 4)]
NMU, NEG_ = len(MAX_UNITS), len(EXP_GROUPS)
NEU = NEG_ * HG
NM_A = sum(1 for i, _, _ in MAX_UNITS if i < 4)
assert NMU == NEU


def attend(nc, io, sb):
    with ExitStack() as ctx:
        def tile(name, shape, dt=F32):
            return ctx.enter_context(nc.sbuf_tensor(name, shape, dt))

        def sem(name):
            return ctx.enter_context(nc.semaphore(name))

        qs = tile("a_qs", [KROWS, NG, HG, S], BF16)
        ks = tile("a_ks", [KROWS, NG, HG, S], BF16)
        vs = [tile(f"a_vs{g}", [P, TB * HG * VA + VPAD]) for g in range(NG)]
        prob = [tile(f"a_prob{r}", [P, HG, 512]) for r in range(3)]
        oT = tile("a_oT", [P, 2, 512])
        mx = tile("a_mx", [P, 2, TB, HG, 2])
        nm = tile("a_nm", [P, 2, 4 * HG])
        nmr = tile("a_nmr", [P, 2, 4 * HG])
        nmp = tile("a_nmp", [P, TB, HG, 3], BF16)
        nmT = tile("a_nmT", [NM, S], BF16)
        rec = tile("a_rec", [P, 2, 4, HG])
        spare = tile("a_spare", [P, 6])
        psM = ctx.enter_context(nc.psum_tensor("a_psM", [P, 2, 512], F32))
        psE = ctx.enter_context(nc.psum_tensor("a_psE", [P, 3, 512], F32))
        psO = ctx.enter_context(nc.psum_tensor("a_psO", [P, 2, 512], F32))
        psX = ctx.enter_context(nc.psum_tensor("a_psX", [P, 512], F32))
        psXb = psX[:, :].bitcast(BF16)

        const_in = sem("const_in")
        stack_in = [sem(f"stack_in{g}") for g in range(NG)]
        nm_in = [sem("nm_in_a"), sem("nm_in_b")]
        max_ready, max_read = sem("max_ready"), sem("max_read")
        score_ready, exp_done, av_done = sem("score_ready"), sem("exp_done"), sem("av_done")
        nm_step, nm_parts, nm_T, nm_copied = sem("nm_step"), sem("nm_parts"), sem("nm_T"), sem("nm_copied")
        o_copied, o_T, rec_done, o_read = sem("o_copied"), sem("o_T"), sem("rec_done"), sem("o_read")
        pad_set = sem("pad_set")
        C_MAX, C_EXP, C_AV, C_O, C_T, C_R = 2, 3, 3, 2, 2, 1

        block = ctx.enter_context(nc.Block())
        NSTAGE = B * NG
        LOADS = 16 * (4 * HG + 2)

        def load_group(sp, b, g):
            for j in range(HG):
                for a in range(3):
                    q_src = io["q_parts"][b, g * HG + j, a]
                    sp.dma_start(qs[3 * DK * a:3 * DK * (a + 1), g, j, :], q_src.unsqueeze(0).broadcast_to((3, DK, S))).then_inc(stack_in[g], 16)
                k_src = io["k_parts"][b, g * HG + j].rearrange("r d n -> (r d) n")
                sp.dma_start(ks[0:ROWS, g, j, :], k_src.unsqueeze(0).broadcast_to((3, 3 * DK, S))).then_inc(stack_in[g], 16)
            sp.dma_start(qs[ROWS:KROWS, g, :, :], io["c_zero"]).then_inc(stack_in[g], 16)
            sp.dma_start(vs[g][:, 0:TB * HG * VA], sb["v_all"][:, g, bass.ts(b, TB), :].rearrange("p t a -> p (t a)")).then_inc(stack_in[g], 16)

        @block.sync
        def _(sp):
            sp.dma_start(ks[ROWS:KROWS, :, :, :], io["c_sel"]).then_inc(const_in, 16)
            for dst, src in ((sb["ident_b"], io["c_ident_b"]), (sb["mask_q"], io["c_mask_q"]), (sb["mask_k"], io["c_mask_k"])):
                sp.dma_start(dst, src).then_inc(const_in, 16)
            for g in range(NG):
                load_group(sp, 0, g)
            with sp.Fori(0, B - 1) as b:
                for g in range(NG):
                    sp.wait_ge(av_done, (b * NG + g) * NEG_ + NEG_ + C_AV)
                    load_group(sp, b + 1, g)

        @block.gpsimd
        def _(pool):
            for g in range(NG):
                pool.memset(vs[g][:, TB * HG * VA:], 0.0).then_inc(pad_set, 1)

        @block.tensor
        def _(pe):
            pe.wait_ge(const_in, 64)
            pe.wait_ge(pad_set, NG)

            def max_unit(s, g, u):
                i, j, kc = MAX_UNITS[u]
                n = min(512, (i + 1) * P - 512 * kc)
                out = psM[:, u % 2, 0:n]
                diag = kc == i // 4
                pe.wait_ge(max_read, s * NMU + (u + 1))
                mm = pe.matmul(out, qs[:, g, j, i * P:(i + 1) * P], ks[:, g, j, 512 * kc:512 * kc + n],
                               start=True, stop=not diag)
                if diag:
                    mm = pe.matmul(out[:, n - P:n], sb["ident_b"], sb["mask_q"], start=False, stop=True)
                mm.then_inc(max_ready, 1)

            def score(e, g, n, j):
                qc, kt = EXP_GROUPS[n]
                q0 = max(512 * qc, kt * P)
                w = 512 * (qc + 1) - q0
                diag = kt * P >= 512 * qc
                u = n * HG + j
                pe.wait_ge(exp_done, e * NEU + (u + 1))
                out = psE[:, u % 3, 0:w]
                mm = pe.matmul(out, ks[:, g, j, kt * P:(kt + 1) * P], qs[:, g, j, q0:q0 + w], start=True, stop=not diag)
                if diag:
                    mm = pe.matmul(out[:, 0:P], sb["ident_b"], sb["mask_k"], start=False, stop=True)
                mm.then_inc(score_ready, 1)

            def values(e, g, n):
                qc, kt = EXP_GROUPS[n]
                q0 = max(0, kt * P - 512 * qc)
                pe.wait_ge(exp_done, e * NEU + (n + 1) * HG + C_EXP)
                if kt == 0:
                    pe.wait_ge(o_copied, e * 2 + qc + 1)
                for j in range(HG):
                    mm = pe.matmul(psO[32 * j:32 * j + 32, qc, q0:512],
                                   vs[g][:, kt * HG * VA + j * VA:kt * HG * VA + j * VA + 32],
                                   prob[n % 3][:, j, 0:512 - q0], start=(kt == 0), stop=(kt == 4 * qc + 3),
                                   skip_group_check=True)
                mm.then_inc(av_done, 1)

            def turn_maxima(s, half):
                pe.wait_ge(nm_parts, 2 * s + half + 1)
                ge(pe, o_read, 2 * s - 2 + half + C_R)
                if half == 1:
                    pe.wait_ge(nm_copied, 2 * s + 1)
                for t in range(4):
                    i = 4 * half + t
                    mm = pe.transpose(psXb[0:NM, t * P:(t + 1) * P], nmp[:, i, :, :].rearrange("p j a -> p (j a)"), sb["ident_b"])
                mm.then_inc(nm_T, 1)

            def turn_outputs(e, qc, maxima):
                pe.wait_ge(o_copied, 2 * e + qc + 1 + C_O)
                if maxima:
                    pe.wait_ge(nm_copied, 2 * e + 2 + qc + 1)
                else:
                    pe.wait_ge(o_read, 2 * e + qc + C_R)
                for t in range(4):
                    mm = pe.transpose(psX[:, t * P:(t + 1) * P], oT[:, qc, t * P:(t + 1) * P], sb["ident"])
                mm.then_inc(o_T, 1)

            def slot(e, g, more):
                g1 = (g + 1) % NG
                if more:
                    pe.wait_ge(stack_in[g1], ((e + 1 - g1) * (LOADS // NG)) + LOADS)
                for n in range(NEG_):
                    if n == 0:
                        pe.wait_ge(nm_in[0], 16 * e + 16)
                    if n == 4:
                        pe.wait_ge(nm_in[1], 16 * e + 16)
                    for j in range(HG):
                        score(e, g, n, j)
                        if more:
                            max_unit(e + 1, g1, n * HG + j)
                    if n:
                        values(e, g, n - 1)
                    if n == 5 and more:
                        turn_maxima(e + 1, 0)
                    if n == 6:
                        turn_outputs(e, 0, more)
                values(e, g, NEG_ - 1)
                if more:
                    turn_maxima(e + 1, 1)
                turn_outputs(e, 1, more)

            pe.wait_ge(stack_in[0], LOADS)
            for u in range(NMU):
                max_unit(0, 0, u)
            turn_maxima(0, 0)
            turn_maxima(0, 1)
            with pe.Fori(0, B - 1) as b:
                for g in range(NG):
                    slot(b * NG + g, g, True)
            for g in range(NG):
                slot((B - 1) * NG + g, g, g < NG - 1)

        @block.scalar
        def _(act):
            def exps(e, n):
                qc, kt = EXP_GROUPS[n]
                w = 512 * (qc + 1) - max(512 * qc, kt * P)
                act.wait_ge(av_done, e * NEG_ + (n + 1))
                for j in range(HG):
                    u = n * HG + j
                    act.wait_ge(score_ready, e * NEU + (u + 1))
                    act.activation(prob[n % 3][:, j, 0:w], psE[:, u % 3, 0:w], ACT.Exp, scale=SCALE0).then_inc(exp_done, 1)

            def copy_maxima(s, half):
                act.wait_ge(nm_T, 2 * s + half + 1)
                if not isinstance(s, int) or s > 0:
                    act.wait_ge(nm_in[half], 16 * s)
                cols = slice(512 * half, 512 * half + 512)
                act.activation(nmT[:, cols], psXb[0:NM, 0:512], ACT.Copy).then_inc(nm_copied, 1)

            def send_maxima(s, g, half):
                act.wait_ge(nm_copied, 2 * s + half + 1)
                cols = slice(512 * half, 512 * half + 512)
                act.dma_start(qs[ROWS:ROWS + NM, g, :, cols], nmT[:, cols].unsqueeze(1).broadcast_to((NM, HG, 512))).then_inc(nm_in[half], 16)

            def copy_outputs(e, qc):
                act.wait_ge(av_done, e * NEG_ + (4 if qc == 0 else NEG_) + C_AV)
                act.wait_ge(o_T, 2 * e + qc - 1 + C_T)
                act.activation(oT[:, qc, :], psO[:, qc, :], ACT.Copy).then_inc(o_copied, 1)

            def slot(e, g, more):
                g1 = (g + 1) % NG
                for n in range(NEG_):
                    exps(e, n)
                    if n == 5:
                        copy_outputs(e, 0)
                    if n == 6 and more:
                        copy_maxima(e + 1, 0)
                        send_maxima(e + 1, g1, 0)
                if more:
                    copy_maxima(e + 1, 1)
                    send_maxima(e + 1, g1, 1)
                copy_outputs(e, 1)

            for half in range(2):
                copy_maxima(0, half)
                send_maxima(0, 0, half)
            with act.Fori(0, B - 1) as b:
                for g in range(NG):
                    slot(b * NG + g, g, True)
            for g in range(NG):
                slot((B - 1) * NG + g, g, g < NG - 1)
            for half in range(2):
                act.wait_ge(nm_in[half], 16 * NSTAGE)

        @block.vector
        def _(dve):
            dve.memset(spare[:, 0:1], 0.0).then_inc(max_read, C_MAX)
            dve.memset(spare[:, 1:2], 0.0).then_inc(exp_done, C_EXP)
            dve.memset(spare[:, 2:3], 0.0).then_inc(av_done, C_AV)
            dve.memset(spare[:, 3:4], 0.0).then_inc(o_copied, C_O)
            dve.memset(spare[:, 4:5], 0.0).then_inc(o_T, C_T)
            dve.memset(spare[:, 5:6], 0.0).then_inc(o_read, C_R)

            def maximum(s, u):
                i, j, kc = MAX_UNITS[u]
                n = min(512, (i + 1) * P - 512 * kc)
                dve.wait_ge(max_ready, s * NMU + (u + 1))
                dve.tensor_reduce(mx[:, 0, i, j, kc:kc + 1], psM[:, u % 2, 0:n], AX.X, ALU.max).then_inc(max_read, 1)

            def cut_maxima(s, half):
                upto = NM_A if half == 0 else NMU
                dve.wait_ge(max_read, s * NMU + upto + C_MAX)
                ge(dve, nm_T, 2 * s + half - 1)
                step = s * 8 + 4 * half
                tiles = slice(4 * half, 4 * half + 4)
                dve.tensor_reduce(nm[:, half, :], mx[:, 0, tiles, :, 0:half + 1].rearrange("p i j k -> p (i j) k"), AX.X, ALU.max, negate=True).then_inc(nm_step, 1)
                dve.wait_ge(nm_step, step + 1)
                part = [nmp[:, tiles, :, a].rearrange("p i j -> p (i j)") for a in range(3)]
                dve.tensor_copy(part[0], nm[:, half, :]).then_inc(nm_step, 1)
                dve.wait_ge(nm_step, step + 2)
                dve.tensor_tensor(nmr[:, half, :], nm[:, half, :], part[0], ALU.subtract).then_inc(nm_step, 1)
                dve.wait_ge(nm_step, step + 3)
                dve.tensor_copy(part[1], nmr[:, half, :]).then_inc(nm_step, 1)
                dve.wait_ge(nm_step, step + 4)
                dve.tensor_tensor(part[2], nmr[:, half, :], part[1], ALU.subtract).then_inc(nm_parts, 1)

            def outputs(b, e, g, qc):
                ps = psX[:, :].rearrange("p (t j c) -> p t j c", t=4, j=HG)
                dve.wait_ge(o_T, 2 * e + qc + 1 + C_T)
                dve.reciprocal(rec[:, qc, :, :], ps[:, :, :, DK]).then_inc(rec_done, 1)
                dve.wait_ge(rec_done, 2 * e + qc + 1)
                out = sb["o_tok"][:, bass.ts(b * 2 + qc, 4), g * HG * DK:(g + 1) * HG * DK].rearrange("p t (j d) -> p t j d", d=DK)
                dve.tensor_tensor(out, ps[:, :, :, 0:DK], rec[:, qc, :, :].unsqueeze(3).broadcast_to((P, 4, HG, DK)), ALU.mult).then_inc(o_read, 1)

            def slot(b, g, more):
                e = b * NG + g
                for u in range(NMU):
                    if more:
                        maximum(e + 1, u)
                    if u == NM_A - 1 and more:
                        cut_maxima(e + 1, 0)
                    if u == 27:
                        outputs(b, e, g, 0)
                if more:
                    cut_maxima(e + 1, 1)
                outputs(b, e, g, 1)

            for u in range(NMU):
                maximum(0, u)
                if u == NM_A - 1:
                    cut_maxima(0, 0)
            cut_maxima(0, 1)
            with dve.Fori(0, B - 1) as b:
                for g in range(NG):
                    slot(b, g, True)
            for g in range(NG):
                slot(B - 1, g, g < NG - 1)


def pipelined(eng, n, ring, steps):
    deepest = max(lag for lag, _ in steps)
    first = -(-(deepest + ring) // ring) * ring
    last = n // ring * ring

    def slot(s, place, whole):
        for lag, fn in steps:
            if whole or 0 <= s - lag < n:
                fn(s - lag, (place - lag) % ring)

    first = min(first, last)
    for s in range(first):
        slot(s, s % ring, False)
    if first < last:
        with eng.Fori(first // ring, last // ring) as k:
            for r in range(ring):
                slot(k * ring + r, r, True)
    for s in range(last, n + deepest):
        slot(s, s % ring, False)


def at_least(eng, sem, base, t, k):
    if isinstance(t, int) and t + k <= 0:
        return
    eng.wait_ge(sem, base + t + k)


def mix(nc, io, sb):
    with ExitStack() as ctx:
        def tile(name, shape, dt=F32):
            return ctx.enter_context(nc.sbuf_tensor(name, shape, dt))

        def sem(name):
            return ctx.enter_context(nc.semaphore("m_" + name))

        oc = tile("m_oc", [P, 2, 4, P])
        ocT = tile("m_ocT", [P, 2, 4, P])
        stats = tile("m_stats", [P, 2, 2, 4, 6])
        mv = tile("m_mv", [P, 2, 2, 4, 2])
        ve = tile("m_ve", [P, 2, 2, 4])
        rstd = tile("m_rstd", [P, 2, 2, 4])
        an = tile("m_an", [P, 2, 4, D])
        psT = ctx.enter_context(nc.psum_tensor("m_psT", [P, 2, 512], F32))
        psA = ctx.enter_context(nc.psum_tensor("m_psA", [P, 4, 512], F32))

        w_in, o_staged, oT_done, oT_copied, a_done = sem("w_in"), sem("o_staged"), sem("oT_done"), sem("oT_copied"), sem("a_done")
        stats_done = [sem("stats_a"), sem("stats_x")]
        mean_done = [sem("mean_a"), sem("mean_x")]
        var_done = [sem("var_a"), sem("var_x")]
        rstd_done = [sem("rstd_a"), sem("rstd_x")]
        an_done, x1_done, xf_done = sem("an_done"), sem("x1_done"), sem("xf_done")
        block = ctx.enter_context(nc.Block())

        @block.sync
        def _(sp):
            sp.dma_start(sb["w_o"], io["W_o"]).then_inc(w_in, 16)

        @block.tensor
        def _(pe):
            pe.wait_ge(w_in, 16)

            def turn(c, r):
                at_least(pe, o_staged, 0, c, 1)
                at_least(pe, oT_copied, 0, c, -1)
                p = r % 2
                for t in range(4):
                    i = pe.transpose(psT[:, p, t * P:(t + 1) * P], oc[:, p, t, :], sb["ident"])
                i.then_inc(oT_done, 1)

            def project_out(c, r):
                at_least(pe, oT_copied, 0, c, 1)
                at_least(pe, an_done, 0, c, -3)
                for t in range(4):
                    i = pe.matmul(psA[:, r, t * P:(t + 1) * P], ocT[:, r % 2, t, :], sb["w_o"], start=True, stop=True)
                i.then_inc(a_done, 1)

            pipelined(pe, NCH, 4, [(0, turn), (0, project_out)])

        @block.scalar
        def _(act):
            def copy(c, r):
                at_least(act, oT_done, 0, c, 1)
                at_least(act, a_done, 0, c, -1)
                act.activation(ocT[:, r % 2, :, :].rearrange("p t c -> p (t c)"), psT[:, r % 2, :], ACT.Copy).then_inc(oT_copied, 1)

            pipelined(act, NCH, 4, [(0, copy)])

        @block.gpsimd
        def _(pool):
            def powers(w):
                def fn(c, r):
                    p = r % 2
                    at_least(pool, mean_done[w], 0, c, 1)
                    pool.tensor_tensor(ve[:, w, p, :], mv[:, w, p, :, 1], sb["eps"][:, 0:4], ALU.add).then_inc(var_done[w], 1)
                    at_least(pool, var_done[w], 0, c, 1)
                    pool.tensor_tensor(rstd[:, w, p, :], ve[:, w, p, :], sb["mhalf"][:, 0:4], ALU.pow).then_inc(rstd_done[w], 1)
                return fn

            pipelined(pool, NCH, 4, [(0, powers(0)), (1, powers(1))])

        @block.vector
        def _(dve):
            def stage(c, r):
                at_least(dve, oT_done, 0, c, -1)
                dve.tensor_copy(oc[:, r % 2, :, :], sb["o_tok"][:, bass.ts(c, 4), :]).then_inc(o_staged, 1)

            def moments(w, c, p, source):
                for t in range(4):
                    i = dve.bn_stats(stats[:, w, p, t, :], source(t))
                i.then_inc(stats_done[w], 1)
                at_least(dve, stats_done[w], 0, c, 1)
                carry_wait(dve, sb)
                for t in range(4):
                    i = dve.bn_aggr(mv[:, w, p, t, :], stats[:, w, p, t, :])
                i.then_inc(mean_done[w], 1)

            def moments_a(c, r):
                at_least(dve, a_done, 0, c, 1)
                moments(0, c, r % 2, lambda t: psA[:, r, t * P:(t + 1) * P])

            def residual(c, r):
                p = r % 2
                at_least(dve, rstd_done[0], 0, c, 1)
                for t in range(4):
                    i = dve.tensor_scalar(an[:, p, t, :], psA[:, r, t * P:(t + 1) * P], mv[:, 0, p, t, 0:1],
                                          rstd[:, 0, p, t:t + 1], ALU.subtract, ALU.mult)
                i.then_inc(an_done, 1)
                at_least(dve, an_done, 0, c, 1)
                x = sb["x"][:, bass.ts(c, 4), :]
                dve.tensor_tensor(x, x, an[:, p, :, :], ALU.add).then_inc(x1_done, 1)
                at_least(dve, x1_done, 0, c, 1)
                moments(1, c, p, lambda t: sb["x"][:, c * 4 + t, :])

            def layers_input(c, r):
                p = r % 2
                at_least(dve, rstd_done[1], 0, c, 1)
                for t in range(4):
                    i = dve.tensor_scalar(sb["xf"][:, c * 4 + t, :], sb["x"][:, c * 4 + t, :], mv[:, 1, p, t, 0:1],
                                          rstd[:, 1, p, t:t + 1], ALU.subtract, ALU.mult)
                i.then_inc(xf_done, 1)

            pipelined(dve, NCH, 4, [(0, stage), (1, moments_a), (3, layers_input), (2, residual)])


def window(nc, io, sb, layer):
    base = layer * NT
    with ExitStack() as ctx:
        def tile(name, shape, dt=F32):
            return ctx.enter_context(nc.sbuf_tensor(name, shape, dt))

        def sem(name):
            return ctx.enter_context(nc.semaphore("w_" + name))

        wqkv, wo = tile("w_wqkv", [P, 3 * INNER]), tile("w_wo", [P, 4, D])
        scales = tile("w_scales", [P, 2, DH])
        cos, sin = tile("w_cos", [P, TB, 2, DH]), tile("w_sin", [P, TB, 2, DH])
        xc = tile("w_xc", [P, 2, D])
        hT = tile("w_hT", [P, 2, P + 1])
        sq = tile("w_sq", [P, 2 * INNER])
        ss, rn = tile("w_ss", [P, 2, 16]), tile("w_rn", [P, 2, 16])
        ssm = tile("w_ssm", [P, 2, 16])
        qn, t1, t2 = tile("w_qn", [P, 2 * INNER]), tile("w_t1", [P, 2 * INNER]), tile("w_t2", [P, 2 * INNER])
        rot = tile("w_rot", [P, 2 * INNER])
        qT, kT = tile("w_qT", [P, 2, 4, P]), tile("w_kT", [P, 2, 4, KEYS])
        v = [tile(f"w_v{r}", [P, INNER]) for r in range(4)]
        nmx, bias = tile("w_nmx", [P, 2, HEADS]), tile("w_bias", [P, 2, HEADS])
        den, rden = tile("w_den", [P, 2, HEADS]), tile("w_rden", [P, 2, HEADS])
        prob = tile("w_prob", [P, 2, HEADS, KEYS])
        pT = tile("w_pT", [P, 2, 2, 2, P])
        oT = tile("w_oT", [P, 4, P])
        psQK = ctx.enter_context(nc.psum_tensor("w_psQK", [P, 2, 512], F32))
        psM = ctx.enter_context(nc.psum_tensor("w_psM", [P, 512], F32))
        psT = ctx.enter_context(nc.psum_tensor("w_psT", [P, 2, 512], F32))
        psS = ctx.enter_context(nc.psum_tensor("w_psS", [P, 2, 512], F32))
        psO = ctx.enter_context(nc.psum_tensor("w_psO", [P, 512], F32))

        w_in, tables = sem("w_in"), sem("tables")
        xc_in = [sem("xc_in0"), sem("xc_in1")]
        zeroed = sem("zeroed")
        xT_done, hT_copied, carried = sem("xT_done"), sem("hT_copied"), sem("carried")
        qk_done, v_done, sq_done, ss_done, ssm_done, rn_done = (sem(x) for x in ("qk_done", "v_done", "sq_done", "ss_done", "ssm_done", "rn_done"))
        v_copied, qn_done, t1_done, t2_done, rot_done = (sem(x) for x in ("v_copied", "qn_done", "t1_done", "t2_done", "rot_done"))
        qkT_done, qkT_copied, prev_copied = sem("qkT_done"), sem("qkT_copied"), sem("prev_copied")
        s_done, max_done, bias_done, exp_done = sem("s_done"), sem("max_done"), sem("bias_done"), sem("exp_done")
        rden_done, prob_done, pT_done, pT_copied_a, pT_copied_v = (sem(x) for x in ("rden_done", "prob_done", "pT_done", "pT_copied_a", "pT_copied_v"))
        av_done, oT_copied, y_done, xf_done = sem("av_done"), sem("oT_copied"), sem("y_done"), sem("xf_done")
        block = ctx.enter_context(nc.Block())

        def pairs(eng, s, t, k):
            if isinstance(t, int) and 4 * t + k <= 0:
                return
            eng.wait_ge(s, base * 4 + t * 4 + k)

        @block.sync
        def _(sp):
            def load_x(t, r):
                at_least(sp, xT_done, base, t, -1)
                sp.dma_start(xc[:, r % 2, :], sb["xf"][:, t, :]).then_inc(xc_in[r % 2], 16)

            sp.dma_start(wqkv[:, :], io["wqkv"][layer]).then_inc(w_in, 16)
            sp.dma_start(wo[:, :, :], io["wo"][layer].rearrange("(c p) n -> p c n", p=P)).then_inc(w_in, 16)
            for w, name in ((0, "q_scale"), (1, "k_scale")):
                sp.dma_start(scales[:, w, :], io[name][bass.ds(layer, 1), :].broadcast_to((P, DH))).then_inc(w_in, 16)
            sp.dma_start(cos[:, :, :, :], io["c_cos"]).then_inc(w_in, 16)
            sp.dma_start(sin[:, :, :, :], io["c_sin"]).then_inc(w_in, 16)
            sp.dma_start(sb["mask_w"], io["c_mask_w"]).then_inc(w_in, 16)
            sp.dma_start(sb["carry"], io["c_carry"]).then_inc(w_in, 16)
            pipelined(sp, NT, 4, [(0, load_x)])

        @block.tensor
        def _(pe):
            def turn_x(t, r):
                p = r % 2
                pe.wait_ge(xc_in[p], (base + t - p) * 8 + 16)
                at_least(pe, v_copied, base, t, 0)
                at_least(pe, xf_done, base, t, -2)
                pe.transpose(psM[:, 0:P], xc[:, p, :], sb["ident"]).then_inc(xT_done, 1)

            def qkv(t, r):
                p = r % 2
                at_least(pe, hT_copied, base, t, 1)
                at_least(pe, carried, base, t, 1)
                at_least(pe, qn_done, base, t, 0)
                for w in range(2):
                    i = pe.matmul(psQK[:, w, :], hT[:, p, 0:P], wqkv[:, w * INNER:(w + 1) * INNER], start=True, stop=True)
                i.then_inc(qk_done, 1)
                at_least(pe, xf_done, base, t, -2)
                pe.matmul(psM[:, :], hT[:, p, 0:P], wqkv[:, 2 * INNER:3 * INNER], start=True, stop=True).then_inc(v_done, 1)

            def turn_qk(t, r):
                at_least(pe, rot_done, base, t, 1)
                pairs(pe, pT_copied_a, t, -4)
                pairs(pe, pT_copied_v, t, -4)
                for w in range(2):
                    for c in range(4):
                        i = pe.transpose(psT[:, w, c * P:(c + 1) * P], rot[:, w * INNER + c * P:w * INNER + (c + 1) * P], sb["ident"])
                i.then_inc(qkT_done, 1)

            def scores(t, r, pair):
                p = r % 2
                if pair == 0:
                    at_least(pe, qkT_copied, base, t, 1)
                    at_least(pe, prev_copied, base, t, 1)
                pairs(pe, exp_done, t, pair - 1)
                both = psS[:, pair % 2, 0:2 * KEYS].rearrange("p (h k) -> p h k", h=2)
                pe.matmul(both, sb["ident_b"], sb["mask_w"][:, t % TB, :].unsqueeze(1).broadcast_to((P, 2, KEYS)),
                          start=True, stop=False, skip_group_check=True)
                rows = slice(DH * (pair % 2), DH * (pair % 2) + DH)
                for n in range(2):
                    c = 2 * (pair // 2) + n
                    i = pe.matmul(both[:, n, :], qT[rows, p, c, :], kT[rows, p, c, :], start=False, stop=True, skip_group_check=True)
                i.then_inc(s_done, 1)

            def turn_p(t, r, pair):
                p = r % 2
                if pair == 0:
                    at_least(pe, prob_done, base, t, 1)
                    at_least(pe, qkT_copied, base, t, 1 if isinstance(t, int) and t == NT - 1 else 2)
                if pair >= 2:
                    pairs(pe, pT_copied_a, t, pair - 1)
                    pairs(pe, pT_copied_v, t, pair - 1)
                for half in range(2):
                    h = 2 * pair + half
                    for blk, c0 in ((0, 0), (1, WIN)):
                        i = pe.transpose(psT[:, pair % 2, (2 * half + blk) * P:(2 * half + blk + 1) * P],
                                         prob[:, p, h, c0:c0 + P], sb["ident"])
                i.then_inc(pT_done, 1)

            def values(t, r, pair):
                pairs(pe, pT_copied_a, t, pair + 1)
                pairs(pe, pT_copied_v, t, pair + 1)
                if pair == 0:
                    at_least(pe, oT_copied, base, t, 0)
                own, before = v[r], v[(r - 1) % 4]
                for blk in range(2):
                    for half in range(2):
                        h = 2 * pair + half
                        cols = slice(h * DH, (h + 1) * DH)
                        out = psO[DH * half:DH * half + DH, pair * P:(pair + 1) * P]
                        if blk == 0:
                            i = pe.matmul(out, own[:, cols], pT[:, pair % 2, half, 0, :], start=True, stop=False, skip_group_check=True)
                        else:
                            i = pe.matmul(out, before[WIN:P, cols], pT[WIN:P, pair % 2, half, 1, :], start=False, stop=True, skip_group_check=True)
                i.then_inc(av_done, 1)

            def attention(s, r):
                for pair in range(4):
                    if not isinstance(s, int) or 0 <= s - 1 < NT:
                        scores(s - 1, (r - 1) % 4, pair)
                    if not isinstance(s, int) or 0 <= s - 2 < NT:
                        turn_p(s - 2, (r - 2) % 4, pair)
                        if pair:
                            values(s - 2, (r - 2) % 4, pair - 1)
                if not isinstance(s, int) or 0 <= s - 2 < NT:
                    values(s - 2, (r - 2) % 4, 3)

            def out(t, r):
                at_least(pe, oT_copied, base, t, 1)
                at_least(pe, xf_done, base, t, 0)
                for c in range(4):
                    i = pe.matmul(psM[:, 0:P], oT[:, c, :], wo[:, c, :], start=(c == 0), stop=(c == 3))
                i.then_inc(y_done, 1)

            pe.wait_ge(w_in, (layer + 1) * (8 * 16))

            def slot(s, r, whole):
                def runs(t):
                    return whole or 0 <= t < NT
                if runs(s):
                    qkv(s, r)
                if runs(s - 1):
                    turn_qk(s - 1, (r - 1) % 4)
                attention(s, r)
                if runs(s - 2):
                    at_least(pe, v_copied, base, s, 1) if runs(s) else None
                    out(s - 2, (r - 2) % 4)
                if runs(s + 1):
                    at_least(pe, v_copied, base, s, 1)
                    turn_x(s + 1, (r + 1) % 4)

            turn_x(0, 0)
            for s in range(8):
                slot(s, s % 4, False)
            with pe.Fori(2, NT // 4 - 1) as k:
                for r in range(4):
                    slot(k * 4 + r, r, True)
            for s in range(NT - 4, NT + 2):
                slot(s, s % 4, False)

        @block.scalar
        def _(act):
            def copy_hT(t, r):
                p = r % 2
                at_least(act, xT_done, base, t, 1)
                at_least(act, v_done, base, t, -1)
                at_least(act, carried, base, t, 0)
                act.activation(hT[0:WIN, p, 0:P], psM[0:WIN, 0:P], ACT.Copy)
                act.activation(hT[WIN:P, p, 1:P + 1], psM[WIN:P, 0:P], ACT.Copy).then_inc(hT_copied, 1)

            def squares(t, r):
                at_least(act, qk_done, base, t, 1)
                at_least(act, ss_done, base, t, 0)
                act.activation(sq[:, :].rearrange("p (w n) -> p w n", w=2), psQK[:, :, :], ACT.Square).then_inc(sq_done, 1)

            def copy_v(t, r):
                at_least(act, v_done, base, t, 1)
                pairs(act, av_done, t, -8)
                act.activation(v[r][:, :], psM[:, :], ACT.Copy).then_inc(v_copied, 1)

            def copy_qkT(t, r):
                p = r % 2
                at_least(act, qkT_done, base, t, 1)
                at_least(act, prev_copied, base, t, 0)
                act.activation(qT[:, p, :, :], psT[:, 0, :].rearrange("p (c n) -> p c n", c=4), ACT.Copy)
                act.activation(kT[:, p, :, 0:P], psT[:, 1, :].rearrange("p (c n) -> p c n", c=4), ACT.Copy).then_inc(qkT_copied, 1)

            def exps(t, r, pair):
                p = r % 2
                pairs(act, bias_done, t, pair + 1)
                for n in range(2):
                    h = 4 * (pair // 2) + pair % 2 + 2 * n
                    i = act.activation(prob[:, p, h, :], psS[:, pair % 2, n * KEYS:(n + 1) * KEYS], ACT.Exp,
                                       bias=bias[:, p, h:h + 1], scale=QK_SCALE, accum_out=den[:, p, h:h + 1])
                i.then_inc(exp_done, 1)

            def copy_pT(t, r, pair):
                pairs(act, pT_done, t, pair + 1)
                pairs(act, av_done, t, pair - 1)
                act.activation(pT[:, pair % 2, 0, :, :], psT[:, pair % 2, 0:2 * P].rearrange("p (b n) -> p b n", b=2), ACT.Copy).then_inc(pT_copied_a, 1)

            def copy_oT(t, r):
                pairs(act, av_done, t, 4)
                at_least(act, y_done, base, t, 0)
                act.activation(oT[:, :, :], psO[:, :].rearrange("p (c n) -> p c n", c=4), ACT.Copy).then_inc(oT_copied, 1)

            def slot(s, r, whole):
                def runs(t):
                    return whole or 0 <= t < NT
                if runs(s):
                    copy_hT(s, r)
                    squares(s, r)
                    copy_v(s, r)
                if runs(s - 1):
                    copy_qkT(s - 1, (r - 1) % 4)
                for pair in range(4):
                    if runs(s - 1):
                        exps(s - 1, (r - 1) % 4, pair)
                    if runs(s - 2):
                        copy_pT(s - 2, (r - 2) % 4, pair)
                if runs(s - 2):
                    copy_oT(s - 2, (r - 2) % 4)

            for s in range(8):
                slot(s, s % 4, False)
            with act.Fori(2, NT // 4) as k:
                for r in range(4):
                    slot(k * 4 + r, r, True)
            for s in range(NT, NT + 2):
                slot(s, s % 4, False)

        @block.gpsimd
        def _(pool):
            def norms(t, r):
                p = r % 2
                at_least(pool, ssm_done, base, t, 1)
                at_least(pool, qn_done, base, t, -1)
                pool.tensor_tensor(rn[:, p, :], ssm[:, p, :], sb["mhalf"][:, 0:16], ALU.pow).then_inc(rn_done, 1)

            def rotate(t, r):
                at_least(pool, qn_done, base, t, 1)
                for half in range(2):
                    out, src = (x[:, :].rearrange("p (w h u d) -> p w h u d", w=2, h=HEADS, u=2) for x in (t2, qn))
                    for w in range(2):
                        tab = sin[:, t % TB, w, half * 32:half * 32 + 32].unsqueeze(1).broadcast_to((P, HEADS, 32))
                        i = pool.tensor_tensor(out[:, w, :, half, :], src[:, w, :, 1 - half, :], tab, ALU.mult)
                i.then_inc(t2_done, 1)
                at_least(pool, t2_done, base, t, 1)
                at_least(pool, t1_done, base, t, 1)
                at_least(pool, qkT_done, base, t, 0)
                pool.tensor_tensor(rot[:, :], t1[:, :], t2[:, :], ALU.add).then_inc(rot_done, 1)

            pool.wait_ge(tables, layer * 6 + 6)
            pipelined(pool, NT, 4, [(0, norms), (0, rotate)])

        @block.vector
        def _(dve):
            dve.memset(hT[WIN:P, 1, P:P + 1], 0.0).then_inc(zeroed, 1)
            dve.memset(kT[:, 1, :, :], 0.0).then_inc(zeroed, 1)
            dve.memset(v[3][:, :], 0.0).then_inc(zeroed, 1)
            dve.wait_ge(w_in, (layer + 1) * (8 * 16))
            for w in range(2):
                sc = scales[:, w, :].unsqueeze(1).broadcast_to((P, TB, DH))
                dve.tensor_tensor(cos[:, :, w, :], cos[:, :, w, :], sc, ALU.mult).then_inc(tables, 1)
                for half in range(2):
                    sc = scales[:, w, 32 - 32 * half:64 - 32 * half].unsqueeze(1).broadcast_to((P, TB, 32))
                    part = sin[:, :, w, 32 * half:32 * half + 32]
                    dve.tensor_tensor(part, part, sc, ALU.mult).then_inc(tables, 1)
            dve.wait_ge(zeroed, layer * 3 + 3)
            dve.wait_ge(tables, layer * 6 + 6)

            def carry(t, r):
                p = r % 2
                at_least(dve, hT_copied, base, t, 0)
                at_least(dve, v_done, base, t, -1)
                dve.tensor_scalar(hT[WIN:P, p, 0:1], hT[WIN:P, 1 - p, P:P + 1], sb["carry"][WIN:P, bass.ds(t % TB, 1)], None, ALU.mult).then_inc(carried, 1)

            def sums(t, r):
                at_least(dve, sq_done, base, t, 1)
                at_least(dve, rn_done, base, t, -1)
                dve.tensor_reduce(ss[:, r % 2, :], sq[:, :].rearrange("p (h d) -> p h d", d=DH), AX.X, ALU.add).then_inc(ss_done, 1)
                at_least(dve, ss_done, base, t, 1)
                dve.tensor_scalar(ssm[:, r % 2, :], ss[:, r % 2, :], 1e-24, None, ALU.max).then_inc(ssm_done, 1)

            def normalise(t, r):
                p = r % 2
                at_least(dve, rn_done, base, t, 1)
                at_least(dve, t2_done, base, t, 0)
                dve.tensor_tensor(qn[:, :].rearrange("p (h d) -> p h d", d=DH), psQK[:, :, :].rearrange("p w (h d) -> p (w h) d", d=DH),
                                  rn[:, p, :].unsqueeze(2).broadcast_to((P, 16, DH)), ALU.mult).then_inc(qn_done, 1)
                at_least(dve, qn_done, base, t, 1)
                at_least(dve, rot_done, base, t, 0)
                dve.tensor_tensor(t1[:, :].rearrange("p (w h d) -> p w h d", w=2, d=DH), qn[:, :].rearrange("p (w h d) -> p w h d", w=2, d=DH),
                                  cos[:, t % TB, :, :].unsqueeze(2).broadcast_to((P, 2, HEADS, DH)), ALU.mult).then_inc(t1_done, 1)

            def copy_prev(t, r):
                p = r % 2
                at_least(dve, qkT_copied, base, t, 0)
                pairs(dve, s_done, t, -4)
                dve.tensor_copy(kT[:, p, :, P:KEYS], kT[:, 1 - p, :, WIN:P]).then_inc(prev_copied, 1)

            def maxima(t, r, pair):
                p = r % 2
                pairs(dve, s_done, t, pair + 1)
                h = 4 * (pair // 2) + pair % 2
                hs = slice(h, h + 3, 2)
                dve.tensor_reduce(nmx[:, p, hs], psS[:, pair % 2, 0:2 * KEYS].rearrange("p (h k) -> p h k", h=2), AX.X, ALU.max).then_inc(max_done, 1)
                pairs(dve, max_done, t, pair + 1)
                pairs(dve, exp_done, t, pair - 7)
                dve.tensor_scalar(bias[:, p, hs], nmx[:, p, hs], -QK_SCALE, None, ALU.mult).then_inc(bias_done, 1)

            def copy_pT(t, r, pair):
                pairs(dve, pT_done, t, pair + 1)
                pairs(dve, av_done, t, pair - 1)
                pairs(dve, pT_copied_a, t, pair + 1)
                dve.tensor_copy(pT[:, pair % 2, 1, :, :], psT[:, pair % 2, 2 * P:4 * P].rearrange("p (b n) -> p b n", b=2)).then_inc(pT_copied_v, 1)

            def divide(t, r):
                p = r % 2
                pairs(dve, exp_done, t, 4)
                dve.reciprocal(rden[:, p, :], den[:, p, :]).then_inc(rden_done, 1)
                at_least(dve, rden_done, base, t, 1)
                dve.tensor_tensor(prob[:, p, :, :], prob[:, p, :, :], rden[:, p, :].unsqueeze(2).broadcast_to((P, HEADS, KEYS)), ALU.mult).then_inc(prob_done, 1)

            def residual(t, r):
                at_least(dve, y_done, base, t, 1)
                dve.tensor_tensor(sb["xf"][:, t, :], sb["xf"][:, t, :], psM[:, 0:P], ALU.add).then_inc(xf_done, 1)

            def slot(s, r, whole):
                def runs(t):
                    return whole or 0 <= t < NT
                if runs(s):
                    carry(s, r)
                    sums(s, r)
                if runs(s - 1):
                    copy_prev(s - 1, (r - 1) % 4)
                for pair in range(4):
                    if runs(s - 1):
                        maxima(s - 1, (r - 1) % 4, pair)
                    if runs(s - 2):
                        copy_pT(s - 2, (r - 2) % 4, pair)
                    if pair == 1 and runs(s):
                        normalise(s, r)
                if runs(s - 1):
                    divide(s - 1, (r - 1) % 4)
                if runs(s - 2):
                    residual(s - 2, (r - 2) % 4)

            for s in range(8):
                slot(s, s % 4, False)
            with dve.Fori(2, NT // 4) as k:
                for r in range(4):
                    slot(k * 4 + r, r, True)
            for s in range(NT, NT + 2):
                slot(s, s % 4, False)


def mlp(nc, io, sb, layer):
    base = layer * NCH
    with ExitStack() as ctx:
        def tile(name, shape, dt=F32):
            return ctx.enter_context(nc.sbuf_tensor(name, shape, dt))

        def sem(name):
            return ctx.enter_context(nc.semaphore("f_" + name))

        w1, w2 = tile("f_w1", [P, 2 * HID]), tile("f_w2", [HC, 3, D])
        b1 = tile("f_b1", [HC, 2, 3])
        b2 = tile("f_b2", [P, D])
        lg, lb = tile("f_lg", [P, 1]), tile("f_lb", [P, 1])
        shift, carry = tile("f_shift", [P, P]), tile("f_carry", [P, P])
        stats, mv = tile("f_stats", [P, 2, 4, 2, 6]), tile("f_mv", [P, 2, 4, 2])
        ve, rstd = tile("f_ve", [P, 2, 4]), tile("f_rstd", [P, 2, 4])
        hn, hT = tile("f_hn", [P, 2, 4, D]), tile("f_hT", [P, 2, 512])
        gate, act_t = tile("f_gate", [HC, 3, 512]), tile("f_act", [HC, 2, 3, 512])
        last = tile("f_last", [P, NCH + 1, WIN])
        psH = ctx.enter_context(nc.psum_tensor("f_psH", [P, 2, 512], F32))
        psT = ctx.enter_context(nc.psum_tensor("f_psT", [P, 512], F32))
        psU = ctx.enter_context(nc.psum_tensor("f_psU", [P, 3, 512], F32))
        psY = ctx.enter_context(nc.psum_tensor("f_psY", [P, 2, 512], F32))

        w_in, last_set = sem("w_in"), sem("last_set")
        shifted, stats_done, mean_done, var_done, rstd_done = (sem(x) for x in ("shifted", "stats_done", "mean_done", "var_done", "rstd_done"))
        hn_done, hnT_done, hT_done, u_done, gate_done, act_done = (sem(x) for x in ("hn_done", "hnT_done", "hT_done", "u_done", "gate_done", "act_done"))
        y_done, y_added, xf_done = sem("y_done"), sem("y_added"), sem("xf_done")
        block = ctx.enter_context(nc.Block())
        def units(eng, s, c, k, per=3):
            if isinstance(c, int) and per * c + k <= 0:
                return
            eng.wait_ge(s, base * per + c * per + k)

        @block.sync
        def _(sp):
            ly = bass.ds(layer, 1)
            sp.dma_start(w1[:, :], io["w1"][layer]).then_inc(w_in, 16)
            w2_l = io["w2"][layer]
            sp.dma_start(w2[:, 0:2, :], w2_l[0:2 * HC, :].rearrange("(c p) n -> p c n", p=HC)).then_inc(w_in, 16)
            sp.dma_start(w2[0:HCS[2], 2, :], w2_l[2 * HC:HID, :]).then_inc(w_in, 16)
            b1_l = io["b1"][layer].rearrange("(w n) -> w n", w=2)
            with nc.allow_non_contiguous_dma("a bias to a partition each"):
                for w in range(2):
                    for c in range(3):
                        sp.dma_start(b1[0:HCS[c], w, c:c + 1], b1_l[w, c * HC:c * HC + HCS[c]].unsqueeze(1)).then_inc(w_in, 16)
                sp.dma_start(lg[:, :], io["ln_g"][layer].unsqueeze(1)).then_inc(w_in, 16)
                sp.dma_start(lb[:, :], io["ln_b"][layer].unsqueeze(1)).then_inc(w_in, 16)
            sp.dma_start(b2[:, :], io["b2"][ly, :].broadcast_to((P, D))).then_inc(w_in, 16)
            sp.dma_start(shift[:, :], io["c_shift"]).then_inc(w_in, 16)
            sp.dma_start(carry[:, :], io["c_carry_m"]).then_inc(w_in, 16)

        LOADS = 16 * 14

        @block.tensor
        def _(pe):
            def shift_half(c, r):
                p = r % 2
                at_least(pe, hn_done, base, c, -1)
                out = psH[:, p, 0:4 * WIN].rearrange("p (t d) -> p t d", t=4)
                pe.matmul(out, shift[:, :], sb["xf"][:, bass.ts(c, 4), WIN:D], start=True, stop=False, skip_group_check=True)
                pe.matmul(out[:, 0, :], carry[:, :], last[:, c, :], start=False, stop=False, skip_group_check=True)
                pe.matmul(out[:, 1:4, :], carry[:, :], sb["xf"][:, bass.ds(c * 4, 3), WIN:D], start=False, stop=True, skip_group_check=True).then_inc(shifted, 1)

            def turn(c, r):
                at_least(pe, hn_done, base, c, 1)
                at_least(pe, hT_done, base, c, 0)
                for t in range(4):
                    i = pe.transpose(psT[:, t * P:(t + 1) * P], hn[:, r % 2, t, :], sb["ident"])
                i.then_inc(hnT_done, 1)

            def up(c, r):
                at_least(pe, hT_done, base, c, 1)
                n = 0
                for m in range(3):
                    for w in (1, 0):
                        units(pe, gate_done if (n - 3) % 2 == 0 else act_done, c, (n - 3) // 2 + 1)
                        M = HCS[m]
                        pe.matmul(psU[0:M, n % 3, :], w1[:, w * HID + m * HC:w * HID + m * HC + M], hT[:, r % 2, :],
                                  start=True, stop=True).then_inc(u_done, 1)
                        n += 1

            def down(c, r):
                p = r % 2
                units(pe, act_done, c, 3)
                at_least(pe, y_added, base, c, -1)
                for t in range(4):
                    for m in range(3):
                        M = HCS[m]
                        i = pe.matmul(psY[:, p, t * P:(t + 1) * P], act_t[0:M, p, m, t * P:(t + 1) * P], w2[0:M, m, :],
                                      start=(m == 0), stop=(m == 2))
                i.then_inc(y_done, 1)

            pe.wait_ge(w_in, (layer + 1) * LOADS)
            pe.wait_ge(last_set, (layer + 1) * 3)
            pipelined(pe, NCH, 2, [(0, shift_half), (3, down), (1, turn), (2, up)])

        @block.gpsimd
        def _(pool):
            def powers(c, r):
                p = r % 2
                at_least(pool, mean_done, base, c, 1)
                pool.tensor_tensor(ve[:, p, :], mv[:, p, :, 1], sb["eps"][:, 0:4], ALU.add).then_inc(var_done, 1)
                at_least(pool, var_done, base, c, 1)
                pool.tensor_tensor(rstd[:, p, :], ve[:, p, :], sb["mhalf"][:, 0:4], ALU.pow).then_inc(rstd_done, 1)

            pipelined(pool, NCH, 2, [(0, powers)])

        @block.scalar
        def _(act):
            act.wait_ge(w_in, (layer + 1) * LOADS)

            def affine(c, r):
                at_least(act, hnT_done, base, c, 1)
                units(act, u_done, c, -6, 6)
                act.activation(hT[:, r % 2, :], psT[:, :], ACT.Identity, scale=lg[:, 0:1], bias=lb[:, 0:1]).then_inc(hT_done, 1)

            def gelu(c, r):
                for m in range(3):
                    M = HCS[m]
                    units(act, u_done, c, 2 * m + 1, 6)
                    units(act, act_done, c, m - 2)
                    act.activation(gate[0:M, m, :], psU[0:M, (2 * m) % 3, :], ACT.Gelu, bias=b1[0:M, 1, m:m + 1]).then_inc(gate_done, 1)

            pipelined(act, NCH, 2, [(1, affine), (2, gelu)])

        @block.vector
        def _(dve):
            def statistics(c, r):
                p = r % 2
                at_least(dve, shifted, base, c, 1)
                for t in range(4):
                    dve.bn_stats(stats[:, p, t, 0, :], sb["xf"][:, c * 4 + t, 0:WIN])
                    i = dve.bn_stats(stats[:, p, t, 1, :], psH[:, p, t * WIN:(t + 1) * WIN])
                i.then_inc(stats_done, 1)
                at_least(dve, stats_done, base, c, 1)
                carry_wait(dve, sb)
                for t in range(4):
                    i = dve.bn_aggr(mv[:, p, t, :], stats[:, p, t, :, :].rearrange("p a b -> p (a b)"))
                i.then_inc(mean_done, 1)

            def norm(c, r):
                p = r % 2
                at_least(dve, rstd_done, base, c, 1)
                at_least(dve, hnT_done, base, c, -1)
                for t in range(4):
                    dve.tensor_scalar(hn[:, p, t, 0:WIN], sb["xf"][:, c * 4 + t, 0:WIN], mv[:, p, t, 0:1], rstd[:, p, t:t + 1], ALU.subtract, ALU.mult)
                    i = dve.tensor_scalar(hn[:, p, t, WIN:D], psH[:, p, t * WIN:(t + 1) * WIN], mv[:, p, t, 0:1], rstd[:, p, t:t + 1], ALU.subtract, ALU.mult)
                i.then_inc(hn_done, 1)

            def gated(c, r):
                p = r % 2
                for m in range(3):
                    M = HCS[m]
                    units(dve, u_done, c, 2 * m + 2, 6)
                    units(dve, gate_done, c, m + 1)
                    if m == 0:
                        at_least(dve, y_done, base, c, -1)
                    dve.scalar_tensor_tensor(out=act_t[0:M, p, m, :], in0=psU[0:M, (2 * m + 1) % 3, :], scalar=b1[0:M, 0, m:m + 1],
                                             in1=gate[0:M, m, :], op0=ALU.add, op1=ALU.mult).then_inc(act_done, 1)

            def residual(c, r):
                xs = sb["xf"][:, bass.ts(c, 4), :]
                at_least(dve, y_done, base, c, 1)
                dve.tensor_tensor(xs, xs, psY[:, r % 2, :].rearrange("p (t n) -> p t n", t=4), ALU.add).then_inc(y_added, 1)
                at_least(dve, y_added, base, c, 1)
                dve.tensor_tensor(xs, xs, b2[:, :].unsqueeze(1).broadcast_to((P, 4, D)), ALU.add).then_inc(xf_done, 1)

            dve.memset(last[:, :, :], 0.0).then_inc(last_set, 1)
            dve.wait_ge(last_set, layer * 3 + 1)
            src = sb["xf"].rearrange("p (b u t) n -> p b u t n", b=B, u=2)[:, :, 0, 3, WIN:D]
            dst = last[:, 0:NCH, :].rearrange("p (b u) n -> p b u n", u=2)[:, :, 1, :]
            dve.tensor_copy(dst, src).then_inc(last_set, 2)
            dve.wait_ge(w_in, (layer + 1) * LOADS)
            pipelined(dve, NCH, 2, [(3, residual), (0, statistics), (2, gated), (0, norm)])


def last_norm(nc, io, sb):
    with ExitStack() as ctx:
        def tile(name, shape, dt=F32):
            return ctx.enter_context(nc.sbuf_tensor(name, shape, dt))

        def sem(name):
            return ctx.enter_context(nc.semaphore("l_" + name))

        stats, mv = tile("l_stats", [P, 2, 4, 6]), tile("l_mv", [P, 2, 4, 2])
        ve, rstd = tile("l_ve", [P, 2, 4]), tile("l_rstd", [P, 2, 4])
        yn, y = tile("l_yn", [P, 2, 4, D]), tile("l_y", [P, 2, 4, D])
        stats_done, mean_done, var_done, rstd_done, yn_done, y_done = (sem(x) for x in ("stats_done", "mean_done", "var_done", "rstd_done", "yn_done", "y_done"))
        y_out = [sem("y_out0"), sem("y_out1")]
        block = ctx.enter_context(nc.Block())
        out_v = io["out"].rearrange("b (t p) c -> p (b t) c", p=P)

        @block.sync
        def _(sp):
            with sp.Fori(0, NCH // 2) as pair:
                for p in range(2):
                    c = pair * 2 + p
                    sp.wait_ge(y_done, c + 1)
                    sp.dma_start(out_v[:, bass.ts(c, 4), :], y[:, p, :, :]).then_inc(y_out[p], 16)
            for p in range(2):
                sp.wait_ge(y_out[p], 16 * (NCH // 2))

        @block.gpsimd
        def _(pool):
            def powers(c, r):
                p = r % 2
                at_least(pool, mean_done, 0, c, 1)
                pool.tensor_tensor(ve[:, p, :], mv[:, p, :, 1], sb["eps"][:, 0:4], ALU.add).then_inc(var_done, 1)
                at_least(pool, var_done, 0, c, 1)
                pool.tensor_tensor(rstd[:, p, :], ve[:, p, :], sb["mhalf"][:, 0:4], ALU.pow).then_inc(rstd_done, 1)

            pipelined(pool, NCH, 2, [(0, powers)])

        @block.vector
        def _(dve):
            def moments(c, r):
                p = r % 2
                for t in range(4):
                    i = dve.bn_stats(stats[:, p, t, :], sb["xf"][:, c * 4 + t, :])
                i.then_inc(stats_done, 1)
                at_least(dve, stats_done, 0, c, 1)
                carry_wait(dve, sb)
                for t in range(4):
                    i = dve.bn_aggr(mv[:, p, t, :], stats[:, p, t, :])
                i.then_inc(mean_done, 1)

            def finish(c, r):
                p = r % 2
                at_least(dve, rstd_done, 0, c, 1)
                for t in range(4):
                    i = dve.tensor_scalar(yn[:, p, t, :], sb["xf"][:, c * 4 + t, :], mv[:, p, t, 0:1], rstd[:, p, t:t + 1], ALU.subtract, ALU.mult)
                i.then_inc(yn_done, 1)
                at_least(dve, yn_done, 0, c, 1)
                if not isinstance(c, int) or c >= 2:
                    dve.wait_ge(y_out[p], (c - p) * 8)
                dve.tensor_tensor(y[:, p, :, :], yn[:, p, :, :], sb["x"][:, bass.ts(c, 4), :], ALU.add).then_inc(y_done, 1)

            pipelined(dve, NCH, 2, [(0, moments), (1, finish)])


def latent_attention_and_window_layers(nc, io):
    io["q_parts"] = nc.dram_tensor("q_parts", (B, NH, 3, DK, S), BF16).ap()
    io["k_parts"] = nc.dram_tensor("k_parts", (B, NH, 3, DK, S), BF16).ap()
    with ExitStack() as ctx:
        def tile(name, shape, dt=F32):
            return ctx.enter_context(nc.sbuf_tensor(name, shape, dt))

        sb = {
            "x": tile("x_sb", [P, NT, D])[:, :, :],
            "ident": tile("ident", [P, P])[:, :],
            "ident_b": tile("ident_b", [P, P], BF16)[:, :],
            "mhalf": tile("mhalf", [P, 16])[:, :],
            "eps": tile("eps", [P, 16])[:, :],
            "spare": tile("spare", [P, 1])[:, :],
            "carry": tile("carry", [P, TB])[:, :],
            "xf": tile("xf_sb", [P, NT, D])[:, :, :],
        }
        with ExitStack() as first:
            def early(name, shape, dt=F32):
                return first.enter_context(nc.sbuf_tensor(name, shape, dt))[:]

            sb["mask_q"] = early("mask_q", [P, P], BF16)
            sb["mask_k"] = early("mask_k", [P, P], BF16)
            sb["w_down"] = early("w_down", [P, 2 * DC])
            sb["w_uq"] = early("w_uq", [DC, D])
            sb["w_ukv"] = early("w_ukv", [2 * DC, 2 * D])
            sb["w_o"] = early("w_o", [P, D])
            sb["v_all"] = early("v_all", [P, NG, NT, HG * VA])
            project(nc, io, sb)
            sb["o_tok"] = early("o_tok", [P, NT, D])
            attend(nc, io, sb)
            mix(nc, io, sb)
        sb["mask_w"] = tile("mask_w", [P, TB, KEYS], BF16)[:, :, :]
        with nc.Fori(0, DEPTH) as layer:
            window(nc, io, sb, layer)
            mlp(nc, io, sb, layer)
        last_norm(nc, io, sb)


def constants():
    bf, f = mybir.dt.np(BF16), np.float32
    c = {"c_ident": np.eye(P, dtype=f), "c_ident_b": np.eye(P).astype(bf)}
    i, j = np.arange(P)[:, None], np.arange(P)[None, :]
    c["c_mask_q"] = np.where(j > i, NEG, 0.0).astype(bf)
    c["c_mask_k"] = np.where(i > j, NEG, 0.0).astype(bf)
    c["c_zero"] = np.zeros((KROWS - ROWS, HG, S), bf)
    sel = np.zeros((KROWS - ROWS, NG, HG, S), bf)
    for h in range(HG):
        sel[3 * h:3 * h + 3, :, h, :] = 1
    c["c_sel"] = sel
    key = np.concatenate([np.arange(P), np.arange(-WIN, 0)])[None, :]
    ok = (key <= i) & (i <= key + WIN)
    mask = np.broadcast_to(ok[:, None, :], (P, TB, KEYS)).copy()
    mask[:, 0, P:] = False
    c["c_mask_w"] = np.where(mask, 0.0, NEG).astype(bf)
    c["c_carry"] = np.broadcast_to((np.arange(TB) > 0).astype(f), (P, TB)).copy()
    c["c_shift"] = np.eye(P, k=1, dtype=f)
    c["c_carry_m"] = np.zeros((P, P), f)
    c["c_carry_m"][P - 1, 0] = 1
    half = np.arange(0, DH, 2, dtype=f)
    inv = (f(1.0) / np.power(f(10000.0), half / f(DH))).astype(f)
    t = np.arange(S, dtype=f)
    freqs = (t[:, None] * inv[None, :]).astype(f)
    base = ((half + f(0.4 * DH)) / f(1.4 * DH)).astype(f)
    power = ((t - f(S // 2)) / f(WIN // 2)).astype(f)
    scale = np.power(base[None, :], power[:, None]).astype(f)
    cos, sin = np.cos(freqs).astype(f), np.sin(freqs).astype(f)
    two = lambda a, b: np.concatenate([a, b], axis=-1)
    cosines = np.stack([two(cos * scale, cos * scale), two(cos / scale, cos / scale)], 1)
    sines = np.stack([two(-sin * scale, sin * scale), two(-sin / scale, sin / scale)], 1)
    for name, x in (("c_cos", cosines), ("c_sin", sines)):
        c[name] = np.ascontiguousarray(x.reshape(TB, P, 2, DH).transpose(1, 0, 2, 3).astype(f))
    return c


_INS = {"x": "L0_attn_x", "W_dq": "L0_attn_W_dq", "W_uq": "L0_attn_W_uq", "W_dkv": "L0_attn_W_dkv",
        "W_uk": "L0_attn_W_uk", "W_uv": "L0_attn_W_uv", "W_o": "L0_attn_W_o", "wqkv": "L0_ffn_wqkv",
        "q_scale": "L0_ffn_q_scale", "k_scale": "L0_ffn_k_scale", "wo": "L0_ffn_wo", "ln_g": "L0_ffn_ln_g",
        "ln_b": "L0_ffn_ln_b", "w1": "L0_ffn_w1", "b1": "L0_ffn_b1", "w2": "L0_ffn_w2", "b2": "L0_ffn_b2"}


def kernel(**inputs):
    import concourse.bacc as bacc
    from concourse.bass_utils import run_bass_kernel_spmd as run

    nc = bacc.Bacc("TRN2", target_bir_lowering=False, num_devices=1)
    nc.disable_value_cache = True
    arrays, io = {}, {}
    given = {short: np.ascontiguousarray(inputs[name]) for short, name in _INS.items()}
    for short, a in {**given, **constants()}.items():
        arrays["in_" + short] = a
        io[short] = nc.dram_tensor("in_" + short, a.shape, mybir.dt.from_np(a.dtype), kind="ExternalInput").ap()
    io["out"] = nc.dram_tensor("out_x", (B, S, D), F32, kind="ExternalOutput").ap()
    latent_attention_and_window_layers(nc, io)
    return run(nc, [arrays], core_ids=[0]).results[0]["out_x"]
```

```python
from contextlib import ExitStack

import numpy as np
import concourse.bass as bass
from concourse import mybir

F32 = mybir.dt.float32
BF16 = mybir.dt.bfloat16
ALU = mybir.AluOpType
ACT = mybir.ActivationFunctionType
AX = mybir.AxisListType

B, S, D = 4, 1024, 128
P = 128
NT = B * S // P
TB = S // P
NCH = NT // 4
NH, DK, DC = 16, 8, 32
HG = 4
NG = NH // HG
NPAIR = 9
ROWS = NPAIR * DK
KROWS = 96
NM = 3 * HG
VA = DK + 1
VPAD = 32 - VA
SCALE0 = float(1.0 / np.sqrt(np.float32(DK)))
NEG = -1e30
EPS = 1e-5
DEPTH, HEADS, DH, WIN = 2, 8, 64, 64
INNER = HEADS * DH
QK_SCALE = 8.0
KEYS = 3 * WIN
HID = int(D * 4 * 2 / 3)
HC = 114
HCS = [HC, HC, HID - 2 * HC]


def ge(eng, sem, count):
    if isinstance(count, int) and count <= 0:
        return
    eng.wait_ge(sem, count)


def carry_wait(dve, sb):
    dve.memset(sb["spare"], 0.0)


def project(nc, io, sb):
    with ExitStack() as ctx:
        def tile(name, shape, dt=F32):
            return ctx.enter_context(nc.sbuf_tensor(name, shape, dt))

        def sem(name):
            return ctx.enter_context(nc.semaphore(name))

        stats = tile("p_stats", [P, 2, 4, 6])
        mv = tile("p_mv", [P, 2, 4, 2])
        rstd = tile("p_rstd", [P, 2, 4])
        ve = tile("p_ve", [P, 2, 4])
        xn = tile("p_xn", [P, 2, 4, D])
        xnT = tile("p_xnT", [P, 2, 512])
        cT = tile("p_cT", [2 * DC, 2, 512])
        rem = tile("p_rem", [P, 2, 2, 512])
        parts = tile("p_parts", [P, 2, 2, 3, 512], BF16)
        psT = ctx.enter_context(nc.psum_tensor("p_psT", [P, 2, 512], F32))
        psC = ctx.enter_context(nc.psum_tensor("p_psC", [P, 2, 512], F32))
        psQK = ctx.enter_context(nc.psum_tensor("p_psQK", [P, 2, 512], F32))
        psV = ctx.enter_context(nc.psum_tensor("p_psV", [P, 512], F32))

        x_first, x_rest, w_in = sem("x_first"), sem("x_rest"), sem("w_in")
        stats_done, mean_done, var_done, rstd_done = sem("stats_done"), sem("mean_done"), sem("var_done"), sem("rstd_done")
        xn_done, xnT_done, xnT_copied = sem("xn_done"), sem("xnT_done"), sem("xnT_copied")
        c_done, c_copied = sem("c_done"), sem("c_copied")
        qk_done, v_done, v_copied = sem("qk_done"), sem("v_done"), sem("v_copied")
        hi_done, rem1_done, mid_done, parts_done = sem("hi_done"), sem("rem1_done"), sem("mid_done"), sem("parts_done")
        parts_out = [sem("parts_out0"), sem("parts_out1")]
        ones_set = sem("ones_set")

        block = ctx.enter_context(nc.Block())
        x_v = io["x"].rearrange("b (t p) c -> p (b t) c", p=P)

        @block.sync
        def _(sp):
            sp.dma_start(sb["x"][:, 0:4, :], x_v[:, 0:4, :]).then_inc(x_first, 16)
            sp.dma_start(sb["x"][:, 4:NT, :], x_v[:, 4:NT, :]).then_inc(x_rest, 16)
            with sp.Fori(0, NCH // 2) as pair:
                for par in range(2):
                    c = pair * 2 + par
                    sp.wait_ge(parts_done, 2 * c + 2)
                    for w, name in ((0, "q_parts"), (1, "k_parts")):
                        for a in range(3):
                            sp.dma_start(io[name][pair, :, a, :, 512 * par:512 * par + 512],
                                         parts[:, par, w, a, :]).then_inc(parts_out[par], 16)
            for par in range(2):
                sp.wait_ge(parts_out[par], 16 * 6 * (NCH // 2))

        @block.scalar
        def _(act):
            loads = [(sb["ident"], io["c_ident"]), (sb["w_down"][:, 0:DC], io["W_dq"]), (sb["w_down"][:, DC:2 * DC], io["W_dkv"]),
                     (sb["w_uq"][0:DC, :], io["W_uq"]), (sb["w_ukv"][DC:2 * DC, 0:D], io["W_uk"]),
                     (sb["w_ukv"][DC:2 * DC, D:2 * D], io["W_uv"])]
            for dst, src in loads:
                act.dma_start(dst, src).then_inc(w_in, 16)

            def copy_xnT(c, par):
                act.wait_ge(xnT_done, c + 1)
                ge(act, c_done, c - 1)
                act.activation(xnT[:, par, :], psT[:, par, :], ACT.Copy).then_inc(xnT_copied, 1)

            def copy_c(c, par):
                act.wait_ge(c_done, c + 1)
                ge(act, v_done, c - 1)
                act.activation(cT[:, par, :], psC[0:2 * DC, par, :], ACT.Copy).then_inc(c_copied, 1)

            def copy_v(c, par):
                act.wait_ge(v_done, c + 1)
                for g in range(NG):
                    src = psV[:, :].rearrange("p (t g j d) -> p g t j d", t=4, g=NG, j=HG)[:, g]
                    dst = sb["v_all"][:, g, bass.ts(c, 4), :].rearrange("p t (j a) -> p t j a", a=VA)[:, :, :, 0:DK]
                    i = act.activation(dst, src, ACT.Copy)
                i.then_inc(v_copied, 1)

            act.wait_ge(ones_set, 3)
            copy_xnT(0, 0)
            copy_c(0, 0)
            copy_v(0, 0)
            copy_xnT(1, 1)
            copy_c(1, 1)
            copy_v(1, 1)
            with act.Fori(1, NCH // 2) as pair:
                for par in range(2):
                    copy_xnT(pair * 2 + par, par)
                    copy_c(pair * 2 + par, par)
                    copy_v(pair * 2 + par, par)

        @block.gpsimd
        def _(pool):
            pool.memset(sb["mhalf"], -0.5).then_inc(ones_set, 1)
            pool.memset(sb["eps"], EPS).then_inc(ones_set, 1)

            def powers(c, par):
                pool.wait_ge(mean_done, c + 1)
                ge(pool, xn_done, c - 1)
                pool.tensor_tensor(ve[:, par, :], mv[:, par, :, 1], sb["eps"][:, 0:4], ALU.add).then_inc(var_done, 1)
                pool.wait_ge(var_done, c + 1)
                pool.tensor_tensor(rstd[:, par, :], ve[:, par, :], sb["mhalf"][:, 0:4], ALU.pow).then_inc(rstd_done, 1)

            pool.wait_ge(ones_set, 3)
            powers(0, 0)
            powers(1, 1)
            with pool.Fori(1, NCH // 2) as pair:
                for par in range(2):
                    powers(pair * 2 + par, par)

        @block.vector
        def _(dve):
            dve.memset(sb["v_all"][:, :, :, :], 1.0).then_inc(ones_set, 1)

            def mean(c, par):
                for t in range(4):
                    i = dve.bn_stats(stats[:, par, t, :], sb["x"][:, c * 4 + t, :])
                i.then_inc(stats_done, 1)
                dve.wait_ge(stats_done, c + 1)
                ge(dve, xn_done, c - 1)
                ge(dve, rstd_done, c - 1)
                carry_wait(dve, sb)
                for t in range(4):
                    i = dve.bn_aggr(mv[:, par, t, :], stats[:, par, t, :])
                i.then_inc(mean_done, 1)

            def norm(c, par):
                dve.wait_ge(rstd_done, c + 1)
                ge(dve, xnT_done, c - 1)
                for t in range(4):
                    i = dve.tensor_scalar(xn[:, par, t, :], sb["x"][:, c * 4 + t, :], mv[:, par, t, 0:1],
                                          rstd[:, par, t:t + 1], ALU.subtract, ALU.mult)
                i.then_inc(xn_done, 1)

            def cut(c, par):
                if not isinstance(c, int) or c >= 2:
                    dve.wait_ge(parts_out[par], (c - par) * (8 * 6))
                for w in range(2):
                    dve.wait_ge(qk_done, 2 * c + w + 1)
                    dve.tensor_copy(parts[:, par, w, 0, :], psQK[:, w, :]).then_inc(hi_done, 1)
                    dve.wait_ge(hi_done, 2 * c + w + 1)
                    dve.tensor_tensor(rem[:, par, w, :], psQK[:, w, :], parts[:, par, w, 0, :], ALU.subtract).then_inc(rem1_done, 1)
                    dve.wait_ge(rem1_done, 2 * c + w + 1)
                    dve.tensor_copy(parts[:, par, w, 1, :], rem[:, par, w, :]).then_inc(mid_done, 1)
                    dve.wait_ge(mid_done, 2 * c + w + 1)
                    dve.tensor_tensor(parts[:, par, w, 2, :], rem[:, par, w, :], parts[:, par, w, 1, :], ALU.subtract).then_inc(parts_done, 1)

            dve.wait_ge(x_first, 16)
            mean(0, 0)
            dve.wait_ge(x_rest, 16)
            norm(0, 0)
            mean(1, 1)
            cut(0, 0)
            norm(1, 1)
            mean(2, 0)
            cut(1, 1)
            with dve.Fori(1, NCH // 2 - 1) as pair:
                for par in range(2):
                    c = pair * 2 + par
                    norm(c, par)
                    mean(c + 1, 1 - par)
                    cut(c, par)
            norm(NCH - 2, 0)
            mean(NCH - 1, 1)
            cut(NCH - 2, 0)
            norm(NCH - 1, 1)
            cut(NCH - 1, 1)

        @block.tensor
        def _(pe):
            pe.wait_ge(w_in, 16 * 6)

            def transposes(c, par):
                pe.wait_ge(xn_done, c + 1)
                ge(pe, xnT_copied, c - 1)
                for t in range(4):
                    i = pe.transpose(psT[:, par, t * P:(t + 1) * P], xn[:, par, t, :], sb["ident"])
                i.then_inc(xnT_done, 1)

            def latents(c, par):
                pe.wait_ge(xnT_copied, c + 1)
                ge(pe, c_copied, c - 1)
                pe.matmul(psC[0:2 * DC, par, :], sb["w_down"], xnT[:, par, :], start=True, stop=True).then_inc(c_done, 1)

            def heads(c, par):
                pe.wait_ge(c_copied, c + 1)
                ge(pe, rem1_done, 2 * c - 1)
                pe.matmul(psQK[:, 0, :], sb["w_uq"][0:DC, :], cT[0:DC, par, :], start=True, stop=True).then_inc(qk_done, 1)
                ge(pe, rem1_done, 2 * c)
                pe.matmul(psQK[:, 1, :], sb["w_ukv"][DC:2 * DC, 0:D], cT[DC:2 * DC, par, :], start=True, stop=True).then_inc(qk_done, 1)
                ge(pe, v_copied, c)
                for t in range(4):
                    i = pe.matmul(psV[:, t * P:(t + 1) * P], cT[DC:2 * DC, par, t * P:(t + 1) * P],
                                  sb["w_ukv"][DC:2 * DC, D:2 * D], start=True, stop=True)
                i.then_inc(v_done, 1)

            for c in range(2):
                transposes(c, c)
                latents(c, c)
                heads(c, c)
            with pe.Fori(1, NCH // 2) as pair:
                for par in range(2):
                    c = pair * 2 + par
                    transposes(c, par)
                    latents(c, par)
                    heads(c, par)


MAX_UNITS = [(i, j, kc) for i in range(TB) for j in range(HG) for kc in range(i // 4 + 1)]
EXP_GROUPS = [(qc, kt) for qc in range(2) for kt in range(4 * qc + 4)]
NMU, NEG_ = len(MAX_UNITS), len(EXP_GROUPS)
NEU = NEG_ * HG
NM_A = sum(1 for i, _, _ in MAX_UNITS if i < 4)
assert NMU == NEU


def attend(nc, io, sb):
    with ExitStack() as ctx:
        def tile(name, shape, dt=F32):
            return ctx.enter_context(nc.sbuf_tensor(name, shape, dt))

        def sem(name):
            return ctx.enter_context(nc.semaphore(name))

        qs = tile("a_qs", [KROWS, NG, HG, S], BF16)
        ks = tile("a_ks", [KROWS, NG, HG, S], BF16)
        vs = [tile(f"a_vs{g}", [P, TB * HG * VA + VPAD]) for g in range(NG)]
        prob = [tile(f"a_prob{r}", [P, HG, 512]) for r in range(3)]
        oT = tile("a_oT", [P, 2, 512])
        mx = tile("a_mx", [P, 2, TB, HG, 2])
        nm = tile("a_nm", [P, 2, 4 * HG])
        nmr = tile("a_nmr", [P, 2, 4 * HG])
        nmp = tile("a_nmp", [P, TB, HG, 3], BF16)
        nmT = tile("a_nmT", [NM, S], BF16)
        rec = tile("a_rec", [P, 2, 4, HG])
        spare = tile("a_spare", [P, 6])
        psM = ctx.enter_context(nc.psum_tensor("a_psM", [P, 2, 512], F32))
        psE = ctx.enter_context(nc.psum_tensor("a_psE", [P, 3, 512], F32))
        psO = ctx.enter_context(nc.psum_tensor("a_psO", [P, 2, 512], F32))
        psX = ctx.enter_context(nc.psum_tensor("a_psX", [P, 512], F32))
        psXb = psX[:, :].bitcast(BF16)

        const_in = sem("const_in")
        stack_in = [sem(f"stack_in{g}") for g in range(NG)]
        nm_in = [sem("nm_in_a"), sem("nm_in_b")]
        max_ready, max_read = sem("max_ready"), sem("max_read")
        score_ready, exp_done, av_done = sem("score_ready"), sem("exp_done"), sem("av_done")
        nm_step, nm_parts, nm_T, nm_copied = sem("nm_step"), sem("nm_parts"), sem("nm_T"), sem("nm_copied")
        o_copied, o_T, rec_done, o_read = sem("o_copied"), sem("o_T"), sem("rec_done"), sem("o_read")
        pad_set = sem("pad_set")
        C_MAX, C_EXP, C_AV, C_O, C_T, C_R = 2, 3, 3, 2, 2, 1

        block = ctx.enter_context(nc.Block())
        NSTAGE = B * NG
        LOADS = 16 * (4 * HG + 2)

        def load_group(sp, b, g):
            for j in range(HG):
                for a in range(3):
                    q_src = io["q_parts"][b, g * HG + j, a]
                    sp.dma_start(qs[3 * DK * a:3 * DK * (a + 1), g, j, :], q_src.unsqueeze(0).broadcast_to((3, DK, S))).then_inc(stack_in[g], 16)
                k_src = io["k_parts"][b, g * HG + j].rearrange("r d n -> (r d) n")
                sp.dma_start(ks[0:ROWS, g, j, :], k_src.unsqueeze(0).broadcast_to((3, 3 * DK, S))).then_inc(stack_in[g], 16)
            sp.dma_start(qs[ROWS:KROWS, g, :, :], io["c_zero"]).then_inc(stack_in[g], 16)
            sp.dma_start(vs[g][:, 0:TB * HG * VA], sb["v_all"][:, g, bass.ts(b, TB), :].rearrange("p t a -> p (t a)")).then_inc(stack_in[g], 16)

        @block.sync
        def _(sp):
            sp.dma_start(ks[ROWS:KROWS, :, :, :], io["c_sel"]).then_inc(const_in, 16)
            for dst, src in ((sb["ident_b"], io["c_ident_b"]), (sb["mask_q"], io["c_mask_q"]), (sb["mask_k"], io["c_mask_k"])):
                sp.dma_start(dst, src).then_inc(const_in, 16)
            for g in range(NG):
                load_group(sp, 0, g)
            with sp.Fori(0, B - 1) as b:
                for g in range(NG):
                    sp.wait_ge(av_done, (b * NG + g) * NEG_ + NEG_ + C_AV)
                    load_group(sp, b + 1, g)

        @block.gpsimd
        def _(pool):
            for g in range(NG):
                pool.memset(vs[g][:, TB * HG * VA:], 0.0).then_inc(pad_set, 1)

        @block.tensor
        def _(pe):
            pe.wait_ge(const_in, 64)
            pe.wait_ge(pad_set, NG)

            def max_unit(s, g, u):
                i, j, kc = MAX_UNITS[u]
                n = min(512, (i + 1) * P - 512 * kc)
                out = psM[:, u % 2, 0:n]
                diag = kc == i // 4
                pe.wait_ge(max_read, s * NMU + (u + 1))
                mm = pe.matmul(out, qs[:, g, j, i * P:(i + 1) * P], ks[:, g, j, 512 * kc:512 * kc + n],
                               start=True, stop=not diag)
                if diag:
                    mm = pe.matmul(out[:, n - P:n], sb["ident_b"], sb["mask_q"], start=False, stop=True)
                mm.then_inc(max_ready, 1)

            def score(e, g, n, j):
                qc, kt = EXP_GROUPS[n]
                q0 = max(512 * qc, kt * P)
                w = 512 * (qc + 1) - q0
                diag = kt * P >= 512 * qc
                u = n * HG + j
                pe.wait_ge(exp_done, e * NEU + (u + 1))
                out = psE[:, u % 3, 0:w]
                mm = pe.matmul(out, ks[:, g, j, kt * P:(kt + 1) * P], qs[:, g, j, q0:q0 + w], start=True, stop=not diag)
                if diag:
                    mm = pe.matmul(out[:, 0:P], sb["ident_b"], sb["mask_k"], start=False, stop=True)
                mm.then_inc(score_ready, 1)

            def values(e, g, n):
                qc, kt = EXP_GROUPS[n]
                q0 = max(0, kt * P - 512 * qc)
                pe.wait_ge(exp_done, e * NEU + (n + 1) * HG + C_EXP)
                if kt == 0:
                    pe.wait_ge(o_copied, e * 2 + qc + 1)
                for j in range(HG):
                    mm = pe.matmul(psO[32 * j:32 * j + 32, qc, q0:512],
                                   vs[g][:, kt * HG * VA + j * VA:kt * HG * VA + j * VA + 32],
                                   prob[n % 3][:, j, 0:512 - q0], start=(kt == 0), stop=(kt == 4 * qc + 3),
                                   skip_group_check=True)
                mm.then_inc(av_done, 1)

            def turn_maxima(s, half):
                pe.wait_ge(nm_parts, 2 * s + half + 1)
                ge(pe, o_read, 2 * s - 2 + half + C_R)
                if half == 1:
                    pe.wait_ge(nm_copied, 2 * s + 1)
                for t in range(4):
                    i = 4 * half + t
                    mm = pe.transpose(psXb[0:NM, t * P:(t + 1) * P], nmp[:, i, :, :].rearrange("p j a -> p (j a)"), sb["ident_b"])
                mm.then_inc(nm_T, 1)

            def turn_outputs(e, qc, maxima):
                pe.wait_ge(o_copied, 2 * e + qc + 1 + C_O)
                if maxima:
                    pe.wait_ge(nm_copied, 2 * e + 2 + qc + 1)
                else:
                    pe.wait_ge(o_read, 2 * e + qc + C_R)
                for t in range(4):
                    mm = pe.transpose(psX[:, t * P:(t + 1) * P], oT[:, qc, t * P:(t + 1) * P], sb["ident"])
                mm.then_inc(o_T, 1)

            def slot(e, g, more):
                g1 = (g + 1) % NG
                if more:
                    pe.wait_ge(stack_in[g1], ((e + 1 - g1) * (LOADS // NG)) + LOADS)
                for n in range(NEG_):
                    if n == 0:
                        pe.wait_ge(nm_in[0], 16 * e + 16)
                    if n == 4:
                        pe.wait_ge(nm_in[1], 16 * e + 16)
                    for j in range(HG):
                        score(e, g, n, j)
                        if more:
                            max_unit(e + 1, g1, n * HG + j)
                    if n:
                        values(e, g, n - 1)
                    if n == 5 and more:
                        turn_maxima(e + 1, 0)
                    if n == 6:
                        turn_outputs(e, 0, more)
                values(e, g, NEG_ - 1)
                if more:
                    turn_maxima(e + 1, 1)
                turn_outputs(e, 1, more)

            pe.wait_ge(stack_in[0], LOADS)
            for u in range(NMU):
                max_unit(0, 0, u)
            turn_maxima(0, 0)
            turn_maxima(0, 1)
            with pe.Fori(0, B - 1) as b:
                for g in range(NG):
                    slot(b * NG + g, g, True)
            for g in range(NG):
                slot((B - 1) * NG + g, g, g < NG - 1)

        @block.scalar
        def _(act):
            def exps(e, n):
                qc, kt = EXP_GROUPS[n]
                w = 512 * (qc + 1) - max(512 * qc, kt * P)
                act.wait_ge(av_done, e * NEG_ + (n + 1))
                for j in range(HG):
                    u = n * HG + j
                    act.wait_ge(score_ready, e * NEU + (u + 1))
                    act.activation(prob[n % 3][:, j, 0:w], psE[:, u % 3, 0:w], ACT.Exp, scale=SCALE0).then_inc(exp_done, 1)

            def copy_maxima(s, half):
                act.wait_ge(nm_T, 2 * s + half + 1)
                if not isinstance(s, int) or s > 0:
                    act.wait_ge(nm_in[half], 16 * s)
                cols = slice(512 * half, 512 * half + 512)
                act.activation(nmT[:, cols], psXb[0:NM, 0:512], ACT.Copy).then_inc(nm_copied, 1)

            def send_maxima(s, g, half):
                act.wait_ge(nm_copied, 2 * s + half + 1)
                cols = slice(512 * half, 512 * half + 512)
                act.dma_start(qs[ROWS:ROWS + NM, g, :, cols], nmT[:, cols].unsqueeze(1).broadcast_to((NM, HG, 512))).then_inc(nm_in[half], 16)

            def copy_outputs(e, qc):
                act.wait_ge(av_done, e * NEG_ + (4 if qc == 0 else NEG_) + C_AV)
                act.wait_ge(o_T, 2 * e + qc - 1 + C_T)
                act.activation(oT[:, qc, :], psO[:, qc, :], ACT.Copy).then_inc(o_copied, 1)

            def slot(e, g, more):
                g1 = (g + 1) % NG
                for n in range(NEG_):
                    exps(e, n)
                    if n == 5:
                        copy_outputs(e, 0)
                    if n == 6 and more:
                        copy_maxima(e + 1, 0)
                        send_maxima(e + 1, g1, 0)
                if more:
                    copy_maxima(e + 1, 1)
                    send_maxima(e + 1, g1, 1)
                copy_outputs(e, 1)

            for half in range(2):
                copy_maxima(0, half)
                send_maxima(0, 0, half)
            with act.Fori(0, B - 1) as b:
                for g in range(NG):
                    slot(b * NG + g, g, True)
            for g in range(NG):
                slot((B - 1) * NG + g, g, g < NG - 1)
            for half in range(2):
                act.wait_ge(nm_in[half], 16 * NSTAGE)

        @block.vector
        def _(dve):
            dve.memset(spare[:, 0:1], 0.0).then_inc(max_read, C_MAX)
            dve.memset(spare[:, 1:2], 0.0).then_inc(exp_done, C_EXP)
            dve.memset(spare[:, 2:3], 0.0).then_inc(av_done, C_AV)
            dve.memset(spare[:, 3:4], 0.0).then_inc(o_copied, C_O)
            dve.memset(spare[:, 4:5], 0.0).then_inc(o_T, C_T)
            dve.memset(spare[:, 5:6], 0.0).then_inc(o_read, C_R)

            def maximum(s, u):
                i, j, kc = MAX_UNITS[u]
                n = min(512, (i + 1) * P - 512 * kc)
                dve.wait_ge(max_ready, s * NMU + (u + 1))
                dve.tensor_reduce(mx[:, 0, i, j, kc:kc + 1], psM[:, u % 2, 0:n], AX.X, ALU.max).then_inc(max_read, 1)

            def cut_maxima(s, half):
                upto = NM_A if half == 0 else NMU
                dve.wait_ge(max_read, s * NMU + upto + C_MAX)
                ge(dve, nm_T, 2 * s + half - 1)
                step = s * 8 + 4 * half
                tiles = slice(4 * half, 4 * half + 4)
                dve.tensor_reduce(nm[:, half, :], mx[:, 0, tiles, :, 0:half + 1].rearrange("p i j k -> p (i j) k"), AX.X, ALU.max, negate=True).then_inc(nm_step, 1)
                dve.wait_ge(nm_step, step + 1)
                part = [nmp[:, tiles, :, a].rearrange("p i j -> p (i j)") for a in range(3)]
                dve.tensor_copy(part[0], nm[:, half, :]).then_inc(nm_step, 1)
                dve.wait_ge(nm_step, step + 2)
                dve.tensor_tensor(nmr[:, half, :], nm[:, half, :], part[0], ALU.subtract).then_inc(nm_step, 1)
                dve.wait_ge(nm_step, step + 3)
                dve.tensor_copy(part[1], nmr[:, half, :]).then_inc(nm_step, 1)
                dve.wait_ge(nm_step, step + 4)
                dve.tensor_tensor(part[2], nmr[:, half, :], part[1], ALU.subtract).then_inc(nm_parts, 1)

            def outputs(b, e, g, qc):
                ps = psX[:, :].rearrange("p (t j c) -> p t j c", t=4, j=HG)
                dve.wait_ge(o_T, 2 * e + qc + 1 + C_T)
                dve.reciprocal(rec[:, qc, :, :], ps[:, :, :, DK]).then_inc(rec_done, 1)
                dve.wait_ge(rec_done, 2 * e + qc + 1)
                out = sb["o_tok"][:, bass.ts(b * 2 + qc, 4), g * HG * DK:(g + 1) * HG * DK].rearrange("p t (j d) -> p t j d", d=DK)
                dve.tensor_tensor(out, ps[:, :, :, 0:DK], rec[:, qc, :, :].unsqueeze(3).broadcast_to((P, 4, HG, DK)), ALU.mult).then_inc(o_read, 1)

            def slot(b, g, more):
                e = b * NG + g
                for u in range(NMU):
                    if more:
                        maximum(e + 1, u)
                    if u == NM_A - 1 and more:
                        cut_maxima(e + 1, 0)
                    if u == 27:
                        outputs(b, e, g, 0)
                if more:
                    cut_maxima(e + 1, 1)
                outputs(b, e, g, 1)

            for u in range(NMU):
                maximum(0, u)
                if u == NM_A - 1:
                    cut_maxima(0, 0)
            cut_maxima(0, 1)
            with dve.Fori(0, B - 1) as b:
                for g in range(NG):
                    slot(b, g, True)
            for g in range(NG):
                slot(B - 1, g, g < NG - 1)


def pipelined(eng, n, ring, steps):
    deepest = max(lag for lag, _ in steps)
    first = -(-(deepest + ring) // ring) * ring
    last = n // ring * ring

    def slot(s, place, whole):
        for lag, fn in steps:
            if whole or 0 <= s - lag < n:
                fn(s - lag, (place - lag) % ring)

    first = min(first, last)
    for s in range(first):
        slot(s, s % ring, False)
    if first < last:
        with eng.Fori(first // ring, last // ring) as k:
            for r in range(ring):
                slot(k * ring + r, r, True)
    for s in range(last, n + deepest):
        slot(s, s % ring, False)


def at_least(eng, sem, base, t, k):
    if isinstance(t, int) and t + k <= 0:
        return
    eng.wait_ge(sem, base + t + k)


def mix(nc, io, sb):
    with ExitStack() as ctx:
        def tile(name, shape, dt=F32):
            return ctx.enter_context(nc.sbuf_tensor(name, shape, dt))

        def sem(name):
            return ctx.enter_context(nc.semaphore("m_" + name))

        oc = tile("m_oc", [P, 2, 4, P])
        ocT = tile("m_ocT", [P, 2, 4, P])
        stats = tile("m_stats", [P, 2, 2, 4, 6])
        mv = tile("m_mv", [P, 2, 2, 4, 2])
        ve = tile("m_ve", [P, 2, 2, 4])
        rstd = tile("m_rstd", [P, 2, 2, 4])
        an = tile("m_an", [P, 2, 4, D])
        psT = ctx.enter_context(nc.psum_tensor("m_psT", [P, 2, 512], F32))
        psA = ctx.enter_context(nc.psum_tensor("m_psA", [P, 4, 512], F32))

        w_in, o_staged, oT_done, oT_copied, a_done = sem("w_in"), sem("o_staged"), sem("oT_done"), sem("oT_copied"), sem("a_done")
        stats_done = [sem("stats_a"), sem("stats_x")]
        mean_done = [sem("mean_a"), sem("mean_x")]
        var_done = [sem("var_a"), sem("var_x")]
        rstd_done = [sem("rstd_a"), sem("rstd_x")]
        an_done, x1_done, xf_done = sem("an_done"), sem("x1_done"), sem("xf_done")
        block = ctx.enter_context(nc.Block())

        @block.sync
        def _(sp):
            sp.dma_start(sb["w_o"], io["W_o"]).then_inc(w_in, 16)

        @block.tensor
        def _(pe):
            pe.wait_ge(w_in, 16)

            def turn(c, r):
                at_least(pe, o_staged, 0, c, 1)
                at_least(pe, oT_copied, 0, c, -1)
                p = r % 2
                for t in range(4):
                    i = pe.transpose(psT[:, p, t * P:(t + 1) * P], oc[:, p, t, :], sb["ident"])
                i.then_inc(oT_done, 1)

            def project_out(c, r):
                at_least(pe, oT_copied, 0, c, 1)
                at_least(pe, an_done, 0, c, -3)
                for t in range(4):
                    i = pe.matmul(psA[:, r, t * P:(t + 1) * P], ocT[:, r % 2, t, :], sb["w_o"], start=True, stop=True)
                i.then_inc(a_done, 1)

            pipelined(pe, NCH, 4, [(0, turn), (0, project_out)])

        @block.scalar
        def _(act):
            def copy(c, r):
                at_least(act, oT_done, 0, c, 1)
                at_least(act, a_done, 0, c, -1)
                act.activation(ocT[:, r % 2, :, :].rearrange("p t c -> p (t c)"), psT[:, r % 2, :], ACT.Copy).then_inc(oT_copied, 1)

            pipelined(act, NCH, 4, [(0, copy)])

        @block.gpsimd
        def _(pool):
            def powers(w):
                def fn(c, r):
                    p = r % 2
                    at_least(pool, mean_done[w], 0, c, 1)
                    pool.tensor_tensor(ve[:, w, p, :], mv[:, w, p, :, 1], sb["eps"][:, 0:4], ALU.add).then_inc(var_done[w], 1)
                    at_least(pool, var_done[w], 0, c, 1)
                    pool.tensor_tensor(rstd[:, w, p, :], ve[:, w, p, :], sb["mhalf"][:, 0:4], ALU.pow).then_inc(rstd_done[w], 1)
                return fn

            pipelined(pool, NCH, 4, [(0, powers(0)), (1, powers(1))])

        @block.vector
        def _(dve):
            def stage(c, r):
                at_least(dve, oT_done, 0, c, -1)
                dve.tensor_copy(oc[:, r % 2, :, :], sb["o_tok"][:, bass.ts(c, 4), :]).then_inc(o_staged, 1)

            def moments(w, c, p, source):
                for t in range(4):
                    i = dve.bn_stats(stats[:, w, p, t, :], source(t))
                i.then_inc(stats_done[w], 1)
                at_least(dve, stats_done[w], 0, c, 1)
                carry_wait(dve, sb)
                for t in range(4):
                    i = dve.bn_aggr(mv[:, w, p, t, :], stats[:, w, p, t, :])
                i.then_inc(mean_done[w], 1)

            def moments_a(c, r):
                at_least(dve, a_done, 0, c, 1)
                moments(0, c, r % 2, lambda t: psA[:, r, t * P:(t + 1) * P])

            def residual(c, r):
                p = r % 2
                at_least(dve, rstd_done[0], 0, c, 1)
                for t in range(4):
                    i = dve.tensor_scalar(an[:, p, t, :], psA[:, r, t * P:(t + 1) * P], mv[:, 0, p, t, 0:1],
                                          rstd[:, 0, p, t:t + 1], ALU.subtract, ALU.mult)
                i.then_inc(an_done, 1)
                at_least(dve, an_done, 0, c, 1)
                x = sb["x"][:, bass.ts(c, 4), :]
                dve.tensor_tensor(x, x, an[:, p, :, :], ALU.add).then_inc(x1_done, 1)
                at_least(dve, x1_done, 0, c, 1)
                moments(1, c, p, lambda t: sb["x"][:, c * 4 + t, :])

            def layers_input(c, r):
                p = r % 2
                at_least(dve, rstd_done[1], 0, c, 1)
                for t in range(4):
                    i = dve.tensor_scalar(sb["xf"][:, c * 4 + t, :], sb["x"][:, c * 4 + t, :], mv[:, 1, p, t, 0:1],
                                          rstd[:, 1, p, t:t + 1], ALU.subtract, ALU.mult)
                i.then_inc(xf_done, 1)

            pipelined(dve, NCH, 4, [(0, stage), (1, moments_a), (3, layers_input), (2, residual)])


def window(nc, io, sb, layer):
    base = layer * NT
    with ExitStack() as ctx:
        def tile(name, shape, dt=F32):
            return ctx.enter_context(nc.sbuf_tensor(name, shape, dt))

        def sem(name):
            return ctx.enter_context(nc.semaphore("w_" + name))

        wqkv, wo = tile("w_wqkv", [P, 3 * INNER]), tile("w_wo", [P, 4, D])
        scales = tile("w_scales", [P, 2, DH])
        cos, sin = tile("w_cos", [P, TB, 2, DH]), tile("w_sin", [P, TB, 2, DH])
        xc = tile("w_xc", [P, 2, D])
        hT = tile("w_hT", [P, 2, P + 1])
        sq = tile("w_sq", [P, 2 * INNER])
        ss, ssm, rn = tile("w_ss", [P, 2, 16]), tile("w_ssm", [P, 2, 16]), tile("w_rn", [P, 2, 16])
        raw = tile("w_raw", [P, 2, 2 * INNER])
        t1, t2 = tile("w_t1", [P, 2 * INNER]), tile("w_t2", [P, 2 * INNER])
        rot = tile("w_rot", [P, 2, 2 * INNER])
        qT, kT = tile("w_qT", [P, 2, 4, P]), tile("w_kT", [P, 2, 4, KEYS])
        v = [tile(f"w_v{r}", [P, INNER]) for r in range(4)]
        vb = [tile(f"w_vb{r}", [P, INNER]) for r in range(4)]
        nmx, bias = tile("w_nmx", [P, 2, HEADS]), tile("w_bias", [P, 2, HEADS])
        den, rden = tile("w_den", [P, 2, HEADS]), tile("w_rden", [P, 2, HEADS])
        prob = tile("w_prob", [P, 2, 2, 4, P])
        pT = tile("w_pT", [P, 2, 4, P])
        oT = tile("w_oT", [P, 4, P])
        psQK = ctx.enter_context(nc.psum_tensor("w_psQK", [P, 2, 512], F32))
        psV = ctx.enter_context(nc.psum_tensor("w_psV", [P, 512], F32))
        psT = ctx.enter_context(nc.psum_tensor("w_psT", [P, 2, 512], F32))
        psS = ctx.enter_context(nc.psum_tensor("w_psS", [P, 2, 512], F32))
        psO = ctx.enter_context(nc.psum_tensor("w_psO", [P, 512], F32))

        w_in, tables, zeroed = sem("w_in"), sem("tables"), sem("zeroed")
        xc_in = [sem("xc_in0"), sem("xc_in1")]
        vb_in = [sem(f"vb_in{r}") for r in range(4)]
        xT_done, hT_copied, carried = sem("xT_done"), sem("hT_copied"), sem("carried")
        qk_done, v_done, sq_done, ss_done, ssm_done, rn_done = (sem(x) for x in ("qk_done", "v_done", "sq_done", "ss_done", "ssm_done", "rn_done"))
        v_copied, raw_done, t1_done, t2_done, rot_done, unit_done = (sem(x) for x in ("v_copied", "raw_done", "t1_done", "t2_done", "rot_done", "unit_done"))
        qkT_done, qT_copied, kT_copied, prev_copied = sem("qkT_done"), sem("qT_copied"), sem("kT_copied"), sem("prev_copied")
        s_done, max_done, bias_done, exp_done = sem("s_done"), sem("max_done"), sem("bias_done"), sem("exp_done")
        rden_done, prob_done = sem("rden_done"), sem("prob_done")
        pT_done, pT_copied = [sem("pT_done0"), sem("pT_done1")], [sem("pT_copied0"), sem("pT_copied1")]
        av_done, oT_copied, y_done, xf_done = sem("av_done"), sem("oT_copied"), sem("y_done"), sem("xf_done")
        block = ctx.enter_context(nc.Block())

        def halves(eng, s, t, k):
            if isinstance(t, int) and 2 * t + k <= 0:
                return
            eng.wait_ge(s, base * 2 + t * 2 + k)

        def slots(eng, slot):
            for s in range(8):
                slot(s, s % 4, False)
            with eng.Fori(2, NT // 4 - 1) as k:
                for r in range(4):
                    slot(k * 4 + r, r, True)
            for s in range(NT - 4, NT + 4):
                slot(s, s % 4, False)

        @block.sync
        def _(sp):
            loads = [(wqkv[:, :], io["wqkv"][layer]), (wo[:, :, :], io["wo"][layer].rearrange("(c p) n -> p c n", p=P)),
                     (cos[:, :, :, :], io["c_cos"]), (sin[:, :, :, :], io["c_sin"]), (sb["mask_w"], io["c_mask_w"]), (sb["carry"], io["c_carry"])]
            loads += [(scales[:, w, :], io[name][bass.ds(layer, 1), :].broadcast_to((P, DH))) for w, name in ((0, "q_scale"), (1, "k_scale"))]
            for dst, src in loads:
                sp.dma_start(dst, src).then_inc(w_in, 16)

            def load_x(t, r):
                at_least(sp, xT_done, base, t, -1)
                sp.dma_start(xc[:, r % 2, :], sb["xf"][:, t, :]).then_inc(xc_in[r % 2], 16)

            def spread_v(t, r):
                at_least(sp, v_copied, base, t, 1)
                halves(sp, av_done, t, -4)
                sp.dma_start(vb[r][0:WIN, :], v[r][0:WIN, :]).then_inc(vb_in[r], 16)
                sp.dma_start(vb[(r + 1) % 4][WIN:P, :], v[r][WIN:P, :]).then_inc(vb_in[r], 16)

            sp.wait_ge(zeroed, layer * 3 + 3)
            pipelined(sp, NT, 4, [(0, load_x), (2, spread_v)])

        @block.tensor
        def _(pe):
            def turn_x(t, r):
                p = r % 2
                pe.wait_ge(xc_in[p], (base + t - p) * 8 + 16)
                at_least(pe, pT_copied[0], base, t, -3)
                pe.transpose(psT[:, 0, 0:P], xc[:, p, :], sb["ident"]).then_inc(xT_done, 1)

            def project_qk(t, r, w):
                if w == 0:
                    at_least(pe, hT_copied, base, t, 1)
                    at_least(pe, carried, base, t, 1)
                    at_least(pe, raw_done, base, t, 0)
                pe.matmul(psQK[:, w, :], hT[:, r % 2, 0:P], wqkv[:, w * INNER:(w + 1) * INNER], start=True, stop=True).then_inc(qk_done, 1)

            def project_v(t, r):
                at_least(pe, v_copied, base, t, 0)
                pe.matmul(psV[:, :], hT[:, r % 2, 0:P], wqkv[:, 2 * INNER:3 * INNER], start=True, stop=True).then_inc(v_done, 1)

            def turn_qk(t, r):
                at_least(pe, unit_done, base, t, 1)
                at_least(pe, hT_copied, base, t, 3 if not isinstance(t, int) else min(3, NT - t))
                at_least(pe, pT_copied[1], base, t, -1)
                for w in range(2):
                    for c in range(4):
                        i = pe.transpose(psT[:, w, c * P:(c + 1) * P], rot[:, r % 2, w * INNER + c * P:w * INNER + (c + 1) * P], sb["ident"])
                i.then_inc(qkT_done, 1)

            def scores(t, r, w):
                p = r % 2
                if w == 0:
                    at_least(pe, qT_copied, base, t, 1)
                    at_least(pe, kT_copied, base, t, 1)
                    at_least(pe, prev_copied, base, t, 1)
                halves(pe, exp_done, t, w - 1)
                pe.matmul(psS[:, w, :].rearrange("p (c k) -> p c k", c=4), sb["ident_b"],
                          sb["mask_w"][:, t % TB, :].unsqueeze(1).broadcast_to((P, 4, P)), start=True, stop=False, skip_group_check=True)
                rows = slice(DH * w, DH * w + DH)
                for c in range(4):
                    cols = slice(c * P, (c + 1) * P)
                    lower = kT[rows, p, c, :].rearrange("p (a k) -> p a k", a=3)[:, 0:3:2, :]
                    pe.matmul(psS[0:WIN, w, cols].rearrange("p (a k) -> p a k", a=2), qT[rows, p, c, 0:WIN], lower,
                              start=False, stop=True, skip_group_check=True)
                    i = pe.matmul(psS[WIN:P, w, cols], qT[rows, p, c, WIN:P], kT[rows, p, c, 0:P], start=False, stop=True, skip_group_check=True)
                i.then_inc(s_done, 1)

            def turn_p(t, r, b):
                p = r % 2
                if b == 0:
                    at_least(pe, prob_done, base, t, 1)
                    for copied in (qT_copied, kT_copied):
                        at_least(pe, copied, base, t, 1 if isinstance(t, int) and t == NT - 1 else 2)
                for i4 in range(4):
                    i = pe.transpose(psT[:, b, i4 * P:(i4 + 1) * P], prob[:, p, i4 % 2, 2 * b + i4 // 2, :], sb["ident"])
                i.then_inc(pT_done[b], 1)

            def values(t, r, b):
                at_least(pe, pT_copied[b], base, t, 1)
                if b == 0:
                    at_least(pe, xf_done, base, t, 0)
                    pe.wait_ge(vb_in[r], (base + t - r) * 8 + 32)
                    if not isinstance(t, int) or t > 0:
                        rb = (r - 1) % 4
                        pe.wait_ge(vb_in[rb], (base + t - 1 - rb) * 8 + 32)
                for u, src in ((0, vb[r]), (1, v[r])):
                    for i4 in range(4):
                        h = 4 * b + i4
                        c, w = h // 2, h % 2
                        i = pe.matmul(psO[DH * w:DH * w + DH, c * P + WIN * u:c * P + WIN * (u + 1)], src[:, h * DH:(h + 1) * DH],
                                      pT[:, b, i4, WIN * u:WIN * (u + 1)], start=True, stop=True, skip_group_check=True)
                i.then_inc(av_done, 1)

            def out(t, r):
                at_least(pe, oT_copied, base, t, 1)
                for c in range(4):
                    i = pe.matmul(psO[:, 0:P], oT[:, c, :], wo[:, c, :], start=(c == 0), stop=(c == 3), skip_group_check=True)
                i.then_inc(y_done, 1)

            def slot(s, r, whole):
                def runs(t):
                    return whole or 0 <= t < NT
                r2, r3 = (r - 2) % 4, (r - 3) % 4
                if runs(s):
                    project_qk(s, r, 0)
                    project_qk(s, r, 1)
                if runs(s - 4):
                    out(s - 4, r)
                if runs(s - 2):
                    turn_qk(s - 2, r2)
                if runs(s):
                    project_v(s, r)
                if runs(s - 2):
                    scores(s - 2, r2, 0)
                if runs(s - 3):
                    turn_p(s - 3, r3, 0)
                    turn_p(s - 3, r3, 1)
                if runs(s - 2):
                    scores(s - 2, r2, 1)
                if runs(s - 3):
                    values(s - 3, r3, 0)
                if runs(s + 1):
                    turn_x(s + 1, (r + 1) % 4)
                if runs(s - 3):
                    values(s - 3, r3, 1)

            pe.wait_ge(w_in, (layer + 1) * (8 * 16))
            turn_x(0, 0)
            slots(pe, slot)

        @block.scalar
        def _(act):
            def copy_hT(t, r):
                p = r % 2
                at_least(act, xT_done, base, t, 1)
                at_least(act, v_done, base, t, -1)
                at_least(act, carried, base, t, 0)
                act.activation(hT[0:WIN, p, 0:P], psT[0:WIN, 0, 0:P], ACT.Copy)
                act.activation(hT[WIN:P, p, 1:P + 1], psT[WIN:P, 0, 0:P], ACT.Copy).then_inc(hT_copied, 1)

            def copy_raw(t, r):
                halves(act, qk_done, t, 2)
                for used in (t1_done, t2_done):
                    at_least(act, used, base, t, -1)
                act.activation(raw[:, r % 2, :].rearrange("p (w n) -> p w n", w=2), psQK[:, :, :], ACT.Copy).then_inc(raw_done, 1)

            def squares(t, r):
                at_least(act, raw_done, base, t, 1)
                at_least(act, ss_done, base, t, 0)
                act.activation(sq[:, :], raw[:, r % 2, :], ACT.Square).then_inc(sq_done, 1)

            def copy_v(t, r):
                at_least(act, v_done, base, t, 1)
                halves(act, av_done, t, -6)
                if not isinstance(t, int) or t >= 4:
                    act.wait_ge(vb_in[r], (base + t - r) * 8)
                act.activation(v[r][:, :], psV[:, :], ACT.Copy).then_inc(v_copied, 1)

            def copy_qT(t, r):
                at_least(act, qkT_done, base, t, 1)
                act.activation(qT[:, r % 2, :, :], psT[:, 0, :].rearrange("p (c n) -> p c n", c=4), ACT.Copy).then_inc(qT_copied, 1)

            def exps(t, r, w):
                p = r % 2
                halves(act, bias_done, t, w + 1)
                for c in range(4):
                    n = 4 * w + c
                    i = act.activation(prob[:, p, w, c, :], psS[:, w, c * P:(c + 1) * P], ACT.Exp,
                                       bias=bias[:, p, n:n + 1], scale=QK_SCALE, accum_out=den[:, p, n:n + 1])
                i.then_inc(exp_done, 1)

            def copy_pT(t, r):
                at_least(act, pT_done[0], base, t, 1)
                halves(act, av_done, t, -1)
                act.activation(pT[:, 0, :, :], psT[:, 0, :].rearrange("p (b n) -> p b n", b=4), ACT.Copy).then_inc(pT_copied[0], 1)

            def copy_oT(t, r):
                halves(act, av_done, t, 2)
                at_least(act, y_done, base, t, 0)
                act.activation(oT[:, :, :], psO[:, :].rearrange("p (c n) -> p c n", c=4), ACT.Copy).then_inc(oT_copied, 1)

            def slot(s, r, whole):
                def runs(t):
                    return whole or 0 <= t < NT
                r2, r3 = (r - 2) % 4, (r - 3) % 4
                if runs(s - 4):
                    copy_oT(s - 4, r)
                if runs(s):
                    copy_raw(s, r)
                    squares(s, r)
                if runs(s - 2):
                    copy_qT(s - 2, r2)
                if runs(s):
                    copy_v(s, r)
                if runs(s - 3):
                    copy_pT(s - 3, r3)
                if runs(s - 2):
                    exps(s - 2, r2, 0)
                if runs(s + 1):
                    copy_hT(s + 1, (r + 1) % 4)
                if runs(s - 2):
                    exps(s - 2, r2, 1)

            act.wait_ge(zeroed, layer * 3 + 3)
            copy_hT(0, 0)
            slots(act, slot)

        @block.gpsimd
        def _(pool):
            def rotate(t, r):
                at_least(pool, raw_done, base, t, 1)
                at_least(pool, rot_done, base, t, 0)
                out, src = (x.rearrange("p (w h u d) -> p w h u d", w=2, h=HEADS, u=2) for x in (t2[:, :], raw[:, r % 2, :]))
                for half in range(2):
                    for w in range(2):
                        tab = sin[:, t % TB, w, half * 32:half * 32 + 32].unsqueeze(1).broadcast_to((P, HEADS, 32))
                        i = pool.tensor_tensor(out[:, w, :, half, :], src[:, w, :, 1 - half, :], tab, ALU.mult)
                i.then_inc(t2_done, 1)
                at_least(pool, t1_done, base, t, 1)
                at_least(pool, t2_done, base, t, 1)
                at_least(pool, qkT_done, base, t, -1)
                pool.tensor_tensor(rot[:, r % 2, :], t1[:, :], t2[:, :], ALU.add).then_inc(rot_done, 1)

            def norms(t, r):
                p = r % 2
                at_least(pool, ssm_done, base, t, 1)
                at_least(pool, unit_done, base, t, -1)
                pool.tensor_tensor(rn[:, p, :], ssm[:, p, :], sb["mhalf"][:, 0:16], ALU.pow).then_inc(rn_done, 1)

            pool.wait_ge(tables, layer * 6 + 6)
            pipelined(pool, NT, 4, [(0, rotate), (0, norms)])

        @block.vector
        def _(dve):
            dve.memset(hT[WIN:P, 1, P:P + 1], 0.0).then_inc(zeroed, 1)
            dve.memset(kT[:, 1, :, :], 0.0).then_inc(zeroed, 1)
            dve.memset(vb[0][WIN:P, :], 0.0).then_inc(zeroed, 1)
            dve.wait_ge(w_in, (layer + 1) * (8 * 16))
            for w in range(2):
                sc = scales[:, w, :].unsqueeze(1).broadcast_to((P, TB, DH))
                dve.tensor_tensor(cos[:, :, w, :], cos[:, :, w, :], sc, ALU.mult).then_inc(tables, 1)
                for half in range(2):
                    sc = scales[:, w, 32 - 32 * half:64 - 32 * half].unsqueeze(1).broadcast_to((P, TB, 32))
                    part = sin[:, :, w, 32 * half:32 * half + 32]
                    dve.tensor_tensor(part, part, sc, ALU.mult).then_inc(tables, 1)
            dve.wait_ge(zeroed, layer * 3 + 3)
            dve.wait_ge(tables, layer * 6 + 6)

            def carry(t, r):
                p = r % 2
                at_least(dve, hT_copied, base, t, 0)
                at_least(dve, v_done, base, t, -1)
                dve.tensor_scalar(hT[WIN:P, p, 0:1], hT[WIN:P, 1 - p, P:P + 1], sb["carry"][WIN:P, bass.ds(t % TB, 1)], None,
                                  ALU.mult).then_inc(carried, 1)

            def sums(t, r):
                at_least(dve, sq_done, base, t, 1)
                dve.tensor_reduce(ss[:, r % 2, :], sq[:, :].rearrange("p (h d) -> p h d", d=DH), AX.X, ALU.add).then_inc(ss_done, 1)
                at_least(dve, ss_done, base, t, 1)
                at_least(dve, rn_done, base, t, -1)
                dve.tensor_scalar(ssm[:, r % 2, :], ss[:, r % 2, :], 1e-24, None, ALU.max).then_inc(ssm_done, 1)

            def cosines(t, r):
                at_least(dve, raw_done, base, t, 1)
                at_least(dve, rot_done, base, t, 0)
                dve.tensor_tensor(t1[:, :].rearrange("p (w h d) -> p w h d", w=2, d=DH), raw[:, r % 2, :].rearrange("p (w h d) -> p w h d", w=2, d=DH),
                                  cos[:, t % TB, :, :].unsqueeze(2).broadcast_to((P, 2, HEADS, DH)), ALU.mult).then_inc(t1_done, 1)

            def normalise(t, r):
                p = r % 2
                at_least(dve, rn_done, base, t, 1)
                at_least(dve, rot_done, base, t, 1)
                both = rot[:, p, :].rearrange("p (h d) -> p h d", d=DH)
                dve.tensor_tensor(both, both, rn[:, p, :].unsqueeze(2).broadcast_to((P, 16, DH)), ALU.mult).then_inc(unit_done, 1)

            def copy_kT(t, r):
                p = r % 2
                at_least(dve, qkT_done, base, t, 1)
                at_least(dve, prev_copied, base, t, 0)
                dve.tensor_copy(kT[:, p, :, 0:P], psT[:, 1, :].rearrange("p (c n) -> p c n", c=4)).then_inc(kT_copied, 1)
                halves(dve, s_done, t, -2)
                dve.tensor_copy(kT[:, p, :, P:KEYS], kT[:, 1 - p, :, WIN:P]).then_inc(prev_copied, 1)

            def maxima(t, r, w):
                p = r % 2
                halves(dve, s_done, t, w + 1)
                ns = slice(4 * w, 4 * w + 4)
                dve.tensor_reduce(nmx[:, p, ns], psS[:, w, :].rearrange("p (c k) -> p c k", c=4), AX.X, ALU.max).then_inc(max_done, 1)
                halves(dve, max_done, t, w + 1)
                halves(dve, exp_done, t, w - 3)
                dve.tensor_scalar(bias[:, p, ns], nmx[:, p, ns], -QK_SCALE, None, ALU.mult).then_inc(bias_done, 1)

            def copy_pT(t, r):
                at_least(dve, pT_done[1], base, t, 1)
                halves(dve, av_done, t, 0)
                dve.tensor_copy(pT[:, 1, :, :], psT[:, 1, :].rearrange("p (b n) -> p b n", b=4)).then_inc(pT_copied[1], 1)

            def divide(t, r):
                p = r % 2
                halves(dve, exp_done, t, 2)
                dve.reciprocal(rden[:, p, :], den[:, p, :]).then_inc(rden_done, 1)
                at_least(dve, rden_done, base, t, 1)
                pr = prob[:, p, :, :, :].rearrange("p w c k -> p (w c) k")
                dve.tensor_tensor(pr, pr, rden[:, p, :].unsqueeze(2).broadcast_to((P, HEADS, P)), ALU.mult).then_inc(prob_done, 1)

            def residual(t, r):
                at_least(dve, y_done, base, t, 1)
                dve.tensor_tensor(sb["xf"][:, t, :], sb["xf"][:, t, :], psO[:, 0:P], ALU.add).then_inc(xf_done, 1)

            def slot(s, r, whole):
                def runs(t):
                    return whole or 0 <= t < NT
                r2, r3 = (r - 2) % 4, (r - 3) % 4
                if runs(s - 4):
                    residual(s - 4, r)
                if runs(s + 1):
                    carry(s + 1, (r + 1) % 4)
                if runs(s - 2):
                    copy_kT(s - 2, r2)
                if runs(s):
                    cosines(s, r)
                if runs(s - 2):
                    maxima(s - 2, r2, 0)
                if runs(s - 3):
                    copy_pT(s - 3, r3)
                if runs(s - 1):
                    normalise(s - 1, (r - 1) % 4)
                if runs(s - 2):
                    maxima(s - 2, r2, 1)
                if runs(s):
                    sums(s, r)
                if runs(s - 2):
                    divide(s - 2, r2)

            carry(0, 0)
            slots(dve, slot)


def mlp(nc, io, sb, layer):
    base = layer * NCH
    with ExitStack() as ctx:
        def tile(name, shape, dt=F32):
            return ctx.enter_context(nc.sbuf_tensor(name, shape, dt))

        def sem(name):
            return ctx.enter_context(nc.semaphore("f_" + name))

        w1, w2 = tile("f_w1", [P, 2 * HID]), tile("f_w2", [HC, 3, D])
        b1 = tile("f_b1", [HC, 2, 3])
        b2 = tile("f_b2", [P, D])
        lg, lb = tile("f_lg", [P, 1]), tile("f_lb", [P, 1])
        shift, carry = tile("f_shift", [P, P]), tile("f_carry", [P, P])
        stats, mv = tile("f_stats", [P, 2, 4, 2, 6]), tile("f_mv", [P, 2, 4, 2])
        ve, rstd = tile("f_ve", [P, 2, 4]), tile("f_rstd", [P, 2, 4])
        hn, hT = tile("f_hn", [P, 2, 4, D]), tile("f_hT", [P, 2, 512])
        gate, act_t = tile("f_gate", [HC, 3, 512]), tile("f_act", [HC, 2, 3, 512])
        last = tile("f_last", [P, NCH + 1, WIN])
        psH = ctx.enter_context(nc.psum_tensor("f_psH", [P, 2, 512], F32))
        psT = ctx.enter_context(nc.psum_tensor("f_psT", [P, 512], F32))
        psU = ctx.enter_context(nc.psum_tensor("f_psU", [P, 3, 512], F32))
        psY = ctx.enter_context(nc.psum_tensor("f_psY", [P, 2, 512], F32))

        w_in, last_set = sem("w_in"), sem("last_set")
        shifted, stats_done, mean_done, var_done, rstd_done = (sem(x) for x in ("shifted", "stats_done", "mean_done", "var_done", "rstd_done"))
        hn_done, hnT_done, hT_done, u_done, gate_done, act_done = (sem(x) for x in ("hn_done", "hnT_done", "hT_done", "u_done", "gate_done", "act_done"))
        y_done, y_added, xf_done = sem("y_done"), sem("y_added"), sem("xf_done")
        block = ctx.enter_context(nc.Block())
        def units(eng, s, c, k, per=3):
            if isinstance(c, int) and per * c + k <= 0:
                return
            eng.wait_ge(s, base * per + c * per + k)

        @block.sync
        def _(sp):
            ly = bass.ds(layer, 1)
            sp.dma_start(w1[:, :], io["w1"][layer]).then_inc(w_in, 16)
            w2_l = io["w2"][layer]
            sp.dma_start(w2[:, 0:2, :], w2_l[0:2 * HC, :].rearrange("(c p) n -> p c n", p=HC)).then_inc(w_in, 16)
            sp.dma_start(w2[0:HCS[2], 2, :], w2_l[2 * HC:HID, :]).then_inc(w_in, 16)
            b1_l = io["b1"][layer].rearrange("(w n) -> w n", w=2)
            with nc.allow_non_contiguous_dma("a bias to a partition each"):
                for w in range(2):
                    for c in range(3):
                        sp.dma_start(b1[0:HCS[c], w, c:c + 1], b1_l[w, c * HC:c * HC + HCS[c]].unsqueeze(1)).then_inc(w_in, 16)
                sp.dma_start(lg[:, :], io["ln_g"][layer].unsqueeze(1)).then_inc(w_in, 16)
                sp.dma_start(lb[:, :], io["ln_b"][layer].unsqueeze(1)).then_inc(w_in, 16)
            sp.dma_start(b2[:, :], io["b2"][ly, :].broadcast_to((P, D))).then_inc(w_in, 16)
            sp.dma_start(shift[:, :], io["c_shift"]).then_inc(w_in, 16)
            sp.dma_start(carry[:, :], io["c_carry_m"]).then_inc(w_in, 16)

        LOADS = 16 * 14

        @block.tensor
        def _(pe):
            def shift_half(c, r):
                p = r % 2
                at_least(pe, hn_done, base, c, -1)
                out = psH[:, p, 0:4 * WIN].rearrange("p (t d) -> p t d", t=4)
                pe.matmul(out, shift[:, :], sb["xf"][:, bass.ts(c, 4), WIN:D], start=True, stop=False, skip_group_check=True)
                pe.matmul(out[:, 0, :], carry[:, :], last[:, c, :], start=False, stop=False, skip_group_check=True)
                pe.matmul(out[:, 1:4, :], carry[:, :], sb["xf"][:, bass.ds(c * 4, 3), WIN:D], start=False, stop=True, skip_group_check=True).then_inc(shifted, 1)

            def turn(c, r):
                at_least(pe, hn_done, base, c, 1)
                at_least(pe, hT_done, base, c, 0)
                for t in range(4):
                    i = pe.transpose(psT[:, t * P:(t + 1) * P], hn[:, r % 2, t, :], sb["ident"])
                i.then_inc(hnT_done, 1)

            def up(c, r):
                at_least(pe, hT_done, base, c, 1)
                n = 0
                for m in range(3):
                    for w in (1, 0):
                        units(pe, gate_done if (n - 3) % 2 == 0 else act_done, c, (n - 3) // 2 + 1)
                        M = HCS[m]
                        pe.matmul(psU[0:M, n % 3, :], w1[:, w * HID + m * HC:w * HID + m * HC + M], hT[:, r % 2, :],
                                  start=True, stop=True).then_inc(u_done, 1)
                        n += 1

            def down(c, r):
                p = r % 2
                units(pe, act_done, c, 3)
                at_least(pe, y_added, base, c, -1)
                for t in range(4):
                    for m in range(3):
                        M = HCS[m]
                        i = pe.matmul(psY[:, p, t * P:(t + 1) * P], act_t[0:M, p, m, t * P:(t + 1) * P], w2[0:M, m, :],
                                      start=(m == 0), stop=(m == 2))
                i.then_inc(y_done, 1)

            pe.wait_ge(w_in, (layer + 1) * LOADS)
            pe.wait_ge(last_set, (layer + 1) * 3)
            pipelined(pe, NCH, 2, [(0, shift_half), (3, down), (1, turn), (2, up)])

        @block.gpsimd
        def _(pool):
            def powers(c, r):
                p = r % 2
                at_least(pool, mean_done, base, c, 1)
                pool.tensor_tensor(ve[:, p, :], mv[:, p, :, 1], sb["eps"][:, 0:4], ALU.add).then_inc(var_done, 1)
                at_least(pool, var_done, base, c, 1)
                pool.tensor_tensor(rstd[:, p, :], ve[:, p, :], sb["mhalf"][:, 0:4], ALU.pow).then_inc(rstd_done, 1)

            pipelined(pool, NCH, 2, [(0, powers)])

        @block.scalar
        def _(act):
            act.wait_ge(w_in, (layer + 1) * LOADS)

            def affine(c, r):
                at_least(act, hnT_done, base, c, 1)
                units(act, u_done, c, -6, 6)
                act.activation(hT[:, r % 2, :], psT[:, :], ACT.Identity, scale=lg[:, 0:1], bias=lb[:, 0:1]).then_inc(hT_done, 1)

            def gelu(c, r):
                for m in range(3):
                    M = HCS[m]
                    units(act, u_done, c, 2 * m + 1, 6)
                    units(act, act_done, c, m - 2)
                    act.activation(gate[0:M, m, :], psU[0:M, (2 * m) % 3, :], ACT.Gelu, bias=b1[0:M, 1, m:m + 1]).then_inc(gate_done, 1)

            pipelined(act, NCH, 2, [(1, affine), (2, gelu)])

        @block.vector
        def _(dve):
            def statistics(c, r):
                p = r % 2
                at_least(dve, shifted, base, c, 1)
                for t in range(4):
                    dve.bn_stats(stats[:, p, t, 0, :], sb["xf"][:, c * 4 + t, 0:WIN])
                    i = dve.bn_stats(stats[:, p, t, 1, :], psH[:, p, t * WIN:(t + 1) * WIN])
                i.then_inc(stats_done, 1)
                at_least(dve, stats_done, base, c, 1)
                carry_wait(dve, sb)
                for t in range(4):
                    i = dve.bn_aggr(mv[:, p, t, :], stats[:, p, t, :, :].rearrange("p a b -> p (a b)"))
                i.then_inc(mean_done, 1)

            def norm(c, r):
                p = r % 2
                at_least(dve, rstd_done, base, c, 1)
                at_least(dve, hnT_done, base, c, -1)
                for t in range(4):
                    dve.tensor_scalar(hn[:, p, t, 0:WIN], sb["xf"][:, c * 4 + t, 0:WIN], mv[:, p, t, 0:1], rstd[:, p, t:t + 1], ALU.subtract, ALU.mult)
                    i = dve.tensor_scalar(hn[:, p, t, WIN:D], psH[:, p, t * WIN:(t + 1) * WIN], mv[:, p, t, 0:1], rstd[:, p, t:t + 1], ALU.subtract, ALU.mult)
                i.then_inc(hn_done, 1)

            def gated(c, r):
                p = r % 2
                for m in range(3):
                    M = HCS[m]
                    units(dve, u_done, c, 2 * m + 2, 6)
                    units(dve, gate_done, c, m + 1)
                    if m == 0:
                        at_least(dve, y_done, base, c, -1)
                    dve.scalar_tensor_tensor(out=act_t[0:M, p, m, :], in0=psU[0:M, (2 * m + 1) % 3, :], scalar=b1[0:M, 0, m:m + 1],
                                             in1=gate[0:M, m, :], op0=ALU.add, op1=ALU.mult).then_inc(act_done, 1)

            def residual(c, r):
                xs = sb["xf"][:, bass.ts(c, 4), :]
                at_least(dve, y_done, base, c, 1)
                dve.tensor_tensor(xs, xs, psY[:, r % 2, :].rearrange("p (t n) -> p t n", t=4), ALU.add).then_inc(y_added, 1)
                at_least(dve, y_added, base, c, 1)
                dve.tensor_tensor(xs, xs, b2[:, :].unsqueeze(1).broadcast_to((P, 4, D)), ALU.add).then_inc(xf_done, 1)

            dve.memset(last[:, :, :], 0.0).then_inc(last_set, 1)
            dve.wait_ge(last_set, layer * 3 + 1)
            src = sb["xf"].rearrange("p (b u t) n -> p b u t n", b=B, u=2)[:, :, 0, 3, WIN:D]
            dst = last[:, 0:NCH, :].rearrange("p (b u) n -> p b u n", u=2)[:, :, 1, :]
            dve.tensor_copy(dst, src).then_inc(last_set, 2)
            dve.wait_ge(w_in, (layer + 1) * LOADS)
            pipelined(dve, NCH, 2, [(3, residual), (0, statistics), (2, gated), (0, norm)])


def last_norm(nc, io, sb):
    with ExitStack() as ctx:
        def tile(name, shape, dt=F32):
            return ctx.enter_context(nc.sbuf_tensor(name, shape, dt))

        def sem(name):
            return ctx.enter_context(nc.semaphore("l_" + name))

        stats, mv = tile("l_stats", [P, 2, 4, 6]), tile("l_mv", [P, 2, 4, 2])
        ve, rstd = tile("l_ve", [P, 2, 4]), tile("l_rstd", [P, 2, 4])
        yn, y = tile("l_yn", [P, 2, 4, D]), tile("l_y", [P, 2, 4, D])
        stats_done, mean_done, var_done, rstd_done, yn_done, y_done = (sem(x) for x in ("stats_done", "mean_done", "var_done", "rstd_done", "yn_done", "y_done"))
        y_out = [sem("y_out0"), sem("y_out1")]
        block = ctx.enter_context(nc.Block())
        out_v = io["out"].rearrange("b (t p) c -> p (b t) c", p=P)

        @block.sync
        def _(sp):
            with sp.Fori(0, NCH // 2) as pair:
                for p in range(2):
                    c = pair * 2 + p
                    sp.wait_ge(y_done, c + 1)
                    sp.dma_start(out_v[:, bass.ts(c, 4), :], y[:, p, :, :]).then_inc(y_out[p], 16)
            for p in range(2):
                sp.wait_ge(y_out[p], 16 * (NCH // 2))

        @block.gpsimd
        def _(pool):
            def powers(c, r):
                p = r % 2
                at_least(pool, mean_done, 0, c, 1)
                pool.tensor_tensor(ve[:, p, :], mv[:, p, :, 1], sb["eps"][:, 0:4], ALU.add).then_inc(var_done, 1)
                at_least(pool, var_done, 0, c, 1)
                pool.tensor_tensor(rstd[:, p, :], ve[:, p, :], sb["mhalf"][:, 0:4], ALU.pow).then_inc(rstd_done, 1)

            pipelined(pool, NCH, 2, [(0, powers)])

        @block.vector
        def _(dve):
            def moments(c, r):
                p = r % 2
                for t in range(4):
                    i = dve.bn_stats(stats[:, p, t, :], sb["xf"][:, c * 4 + t, :])
                i.then_inc(stats_done, 1)
                at_least(dve, stats_done, 0, c, 1)
                carry_wait(dve, sb)
                for t in range(4):
                    i = dve.bn_aggr(mv[:, p, t, :], stats[:, p, t, :])
                i.then_inc(mean_done, 1)

            def finish(c, r):
                p = r % 2
                at_least(dve, rstd_done, 0, c, 1)
                for t in range(4):
                    i = dve.tensor_scalar(yn[:, p, t, :], sb["xf"][:, c * 4 + t, :], mv[:, p, t, 0:1], rstd[:, p, t:t + 1], ALU.subtract, ALU.mult)
                i.then_inc(yn_done, 1)
                at_least(dve, yn_done, 0, c, 1)
                if not isinstance(c, int) or c >= 2:
                    dve.wait_ge(y_out[p], (c - p) * 8)
                dve.tensor_tensor(y[:, p, :, :], yn[:, p, :, :], sb["x"][:, bass.ts(c, 4), :], ALU.add).then_inc(y_done, 1)

            pipelined(dve, NCH, 2, [(0, moments), (1, finish)])


def latent_attention_and_window_layers(nc, io):
    io["q_parts"] = nc.dram_tensor("q_parts", (B, NH, 3, DK, S), BF16).ap()
    io["k_parts"] = nc.dram_tensor("k_parts", (B, NH, 3, DK, S), BF16).ap()
    with ExitStack() as ctx:
        def tile(name, shape, dt=F32):
            return ctx.enter_context(nc.sbuf_tensor(name, shape, dt))

        sb = {
            "x": tile("x_sb", [P, NT, D])[:, :, :],
            "ident": tile("ident", [P, P])[:, :],
            "ident_b": tile("ident_b", [P, P], BF16)[:, :],
            "mhalf": tile("mhalf", [P, 16])[:, :],
            "eps": tile("eps", [P, 16])[:, :],
            "spare": tile("spare", [P, 1])[:, :],
            "carry": tile("carry", [P, TB])[:, :],
            "xf": tile("xf_sb", [P, NT, D])[:, :, :],
        }
        with ExitStack() as first:
            def early(name, shape, dt=F32):
                return first.enter_context(nc.sbuf_tensor(name, shape, dt))[:]

            sb["mask_q"] = early("mask_q", [P, P], BF16)
            sb["mask_k"] = early("mask_k", [P, P], BF16)
            sb["w_down"] = early("w_down", [P, 2 * DC])
            sb["w_uq"] = early("w_uq", [DC, D])
            sb["w_ukv"] = early("w_ukv", [2 * DC, 2 * D])
            sb["w_o"] = early("w_o", [P, D])
            sb["v_all"] = early("v_all", [P, NG, NT, HG * VA])
            project(nc, io, sb)
            sb["o_tok"] = early("o_tok", [P, NT, D])
            attend(nc, io, sb)
            mix(nc, io, sb)
        sb["mask_w"] = tile("mask_w", [P, TB, P], BF16)[:, :, :]
        with nc.Fori(0, DEPTH) as layer:
            window(nc, io, sb, layer)
            mlp(nc, io, sb, layer)
        last_norm(nc, io, sb)


def constants():
    bf, f = mybir.dt.np(BF16), np.float32
    c = {"c_ident": np.eye(P, dtype=f), "c_ident_b": np.eye(P).astype(bf)}
    i, j = np.arange(P)[:, None], np.arange(P)[None, :]
    c["c_mask_q"] = np.where(j > i, NEG, 0.0).astype(bf)
    c["c_mask_k"] = np.where(i > j, NEG, 0.0).astype(bf)
    c["c_zero"] = np.zeros((KROWS - ROWS, HG, S), bf)
    sel = np.zeros((KROWS - ROWS, NG, HG, S), bf)
    for h in range(HG):
        sel[3 * h:3 * h + 3, :, h, :] = 1
    c["c_sel"] = sel
    key = np.where((j >= WIN) & (i < WIN), j - 2 * WIN, j)
    ok = (key <= i) & (i <= key + WIN)
    mask = np.broadcast_to(ok[:, None, :], (P, TB, P)).copy()
    mask[:WIN, 0, WIN:] = False
    c["c_mask_w"] = np.where(mask, 0.0, NEG).astype(bf)
    c["c_carry"] = np.broadcast_to((np.arange(TB) > 0).astype(f), (P, TB)).copy()
    c["c_shift"] = np.eye(P, k=1, dtype=f)
    c["c_carry_m"] = np.zeros((P, P), f)
    c["c_carry_m"][P - 1, 0] = 1
    half = np.arange(0, DH, 2, dtype=f)
    inv = (f(1.0) / np.power(f(10000.0), half / f(DH))).astype(f)
    t = np.arange(S, dtype=f)
    freqs = (t[:, None] * inv[None, :]).astype(f)
    base = ((half + f(0.4 * DH)) / f(1.4 * DH)).astype(f)
    power = ((t - f(S // 2)) / f(WIN // 2)).astype(f)
    scale = np.power(base[None, :], power[:, None]).astype(f)
    cos, sin = np.cos(freqs).astype(f), np.sin(freqs).astype(f)
    two = lambda a, b: np.concatenate([a, b], axis=-1)
    cosines = np.stack([two(cos * scale, cos * scale), two(cos / scale, cos / scale)], 1)
    sines = np.stack([two(-sin * scale, sin * scale), two(-sin / scale, sin / scale)], 1)
    for name, x in (("c_cos", cosines), ("c_sin", sines)):
        c[name] = np.ascontiguousarray(x.reshape(TB, P, 2, DH).transpose(1, 0, 2, 3).astype(f))
    return c


_INS = {"x": "L0_attn_x", "W_dq": "L0_attn_W_dq", "W_uq": "L0_attn_W_uq", "W_dkv": "L0_attn_W_dkv",
        "W_uk": "L0_attn_W_uk", "W_uv": "L0_attn_W_uv", "W_o": "L0_attn_W_o", "wqkv": "L0_ffn_wqkv",
        "q_scale": "L0_ffn_q_scale", "k_scale": "L0_ffn_k_scale", "wo": "L0_ffn_wo", "ln_g": "L0_ffn_ln_g",
        "ln_b": "L0_ffn_ln_b", "w1": "L0_ffn_w1", "b1": "L0_ffn_b1", "w2": "L0_ffn_w2", "b2": "L0_ffn_b2"}


def kernel(**inputs):
    import concourse.bacc as bacc
    from concourse.bass_utils import run_bass_kernel_spmd as run

    nc = bacc.Bacc("TRN2", target_bir_lowering=False, num_devices=1)
    nc.disable_value_cache = True
    arrays, io = {}, {}
    given = {short: np.ascontiguousarray(inputs[name]) for short, name in _INS.items()}
    for short, a in {**given, **constants()}.items():
        arrays["in_" + short] = a
        io[short] = nc.dram_tensor("in_" + short, a.shape, mybir.dt.from_np(a.dtype), kind="ExternalInput").ap()
    io["out"] = nc.dram_tensor("out_x", (B, S, D), F32, kind="ExternalOutput").ap()
    latent_attention_and_window_layers(nc, io)
    return run(nc, [arrays], core_ids=[0]).results[0]["out_x"]
```

```python
from contextlib import ExitStack

import numpy as np
import concourse.bass as bass
from concourse import mybir

F32 = mybir.dt.float32
BF16 = mybir.dt.bfloat16
ALU = mybir.AluOpType
ACT = mybir.ActivationFunctionType
AX = mybir.AxisListType

B, S, D = 4, 1024, 128
P = 128
NT = B * S // P
TB = S // P
NCH = NT // 4
NH, DK, DC = 16, 8, 32
HG = 4
NG = NH // HG
NPAIR = 9
ROWS = NPAIR * DK
KROWS = 96
NM = 3 * HG
VA = DK + 1
VPAD = 32 - VA
SCALE0 = float(1.0 / np.sqrt(np.float32(DK)))
NEG = -1e30
EPS = 1e-5
DEPTH, HEADS, DH, WIN = 2, 8, 64, 64
INNER = HEADS * DH
QK_SCALE = 8.0
KEYS = 3 * WIN
HID = int(D * 4 * 2 / 3)
HC = 114
HCS = [HC, HC, HID - 2 * HC]


def ge(eng, sem, count):
    if isinstance(count, int) and count <= 0:
        return
    eng.wait_ge(sem, count)


def carry_wait(dve, sb):
    dve.memset(sb["spare"], 0.0)


GROUP_LOADS = 4


def load_group(sp, io, sb, b, g):
    into = sb["stack_in"][g]
    q_src = io["q_parts"][b, g].rearrange("a d j n -> (a d) (j n)").unsqueeze(1).broadcast_to((3 * DK, 3, HG * S))
    k_src = io["k_parts"][b, g].rearrange("d r j n -> (d r) (j n)").unsqueeze(0).broadcast_to((3, 3 * DK, HG * S))
    sp.dma_start(sb["qs"][0:ROWS, g, :, :], q_src).then_inc(into, 16)
    sp.dma_start(sb["ks"][0:ROWS, g, :, :], k_src).then_inc(into, 16)
    sp.dma_start(sb["qs"][ROWS:KROWS, g, :, :], io["c_zero"]).then_inc(into, 16)
    sp.dma_start(sb["vs"][g][:, 0:TB * HG * VA], sb["v_all"][:, g, bass.ts(b, TB), :].rearrange("p t a -> p (t a)")).then_inc(into, 16)


def project(nc, io, sb):
    with ExitStack() as ctx:
        def tile(name, shape, dt=F32):
            return ctx.enter_context(nc.sbuf_tensor(name, shape, dt))

        def sem(name):
            return ctx.enter_context(nc.semaphore(name))

        stats = tile("p_stats", [P, 2, 4, 6])
        mv = tile("p_mv", [P, 2, 4, 2])
        rstd = tile("p_rstd", [P, 2, 4])
        ve = tile("p_ve", [P, 2, 4])
        xn = tile("p_xn", [P, 2, 4, D])
        xnT = tile("p_xnT", [P, 2, 512])
        shift = tile("p_shift", [P, 2, 4])
        w_downT = tile("p_w_downT", [2 * DC, P])
        w_heads = tile("p_w_heads", [P, 3, D])
        rem = tile("p_rem", [P, 2, 2, 512])
        parts = sb["parts"]
        psT = ctx.enter_context(nc.psum_tensor("p_psT", [P, 2, 512], F32))
        psC = ctx.enter_context(nc.psum_tensor("p_psC", [P, 512], F32))
        psQK = ctx.enter_context(nc.psum_tensor("p_psQK", [P, 2, 512], F32))
        psV = ctx.enter_context(nc.psum_tensor("p_psV", [P, 512], F32))

        x_in = [sem("x_first"), sem("x_second"), sem("x_rest")]
        w_in, shift_done = sem("w_in"), sem("shift_done")
        stats_done, mean_done, var_done, rstd_done = sem("stats_done"), sem("mean_done"), sem("var_done"), sem("rstd_done")
        xn_done, xnT_done, xnT_copied = sem("xn_done"), sem("xnT_done"), sem("xnT_copied")
        down_turned, down_copied, w_done = sem("down_turned"), sem("down_copied"), sem("w_done")
        qk_done, v_done, v_copied = sem("qk_done"), sem("v_done"), sem("v_copied")
        hi_done, rem1_done, mid_done, parts_done = sem("hi_done"), sem("rem1_done"), sem("mid_done"), sem("parts_done")
        parts_out = sb["parts_out"]
        ones_set, w_copied = sem("ones_set"), sem("w_copied")

        block = ctx.enter_context(nc.Block())
        x_v = io["x"].rearrange("b (t p) c -> p (b t) c", p=P)

        @block.sync
        def _(sp):
            sp.dma_start(sb["x"][:, 0:4, :], x_v[:, 0:4, :]).then_inc(x_in[0], 16)
            sp.dma_start(sb["x"][:, 4:8, :], x_v[:, 4:8, :]).then_inc(x_in[1], 16)
            sp.wait_ge(w_in, 16 * 6)
            sp.dma_start(sb["x"][:, 8:NT, :], x_v[:, 8:NT, :]).then_inc(x_in[2], 16)
            sp.dma_start(sb["ks"][ROWS:KROWS, :, :, :], io["c_sel"]).then_inc(sb["const_in"], 16)
            for dst, src in ((sb["ident_b"], io["c_ident_b"]), (sb["mask_q"], io["c_mask_q"]), (sb["mask_k"], io["c_mask_k"])):
                sp.dma_start(dst, src).then_inc(sb["const_in"], 16)

            def send(pair, par):
                c = pair * 2 + par
                sp.wait_ge(parts_done, 2 * c + 2)
                cols = slice(512 * par, 512 * par + 512)
                for a in range(3):
                    sp.dma_start(io["q_parts"][pair, :, a, :, :, cols].rearrange("g d j n -> g (d j) n"),
                                 parts[:, par, 0, a, :]).then_inc(parts_out[par], 16)
                    sp.dma_start(io["k_parts"][pair, :, :, a, :, cols].rearrange("g d j n -> (g d) j n"),
                                 parts[:, par, 1, a, :]).then_inc(parts_out[par], 16)

            send(0, 0)
            send(0, 1)
            for par in range(2):
                sp.wait_ge(parts_out[par], 16 * 6)
            sp.wait_ge(v_copied, 2)
            load_group(sp, io, sb, 0, 0)
            with sp.Fori(1, NCH // 2) as pair:
                for par in range(2):
                    send(pair, par)

        @block.scalar
        def _(act):
            loads = [(sb["ident"], io["c_ident"]), (sb["w_down"][:, 0:DC], io["W_dq"]), (sb["w_down"][:, DC:2 * DC], io["W_dkv"]),
                     (sb["w_uq"][0:DC, :], io["W_uq"]), (sb["w_ukv"][DC:2 * DC, 0:D], io["W_uk"]),
                     (sb["w_ukv"][DC:2 * DC, D:2 * D], io["W_uv"])]
            for dst, src in loads:
                act.dma_start(dst, src).then_inc(w_in, 16)

            def copy_xnT(c, par):
                at_least(act, xnT_done, 0, c, 1)
                at_least(act, v_done, 0, c, -1)
                act.activation(xnT[:, par, :], psT[:, par, :], ACT.Copy).then_inc(xnT_copied, 1)

            def normal(c, par):
                at_least(act, shift_done, 0, c, 1)
                at_least(act, xnT_done, 0, c, -1)
                for t in range(4):
                    i = act.activation(xn[:, par, t, :], sb["x"][:, c * 4 + t, :], ACT.Identity,
                                       scale=rstd[:, par, t:t + 1], bias=shift[:, par, t:t + 1])
                i.then_inc(xn_done, 1)

            def copy_v(c, par):
                act.wait_ge(v_done, c + 1)
                if isinstance(c, int) and c == 0:
                    act.wait_ge(ones_set, 3)
                for g in range(NG):
                    src = psV[:, :].rearrange("p (t g j d) -> p g t j d", t=4, g=NG, j=HG)[:, g]
                    dst = sb["v_all"][:, g, bass.ts(c, 4), :].rearrange("p t (j a) -> p t j a", a=VA)[:, :, :, 0:DK]
                    i = act.activation(dst, src, ACT.Copy)
                i.then_inc(v_copied, 1)

            act.wait_ge(down_turned, 1)
            act.activation(w_downT[:, :], psC[0:2 * DC, 0:P], ACT.Copy).then_inc(down_copied, 1)
            pipelined(act, NCH, 2, [(2, copy_xnT), (1, normal), (3, copy_v)])

        @block.gpsimd
        def _(pool):
            pool.memset(sb["mhalf"], -0.5).then_inc(ones_set, 1)
            pool.memset(sb["eps"], EPS).then_inc(ones_set, 1)

            def powers(c, par):
                pool.wait_ge(mean_done, c + 1)
                at_least(pool, xn_done, 0, c, -1)
                pool.tensor_tensor(ve[:, par, :], mv[:, par, :, 1], sb["eps"][:, 0:4], ALU.add).then_inc(var_done, 1)
                pool.wait_ge(var_done, c + 1)
                pool.tensor_tensor(rstd[:, par, :], ve[:, par, :], sb["mhalf"][:, 0:4], ALU.pow).then_inc(rstd_done, 1)

            pool.wait_ge(ones_set, 3)
            pipelined(pool, NCH, 2, [(0, powers)])

        @block.vector
        def _(dve):
            dve.memset(sb["v_all"][:, :, :, :], 1.0).then_inc(ones_set, 1)

            def mean(c, par):
                if isinstance(c, int) and c < 3:
                    dve.wait_ge(x_in[c], 16)
                for t in range(4):
                    i = dve.bn_stats(stats[:, par, t, :], sb["x"][:, c * 4 + t, :])
                i.then_inc(stats_done, 1)
                dve.wait_ge(stats_done, c + 1)
                at_least(dve, shift_done, 0, c, -1)
                at_least(dve, rstd_done, 0, c, -1)
                carry_wait(dve, sb)
                for t in range(4):
                    i = dve.bn_aggr(mv[:, par, t, :], stats[:, par, t, :])
                i.then_inc(mean_done, 1)

            def shifts(c, par):
                dve.wait_ge(rstd_done, c + 1)
                at_least(dve, xn_done, 0, c, -1)
                dve.scalar_tensor_tensor(out=shift[:, par, :], in0=mv[:, par, :, 0], scalar=-1.0, in1=rstd[:, par, :],
                                         op0=ALU.mult, op1=ALU.mult).then_inc(shift_done, 1)

            def cut(c, par, w):
                if w == 0 and (not isinstance(c, int) or c >= 2):
                    dve.wait_ge(parts_out[par], (c - par) * (8 * 6))
                dve.wait_ge(qk_done, 2 * c + w + 1)
                dve.tensor_copy(parts[:, par, w, 0, :], psQK[:, w, :]).then_inc(hi_done, 1)
                dve.wait_ge(hi_done, 2 * c + w + 1)
                dve.tensor_tensor(rem[:, par, w, :], psQK[:, w, :], parts[:, par, w, 0, :], ALU.subtract).then_inc(rem1_done, 1)
                dve.wait_ge(rem1_done, 2 * c + w + 1)
                dve.tensor_copy(parts[:, par, w, 1, :], rem[:, par, w, :]).then_inc(mid_done, 1)
                dve.wait_ge(mid_done, 2 * c + w + 1)
                dve.tensor_tensor(parts[:, par, w, 2, :], rem[:, par, w, :], parts[:, par, w, 1, :], ALU.subtract).then_inc(parts_done, 1)

            def copy_weights():
                dve.wait_ge(w_done, 1)
                for w in range(2):
                    dve.tensor_copy(w_heads[:, w, :].rearrange("p (g d j) -> p g d j", g=NG, j=HG),
                                    psQK[:, w, 0:D].rearrange("p (g j d) -> p g d j", g=NG, j=HG)).then_inc(w_copied, 1)
                dve.tensor_copy(w_heads[:, 2, :], psQK[:, 1, D:2 * D]).then_inc(w_copied, 1)

            def cut_q(c, par):
                if isinstance(c, int) and c == 0:
                    copy_weights()
                cut(c, par, 0)

            def cut_k(c, par):
                cut(c, par, 1)

            pipelined(dve, NCH, 2, [(3, cut_q), (1, shifts), (0, mean), (3, cut_k)])

        @block.tensor
        def _(pe):
            pe.wait_ge(w_in, 16 * 6)
            pe.transpose(psC[0:2 * DC, 0:P], sb["w_down"], sb["ident"]).then_inc(down_turned, 1)
            pe.wait_ge(down_copied, 1)
            pe.matmul(psQK[:, 0, 0:D], w_downT[0:DC, :], sb["w_uq"][0:DC, :], start=True, stop=True)
            pe.matmul(psQK[:, 1, 0:2 * D], w_downT[DC:2 * DC, :], sb["w_ukv"][DC:2 * DC, :], start=True, stop=True).then_inc(w_done, 1)

            def transposes(c, par):
                at_least(pe, xn_done, 0, c, 1)
                at_least(pe, xnT_copied, 0, c, -1)
                for t in range(4):
                    i = pe.transpose(psT[:, par, t * P:(t + 1) * P], xn[:, par, t, :], sb["ident"])
                i.then_inc(xnT_done, 1)

            def heads(c, par):
                if isinstance(c, int) and c == 0:
                    pe.wait_ge(w_copied, 3)
                at_least(pe, xnT_copied, 0, c, 1)
                for w in range(2):
                    if not isinstance(c, int) or c > 0:
                        pe.wait_ge(rem1_done, 2 * c + w - 1)
                    pe.matmul(psQK[:, w, :], w_heads[:, w, :], xnT[:, par, :], start=True, stop=True).then_inc(qk_done, 1)
                if not isinstance(c, int) or c > 0:
                    pe.wait_ge(v_copied, c)
                for t in range(4):
                    i = pe.matmul(psV[:, t * P:(t + 1) * P], xnT[:, par, t * P:(t + 1) * P], w_heads[:, 2, :], start=True, stop=True)
                i.then_inc(v_done, 1)

            pipelined(pe, NCH, 2, [(2, transposes), (3, heads)])


MAX_UNITS = [(i, j, kc) for i in range(TB) for j in range(HG) for kc in range(i // 4 + 1)]
EXP_GROUPS = [(qc, kt) for qc in range(2) for kt in range(4 * qc + 4)]
NMU, NEG_ = len(MAX_UNITS), len(EXP_GROUPS)
NEU = NEG_ * HG
NM_A = sum(1 for i, _, _ in MAX_UNITS if i < 4)
assert NMU == NEU


def attend(nc, io, sb):
    with ExitStack() as ctx:
        def tile(name, shape, dt=F32):
            return ctx.enter_context(nc.sbuf_tensor(name, shape, dt))

        def sem(name):
            return ctx.enter_context(nc.semaphore(name))

        qs, ks, vs = sb["qs"], sb["ks"], sb["vs"]
        prob = [tile(f"a_prob{r}", [P, HG, 512]) for r in range(3)]
        oT = tile("a_oT", [P, 2, 512])
        mx = tile("a_mx", [P, TB, HG, 2])
        nm = tile("a_nm", [P, 2, 4 * HG])
        nmr = tile("a_nmr", [P, 2, 4 * HG])
        nmp = tile("a_nmp", [P, TB, HG, 3], BF16)
        nmT = tile("a_nmT", [NM, S], BF16)
        rec = tile("a_rec", [P, 2, 4, HG])
        spare = tile("a_spare", [P, 6])
        psM = ctx.enter_context(nc.psum_tensor("a_psM", [P, 3, 512], F32))
        psE = ctx.enter_context(nc.psum_tensor("a_psE", [P, 3, 512], F32))
        psO = ctx.enter_context(nc.psum_tensor("a_psO", [P, 2, 512], F32))
        psOb = psO[:, :, :].bitcast(BF16)

        nm_in = [sem("nm_in_a"), sem("nm_in_b")]
        max_ready, max_read = sem("max_ready"), sem("max_read")
        score_ready, exp_done, av_done = sem("score_ready"), sem("exp_done"), sem("av_done")
        nm_step, nm_parts, nm_T, nm_copied = sem("nm_step"), sem("nm_parts"), sem("nm_T"), sem("nm_copied")
        o_copied, o_T, rec_done, o_read = sem("o_copied"), sem("o_T"), sem("rec_done"), sem("o_read")
        pad_set = sem("pad_set")
        C_MAX, C_EXP, C_AV, C_O, C_T, C_R = 3, 3, 3, 2, 2, 2

        block = ctx.enter_context(nc.Block())
        NSTAGE = B * NG

        @block.sync
        def _(sp):
            def send_maxima(s, g, half):
                sp.wait_ge(nm_copied, 2 * s + half + 1)
                cols = slice(512 * half, 512 * half + 512)
                sp.dma_start(qs[ROWS:ROWS + NM, g, :, cols], nmT[:, cols].unsqueeze(1).broadcast_to((NM, HG, 512))).then_inc(nm_in[half], 16)

            for g in range(1, NG):
                load_group(sp, io, sb, 0, g)
            for par in range(2):
                sp.wait_ge(sb["parts_out"][par], 16 * 6 * (NCH // 2))
            send_maxima(0, 0, 0)
            with sp.Fori(0, B - 1) as b:
                for g in range(NG):
                    e = b * NG + g
                    send_maxima(e, g, 1)
                    send_maxima(e + 1, (g + 1) % NG, 0)
                    sp.wait_ge(av_done, e * NEG_ + NEG_ + C_AV)
                    load_group(sp, io, sb, b + 1, g)
            for g in range(NG):
                e = (B - 1) * NG + g
                send_maxima(e, g, 1)
                if g < NG - 1:
                    send_maxima(e + 1, g + 1, 0)
            for half in range(2):
                sp.wait_ge(nm_in[half], 16 * NSTAGE)

        @block.gpsimd
        def _(pool):
            for g in range(NG):
                pool.memset(vs[g][:, TB * HG * VA:], 0.0).then_inc(pad_set, 1)

        @block.tensor
        def _(pe):
            pe.wait_ge(sb["const_in"], 64)
            pe.wait_ge(pad_set, NG)

            def max_unit(s, g, u):
                i, j, kc = MAX_UNITS[u]
                n = min(512, (i + 1) * P - 512 * kc)
                out = psM[:, u % 3, 0:n]
                diag = kc == i // 4
                pe.wait_ge(max_read, s * NMU + (u + 1))
                mm = pe.matmul(out, qs[:, g, j, i * P:(i + 1) * P], ks[:, g, j, 512 * kc:512 * kc + n],
                               start=True, stop=not diag)
                if diag:
                    mm = pe.matmul(out[:, n - P:n], sb["ident_b"], sb["mask_q"], start=False, stop=True)
                mm.then_inc(max_ready, 1)

            def score(e, g, n, j):
                qc, kt = EXP_GROUPS[n]
                q0 = max(512 * qc, kt * P)
                w = 512 * (qc + 1) - q0
                diag = kt * P >= 512 * qc
                u = n * HG + j
                pe.wait_ge(exp_done, e * NEU + (u + 1))
                out = psE[:, u % 3, 0:w]
                mm = pe.matmul(out, ks[:, g, j, kt * P:(kt + 1) * P], qs[:, g, j, q0:q0 + w], start=True, stop=not diag)
                if diag:
                    mm = pe.matmul(out[:, 0:P], sb["ident_b"], sb["mask_k"], start=False, stop=True)
                mm.then_inc(score_ready, 1)

            def values(e, g, n):
                qc, kt = EXP_GROUPS[n]
                q0 = max(0, kt * P - 512 * qc)
                pe.wait_ge(exp_done, e * NEU + (n + 1) * HG + C_EXP)
                if kt == 0:
                    pe.wait_ge(o_read, e * 2 + qc + 1)
                    if isinstance(e, int) and e == 0:
                        pe.wait_ge(nm_copied, qc + 1)
                for j in range(HG):
                    mm = pe.matmul(psO[32 * j:32 * j + 32, qc, q0:512],
                                   vs[g][:, kt * HG * VA + j * VA:kt * HG * VA + j * VA + 32],
                                   prob[n % 3][:, j, 0:512 - q0], start=(kt == 0), stop=(kt == 4 * qc + 3),
                                   skip_group_check=True)
                mm.then_inc(av_done, 1)

            def turn_maxima(s, half):
                pe.wait_ge(nm_parts, 2 * s + half + 1)
                pe.wait_ge(o_copied, 2 * s - 1 + half + C_O)
                for t in range(4):
                    i = 4 * half + t
                    mm = pe.transpose(psOb[0:NM, half, t * P:(t + 1) * P], nmp[:, i, :, :].rearrange("p j a -> p (j a)"), sb["ident_b"])
                mm.then_inc(nm_T, 1)

            def turn_outputs(e, qc, maxima):
                pe.wait_ge(o_copied, 2 * e + qc + 1 + C_O)
                if maxima:
                    pe.wait_ge(nm_copied, 2 * e + 2 + qc + 1)
                for t in range(4):
                    mm = pe.transpose(psO[:, qc, t * P:(t + 1) * P], oT[:, qc, t * P:(t + 1) * P], sb["ident"])
                mm.then_inc(o_T, 1)

            def slot(e, g, first, more):
                g1 = (g + 1) % NG
                if more:
                    pe.wait_ge(sb["stack_in"][g1], (e + 1 - g1) * (16 * GROUP_LOADS // NG) + 16 * GROUP_LOADS)
                for n in range(NEG_):
                    if n == 0:
                        pe.wait_ge(nm_in[0], 16 * e + 16)
                    if n == 4:
                        pe.wait_ge(nm_in[1], 16 * e + 16)
                    for j in range(HG):
                        score(e, g, n, j)
                        if more:
                            max_unit(e + 1, g1, n * HG + j)
                    if n:
                        values(e, g, n - 1)
                    elif not first:
                        values(e - 1, (g - 1) % NG, NEG_ - 1)
                    if n == 1:
                        turn_maxima(e, 1)
                    if n == 3 and not first:
                        turn_outputs(e - 1, 1, True)
                    if n == 5 and more:
                        turn_maxima(e + 1, 0)
                    if n == 7:
                        turn_outputs(e, 0, more)

            pe.wait_ge(sb["stack_in"][0], 16 * GROUP_LOADS)
            for u in range(NMU):
                max_unit(0, 0, u)
                if u == NM_A + 6:
                    turn_maxima(0, 0)
            slot(0, 0, True, True)
            with pe.Fori(0, B - 1) as b:
                for k in range(1, NG + 1):
                    slot(b * NG + k, k % NG, False, True)
            for g in range(1, NG):
                slot((B - 1) * NG + g, g, False, g < NG - 1)
            values(NSTAGE - 1, NG - 1, NEG_ - 1)
            turn_outputs(NSTAGE - 1, 1, False)

        @block.scalar
        def _(act):
            def exps(e, n):
                qc, kt = EXP_GROUPS[n]
                w = 512 * (qc + 1) - max(512 * qc, kt * P)
                act.wait_ge(av_done, e * NEG_ + (n + 1))
                for j in range(HG):
                    u = n * HG + j
                    act.wait_ge(score_ready, e * NEU + (u + 1))
                    act.activation(prob[n % 3][:, j, 0:w], psE[:, u % 3, 0:w], ACT.Exp, scale=SCALE0).then_inc(exp_done, 1)

            def copy_maxima(s, half):
                act.wait_ge(nm_T, 2 * s + half + 1)
                if not isinstance(s, int) or s > 0:
                    act.wait_ge(nm_in[half], 16 * s)
                cols = slice(512 * half, 512 * half + 512)
                act.activation(nmT[:, cols], psOb[0:NM, half, 0:512], ACT.Copy).then_inc(nm_copied, 1)

            def copy_outputs(e, qc):
                act.wait_ge(av_done, e * NEG_ + (4 if qc == 0 else NEG_) + C_AV)
                act.wait_ge(o_T, 2 * e + qc - 1 + C_T)
                act.activation(oT[:, qc, :], psO[:, qc, :], ACT.Copy).then_inc(o_copied, 1)

            def slot(e, first, more):
                for n in range(NEG_):
                    exps(e, n)
                    if n == 0 and not first:
                        copy_outputs(e - 1, 1)
                    if n == 1:
                        copy_maxima(e, 1)
                    if n == 4:
                        copy_outputs(e, 0)
                    if n == 6 and more:
                        copy_maxima(e + 1, 0)

            copy_maxima(0, 0)
            slot(0, True, True)
            with act.Fori(0, B - 1) as b:
                for k in range(1, NG + 1):
                    slot(b * NG + k, False, True)
            for g in range(1, NG):
                slot((B - 1) * NG + g, False, g < NG - 1)
            copy_outputs(NSTAGE - 1, 1)

        @block.vector
        def _(dve):
            dve.memset(spare[:, 0:1], 0.0).then_inc(max_read, C_MAX)
            dve.memset(spare[:, 1:2], 0.0).then_inc(exp_done, C_EXP)
            dve.memset(spare[:, 2:3], 0.0).then_inc(av_done, C_AV)
            dve.memset(spare[:, 3:4], 0.0).then_inc(o_copied, C_O)
            dve.memset(spare[:, 4:5], 0.0).then_inc(o_T, C_T)
            dve.memset(spare[:, 5:6], 0.0).then_inc(o_read, C_R)

            def maximum(s, u):
                i, j, kc = MAX_UNITS[u]
                n = min(512, (i + 1) * P - 512 * kc)
                dve.wait_ge(max_ready, s * NMU + (u + 1))
                dve.tensor_reduce(mx[:, i, j, kc:kc + 1], psM[:, u % 3, 0:n], AX.X, ALU.max).then_inc(max_read, 1)

            def cut_maxima(s, half, k):
                step = s * 8 + 4 * half
                tiles = slice(4 * half, 4 * half + 4)
                part = [nmp[:, tiles, :, a].rearrange("p i j -> p (i j)") for a in range(3)]
                if k == 0:
                    upto = NM_A if half == 0 else NMU
                    dve.wait_ge(max_read, s * NMU + upto + C_MAX)
                    dve.tensor_reduce(nm[:, half, :], mx[:, tiles, :, 0:half + 1].rearrange("p i j k -> p (i j) k"), AX.X, ALU.max, negate=True).then_inc(nm_step, 1)
                    return
                dve.wait_ge(nm_step, step + k)
                if k == 1:
                    ge(dve, nm_T, 2 * s + half - 1)
                    dve.tensor_copy(part[0], nm[:, half, :]).then_inc(nm_step, 1)
                if k == 2:
                    dve.tensor_tensor(nmr[:, half, :], nm[:, half, :], part[0], ALU.subtract).then_inc(nm_step, 1)
                if k == 3:
                    dve.tensor_copy(part[1], nmr[:, half, :]).then_inc(nm_step, 1)
                if k == 4:
                    dve.tensor_tensor(part[2], nmr[:, half, :], part[1], ALU.subtract).then_inc(nm_parts, 1)

            def outputs(b, e, g, qc):
                ps = psO[:, qc, :].rearrange("p (t j c) -> p t j c", t=4, j=HG)
                dve.wait_ge(o_T, 2 * e + qc + 1 + C_T)
                dve.reciprocal(rec[:, qc, :, :], ps[:, :, :, DK]).then_inc(rec_done, 1)
                dve.wait_ge(rec_done, 2 * e + qc + 1)
                out = sb["o_tok"][:, bass.ts(b * 2 + qc, 4), g * HG * DK:(g + 1) * HG * DK].rearrange("p t (j d) -> p t j d", d=DK)
                dve.tensor_tensor(out, ps[:, :, :, 0:DK], rec[:, qc, :, :].unsqueeze(3).broadcast_to((P, 4, HG, DK)), ALU.mult).then_inc(o_read, 1)

            def slot(b, e, g, first, more):
                for u in range(NMU):
                    if more:
                        maximum(e + 1, u)
                    if u < 5:
                        cut_maxima(e, 1, u)
                    if u == 14 and not first:
                        outputs(b if g else b - 1, e - 1, (g - 1) % NG, 1)
                    if NM_A <= u < NM_A + 5 and more:
                        cut_maxima(e + 1, 0, u - NM_A)
                    if u == 30:
                        outputs(b, e, g, 0)

            for u in range(NMU):
                maximum(0, u)
                if NM_A <= u < NM_A + 5:
                    cut_maxima(0, 0, u - NM_A)
            slot(0, 0, 0, True, True)
            with dve.Fori(0, B - 1) as b:
                for k in range(1, NG + 1):
                    slot(b + k // NG, b * NG + k, k % NG, False, True)
            for g in range(1, NG):
                slot(B - 1, (B - 1) * NG + g, g, False, g < NG - 1)
            outputs(B - 1, NSTAGE - 1, NG - 1, 1)


def pipelined(eng, n, ring, steps):
    deepest = max(lag for lag, _ in steps)
    first = -(-(deepest + ring) // ring) * ring
    last = n // ring * ring

    def slot(s, place, whole):
        for lag, fn in steps:
            if whole or 0 <= s - lag < n:
                fn(s - lag, (place - lag) % ring)

    first = min(first, last)
    for s in range(first):
        slot(s, s % ring, False)
    if first < last:
        with eng.Fori(first // ring, last // ring) as k:
            for r in range(ring):
                slot(k * ring + r, r, True)
    for s in range(last, n + deepest):
        slot(s, s % ring, False)


def at_least(eng, sem, base, t, k):
    if isinstance(t, int) and t + k <= 0:
        return
    eng.wait_ge(sem, base + t + k)


WINDOW_LOADS = 16 * (4 + 4 * DEPTH)


def load_window_weights(sp, io, sb):
    loads = [(sb["cos"], io["c_cos"]), (sb["sin"], io["c_sin"]), (sb["mask_w"], io["c_mask_w"]), (sb["carry"], io["c_carry"])]
    for l in range(DEPTH):
        loads += [(sb["wqkv"][:, l * 3 * INNER:(l + 1) * 3 * INNER], io["wqkv"][l]),
                  (sb["wo"][:, l * 4 * D:(l + 1) * 4 * D].rearrange("p (c n) -> p c n", n=D), io["wo"][l].rearrange("(c p) n -> p c n", p=P))]
        loads += [(sb["scales"][:, l, w, :], io[name][l:l + 1, :].broadcast_to((P, DH))) for w, name in ((0, "q_scale"), (1, "k_scale"))]
    for dst, src in loads:
        sp.dma_start(dst, src).then_inc(sb["w_in"], 16)


def load_mlp_weights(nc, sp, io, sb, layer):
    w_in, w2, b1 = sb["f_in"], sb["w2"], sb["b1"]
    sp.dma_start(sb["w1"], io["w1"][layer]).then_inc(w_in, 16)
    w2_l = io["w2"][layer]
    sp.dma_start(w2[:, 0:2, :], w2_l[0:2 * HC, :].rearrange("(c p) n -> p c n", p=HC)).then_inc(w_in, 16)
    sp.dma_start(w2[0:HCS[2], 2, :], w2_l[2 * HC:HID, :]).then_inc(w_in, 16)
    b1_l = io["b1"][layer].rearrange("(w n) -> w n", w=2)
    with nc.allow_non_contiguous_dma("a bias to a partition each"):
        for w in range(2):
            for c in range(3):
                sp.dma_start(b1[0:HCS[c], w, c:c + 1], b1_l[w, c * HC:c * HC + HCS[c]].unsqueeze(1)).then_inc(w_in, 16)
        sp.dma_start(sb["lg"], io["ln_g"][layer].unsqueeze(1)).then_inc(w_in, 16)
        sp.dma_start(sb["lb"], io["ln_b"][layer].unsqueeze(1)).then_inc(w_in, 16)
    sp.dma_start(sb["b2"], io["b2"][bass.ds(layer, 1), :].broadcast_to((P, D))).then_inc(w_in, 16)
    sp.dma_start(sb["shift"], io["c_shift"]).then_inc(w_in, 16)
    sp.dma_start(sb["carry_m"], io["c_carry_m"]).then_inc(w_in, 16)


def mix(nc, io, sb):
    with ExitStack() as ctx:
        def tile(name, shape, dt=F32):
            return ctx.enter_context(nc.sbuf_tensor(name, shape, dt))

        def sem(name):
            return ctx.enter_context(nc.semaphore("m_" + name))

        oc = tile("m_oc", [P, 2, 4, P])
        ocT = tile("m_ocT", [P, 2, 4, P])
        stats = tile("m_stats", [P, 2, 4, 4, 6])
        mv = tile("m_mv", [P, 2, 4, 4, 2])
        ve = tile("m_ve", [P, 2, 4, 4])
        rstd = tile("m_rstd", [P, 2, 4, 4])
        shift = tile("m_shift", [P, 2, 4, 4])
        an = tile("m_an", [P, 2, 4, D])
        psT = ctx.enter_context(nc.psum_tensor("m_psT", [P, 2, 512], F32))
        psA = ctx.enter_context(nc.psum_tensor("m_psA", [P, 4, 512], F32))

        w_in, o_staged, oT_done, oT_copied, a_done = sem("w_in"), sem("o_staged"), sem("oT_done"), sem("oT_copied"), sem("a_done")
        stats_done = [sem("stats_a"), sem("stats_x")]
        mean_done = [sem("mean_a"), sem("mean_x")]
        var_done = [sem("var_a"), sem("var_x")]
        rstd_done = [sem("rstd_a"), sem("rstd_x")]
        shift_done = [sem("shift_a"), sem("shift_x")]
        an_done, x1_done, xf_done = sem("an_done"), sem("x1_done"), sem("xf_done")
        block = ctx.enter_context(nc.Block())

        @block.sync
        def _(sp):
            sp.dma_start(sb["w_o"], io["W_o"]).then_inc(w_in, 16)
            load_window_weights(sp, io, sb)

        @block.tensor
        def _(pe):
            pe.wait_ge(w_in, 16)

            def turn(c, r):
                at_least(pe, o_staged, 0, c, 1)
                at_least(pe, oT_copied, 0, c, -1)
                p = r % 2
                for t in range(4):
                    i = pe.transpose(psT[:, p, t * P:(t + 1) * P], oc[:, p, t, :], sb["ident"])
                i.then_inc(oT_done, 1)

            def project_out(c, r):
                at_least(pe, oT_copied, 0, c, 1)
                at_least(pe, an_done, 0, c, -3)
                for t in range(4):
                    i = pe.matmul(psA[:, r, t * P:(t + 1) * P], ocT[:, r % 2, t, :], sb["w_o"], start=True, stop=True)
                i.then_inc(a_done, 1)

            pipelined(pe, NCH, 4, [(1, turn), (1, project_out)])

        @block.scalar
        def _(act):
            def copy(c, r):
                at_least(act, oT_done, 0, c, 1)
                at_least(act, a_done, 0, c, -1)
                act.activation(ocT[:, r % 2, :, :].rearrange("p t c -> p (t c)"), psT[:, r % 2, :], ACT.Copy).then_inc(oT_copied, 1)

            def stage(c, r):
                at_least(act, oT_done, 0, c, -1)
                act.activation(oc[:, r % 2, :, :], sb["o_tok"][:, bass.ts(c, 4), :], ACT.Copy).then_inc(o_staged, 1)

            def normal(w, c, p, outs, ins, done):
                at_least(act, shift_done[w], 0, c, 1)
                for t in range(4):
                    i = act.activation(outs(t), ins(t), ACT.Identity, scale=rstd[:, w, p, t:t + 1], bias=shift[:, w, p, t:t + 1])
                i.then_inc(done, 1)

            def normal_a(c, r):
                at_least(act, x1_done, 0, c, -1)
                normal(0, c, r, lambda t: an[:, r % 2, t, :], lambda t: psA[:, r, t * P:(t + 1) * P], an_done)

            def layers_input(c, r):
                normal(1, c, r, lambda t: sb["xf"][:, c * 4 + t, :], lambda t: sb["x"][:, c * 4 + t, :], xf_done)

            pipelined(act, NCH, 4, [(1, copy), (0, stage), (3, normal_a), (5, layers_input)])

        @block.gpsimd
        def _(pool):
            def powers(w):
                def fn(c, p):
                    at_least(pool, mean_done[w], 0, c, 1)
                    at_least(pool, (an_done, xf_done)[w], 0, c, -3)
                    pool.tensor_tensor(ve[:, w, p, :], mv[:, w, p, :, 1], sb["eps"][:, 0:4], ALU.add).then_inc(var_done[w], 1)
                    at_least(pool, var_done[w], 0, c, 1)
                    pool.tensor_tensor(rstd[:, w, p, :], ve[:, w, p, :], sb["mhalf"][:, 0:4], ALU.pow).then_inc(rstd_done[w], 1)
                return fn

            pipelined(pool, NCH, 4, [(3, powers(1)), (1, powers(0))])

        @block.vector
        def _(dve):
            def shifts(w, c, p):
                at_least(dve, rstd_done[w], 0, c, 1)
                at_least(dve, (an_done, xf_done)[w], 0, c, -3)
                dve.scalar_tensor_tensor(out=shift[:, w, p, :], in0=mv[:, w, p, :, 0], scalar=-1.0, in1=rstd[:, w, p, :],
                                         op0=ALU.mult, op1=ALU.mult).then_inc(shift_done[w], 1)

            def moments(w, c, p, source):
                for t in range(4):
                    i = dve.bn_stats(stats[:, w, p, t, :], source(t))
                i.then_inc(stats_done[w], 1)
                at_least(dve, stats_done[w], 0, c, 1)
                carry_wait(dve, sb)
                for t in range(4):
                    i = dve.bn_aggr(mv[:, w, p, t, :], stats[:, w, p, t, :])
                i.then_inc(mean_done[w], 1)

            def moments_a(c, r):
                at_least(dve, a_done, 0, c, 1)
                moments(0, c, r, lambda t: psA[:, r, t * P:(t + 1) * P])

            def shifts_a(c, r):
                shifts(0, c, r)

            def shifts_x(c, r):
                shifts(1, c, r)

            def residual(c, r):
                p = r % 2
                at_least(dve, an_done, 0, c, 1)
                x = sb["x"][:, bass.ts(c, 4), :]
                dve.tensor_tensor(x, x, an[:, p, :, :], ALU.add).then_inc(x1_done, 1)
                at_least(dve, x1_done, 0, c, 1)
                moments(1, c, r, lambda t: sb["x"][:, c * 4 + t, :])

            pipelined(dve, NCH, 4, [(1, moments_a), (3, residual), (4, shifts_x), (2, shifts_a)])


def window(nc, io, sb, layer):
    base = layer * NT
    with ExitStack() as ctx:
        def tile(name, shape, dt=F32):
            return ctx.enter_context(nc.sbuf_tensor(name, shape, dt))

        def sem(name):
            return ctx.enter_context(nc.semaphore("w_" + name))

        wqkv, wo = sb["wqkv"], sb["wo"]
        cos, sin = tile("w_cos", [P, TB, 2, DH]), tile("w_sin", [P, TB, 2, DH])
        xc = tile("w_xc", [P, 2, D])
        hT = tile("w_hT", [P, 2, P + 1])
        sq = tile("w_sq", [P, 2 * INNER])
        ss, ssm, rn = tile("w_ss", [P, 2, 16]), tile("w_ssm", [P, 2, 16]), tile("w_rn", [P, 2, 16])
        raw = tile("w_raw", [P, 2, 2 * INNER])
        t1, t2 = tile("w_t1", [P, 2 * INNER]), tile("w_t2", [P, 2 * INNER])
        rot = tile("w_rot", [P, 2, 2 * INNER])
        qT, kT = tile("w_qT", [P, 2, 4, P]), tile("w_kT", [P, 2, 4, KEYS])
        v = [tile(f"w_v{r}", [P, INNER]) for r in range(4)]
        vb = [tile(f"w_vb{r}", [P, INNER]) for r in range(4)]
        nmx, bias = tile("w_nmx", [P, 2, HEADS]), tile("w_bias", [P, 2, HEADS])
        den, rden = tile("w_den", [P, 2, HEADS]), tile("w_rden", [P, 2, HEADS])
        prob = tile("w_prob", [P, 2, 2, 4, P])
        pT = tile("w_pT", [P, 2, 4, P])
        oT = tile("w_oT", [P, 4, P])
        psQK = ctx.enter_context(nc.psum_tensor("w_psQK", [P, 2, 512], F32))
        psV = ctx.enter_context(nc.psum_tensor("w_psV", [P, 512], F32))
        psT = ctx.enter_context(nc.psum_tensor("w_psT", [P, 2, 512], F32))
        psS = ctx.enter_context(nc.psum_tensor("w_psS", [P, 2, 512], F32))
        psO = ctx.enter_context(nc.psum_tensor("w_psO", [P, 512], F32))

        w_in, tables, zeroed = sb["w_in"], sem("tables"), sem("zeroed")
        xc_in = [sem("xc_in0"), sem("xc_in1")]
        vb_in = [sem(f"vb_in{r}") for r in range(4)]
        xT_done, hT_copied, carried = sem("xT_done"), sem("hT_copied"), sem("carried")
        qk_done, v_done, sq_done, ss_done, ssm_done, rn_done = (sem(x) for x in ("qk_done", "v_done", "sq_done", "ss_done", "ssm_done", "rn_done"))
        v_copied, raw_done, t1_done, t2_done, rot_done, unit_done = (sem(x) for x in ("v_copied", "raw_done", "t1_done", "t2_done", "rot_done", "unit_done"))
        qkT_done, qT_copied, kT_copied, prev_copied = sem("qkT_done"), sem("qT_copied"), sem("kT_copied"), sem("prev_copied")
        s_done, max_done, bias_done, exp_done = sem("s_done"), sem("max_done"), sem("bias_done"), sem("exp_done")
        rden_done, prob_done = sem("rden_done"), sem("prob_done")
        pT_done, pT_copied = [sem("pT_done0"), sem("pT_done1")], [sem("pT_copied0"), sem("pT_copied1")]
        av_done, oT_copied, y_done, xf_done = sem("av_done"), sem("oT_copied"), sem("y_done"), sem("xf_done")
        block = ctx.enter_context(nc.Block())

        def halves(eng, s, t, k):
            if isinstance(t, int) and 2 * t + k <= 0:
                return
            eng.wait_ge(s, base * 2 + t * 2 + k)

        def slots(eng, slot):
            for s in range(8):
                slot(s, s % 4, False)
            with eng.Fori(2, NT // 4 - 1) as k:
                for r in range(4):
                    slot(k * 4 + r, r, True)
            for s in range(NT - 4, NT + 4):
                slot(s, s % 4, False)

        @block.sync
        def _(sp):
            def load_x(t, r):
                at_least(sp, xT_done, base, t, -1)
                sp.dma_start(xc[:, r % 2, :], sb["xf"][:, t, :]).then_inc(xc_in[r % 2], 16)

            def spread_v(t, r):
                at_least(sp, v_copied, base, t, 1)
                halves(sp, av_done, t, -4)
                sp.dma_start(vb[r][0:WIN, :], v[r][0:WIN, :]).then_inc(vb_in[r], 16)
                sp.dma_start(vb[(r + 1) % 4][WIN:P, :], v[r][WIN:P, :]).then_inc(vb_in[r], 16)

            sp.wait_ge(zeroed, layer * 3 + 3)
            for t in range(2):
                load_x(t, t)
            load_mlp_weights(nc, sp, io, sb, layer)
            def load_later_x(t, r):
                if not isinstance(t, int) or t >= 2:
                    load_x(t, r)

            pipelined(sp, NT, 4, [(0, load_later_x), (2, spread_v)])

        @block.tensor
        def _(pe):
            def turn_x(t, r):
                p = r % 2
                pe.wait_ge(xc_in[p], (base + t - p) * 8 + 16)
                at_least(pe, pT_copied[0], base, t, -4)
                at_least(pe, hT_copied, base, t, 0)
                pe.transpose(psT[:, 0, 0:P], xc[:, p, :], sb["ident"]).then_inc(xT_done, 1)

            def project_qk(t, r, w):
                if w == 0:
                    at_least(pe, hT_copied, base, t, 1)
                    at_least(pe, carried, base, t, 1)
                    at_least(pe, raw_done, base, t, 0)
                pe.matmul(psQK[:, w, :], hT[:, r % 2, 0:P], wqkv[:, bass.ds(layer * (3 * INNER) + w * INNER, INNER)], start=True, stop=True).then_inc(qk_done, 1)

            def project_v(t, r):
                at_least(pe, v_copied, base, t, 0)
                pe.matmul(psV[:, :], hT[:, r % 2, 0:P], wqkv[:, bass.ds(layer * (3 * INNER) + 2 * INNER, INNER)], start=True, stop=True).then_inc(v_done, 1)

            def turn_qk(t, r):
                at_least(pe, unit_done, base, t, 1)
                at_least(pe, hT_copied, base, t, 4 if not isinstance(t, int) else min(4, NT - t))
                at_least(pe, pT_copied[1], base, t, -1)
                for w in range(2):
                    for c in range(4):
                        i = pe.transpose(psT[:, w, c * P:(c + 1) * P], rot[:, r % 2, w * INNER + c * P:w * INNER + (c + 1) * P], sb["ident"])
                i.then_inc(qkT_done, 1)

            def scores(t, r, w):
                p = r % 2
                if w == 0:
                    at_least(pe, qT_copied, base, t, 1)
                    at_least(pe, kT_copied, base, t, 1)
                    at_least(pe, prev_copied, base, t, 1)
                halves(pe, exp_done, t, w - 1)
                pe.matmul(psS[:, w, :].rearrange("p (c k) -> p c k", c=4), sb["ident_b"],
                          sb["mask_w"][:, t % TB, :].unsqueeze(1).broadcast_to((P, 4, P)), start=True, stop=False, skip_group_check=True)
                rows = slice(DH * w, DH * w + DH)
                for c in range(4):
                    cols = slice(c * P, (c + 1) * P)
                    lower = kT[rows, p, c, :].rearrange("p (a k) -> p a k", a=3)[:, 0:3:2, :]
                    pe.matmul(psS[0:WIN, w, cols].rearrange("p (a k) -> p a k", a=2), qT[rows, p, c, 0:WIN], lower,
                              start=False, stop=True, skip_group_check=True)
                    i = pe.matmul(psS[WIN:P, w, cols], qT[rows, p, c, WIN:P], kT[rows, p, c, 0:P], start=False, stop=True, skip_group_check=True)
                i.then_inc(s_done, 1)

            def turn_p(t, r, b):
                p = r % 2
                if b == 0:
                    at_least(pe, prob_done, base, t, 1)
                    for copied in (qT_copied, kT_copied):
                        at_least(pe, copied, base, t, 1 if isinstance(t, int) and t == NT - 1 else 2)
                for i4 in range(4):
                    i = pe.transpose(psT[:, b, i4 * P:(i4 + 1) * P], prob[:, p, i4 % 2, 2 * b + i4 // 2, :], sb["ident"])
                i.then_inc(pT_done[b], 1)

            def values(t, r, b):
                at_least(pe, pT_copied[b], base, t, 1)
                if b == 0:
                    at_least(pe, xf_done, base, t, 0)
                    pe.wait_ge(vb_in[r], (base + t - r) * 8 + 32)
                    if not isinstance(t, int) or t > 0:
                        rb = (r - 1) % 4
                        pe.wait_ge(vb_in[rb], (base + t - 1 - rb) * 8 + 32)
                for u, src in ((0, vb[r]), (1, v[r])):
                    for i4 in range(4):
                        h = 4 * b + i4
                        c, w = h // 2, h % 2
                        i = pe.matmul(psO[DH * w:DH * w + DH, c * P + WIN * u:c * P + WIN * (u + 1)], src[:, h * DH:(h + 1) * DH],
                                      pT[:, b, i4, WIN * u:WIN * (u + 1)], start=True, stop=True, skip_group_check=True)
                i.then_inc(av_done, 1)

            def out(t, r):
                at_least(pe, oT_copied, base, t, 1)
                for c in range(4):
                    i = pe.matmul(psO[:, 0:P], oT[:, c, :], wo[:, bass.ds(layer * (4 * D) + c * D, D)], start=(c == 0), stop=(c == 3), skip_group_check=True)
                i.then_inc(y_done, 1)

            def slot(s, r, whole):
                def runs(t):
                    return whole or 0 <= t < NT
                r2, r3 = (r - 2) % 4, (r - 3) % 4
                if runs(s):
                    project_qk(s, r, 0)
                    project_qk(s, r, 1)
                if runs(s - 2):
                    turn_qk(s - 2, r2)
                if runs(s - 4):
                    out(s - 4, r)
                if runs(s):
                    project_v(s, r)
                if runs(s - 2):
                    scores(s - 2, r2, 0)
                if runs(s - 3):
                    turn_p(s - 3, r3, 0)
                    turn_p(s - 3, r3, 1)
                if runs(s - 2):
                    scores(s - 2, r2, 1)
                if runs(s - 3):
                    values(s - 3, r3, 0)
                if runs(s + 2):
                    turn_x(s + 2, (r + 2) % 4)
                if runs(s - 3):
                    values(s - 3, r3, 1)

            pe.wait_ge(w_in, WINDOW_LOADS)
            turn_x(0, 0)
            turn_x(1, 1)
            slots(pe, slot)

        @block.scalar
        def _(act):
            def copy_hT(t, r):
                p = r % 2
                at_least(act, xT_done, base, t, 1)
                at_least(act, v_done, base, t, -1)
                at_least(act, carried, base, t, 0)
                act.activation(hT[0:WIN, p, 0:P], psT[0:WIN, 0, 0:P], ACT.Copy)
                act.activation(hT[WIN:P, p, 1:P + 1], psT[WIN:P, 0, 0:P], ACT.Copy).then_inc(hT_copied, 1)

            def copy_raw(t, r):
                halves(act, qk_done, t, 2)
                for used in (t1_done, t2_done):
                    at_least(act, used, base, t, -1)
                act.activation(raw[:, r % 2, :].rearrange("p (w n) -> p w n", w=2), psQK[:, :, :], ACT.Copy).then_inc(raw_done, 1)

            def squares(t, r):
                at_least(act, raw_done, base, t, 1)
                at_least(act, ss_done, base, t, 0)
                act.activation(sq[:, :], raw[:, r % 2, :], ACT.Square).then_inc(sq_done, 1)

            def copy_v(t, r):
                at_least(act, v_done, base, t, 1)
                halves(act, av_done, t, -6)
                if not isinstance(t, int) or t >= 4:
                    act.wait_ge(vb_in[r], (base + t - r) * 8)
                act.activation(v[r][:, :], psV[:, :], ACT.Copy).then_inc(v_copied, 1)

            def copy_qT(t, r):
                at_least(act, qkT_done, base, t, 1)
                act.activation(qT[:, r % 2, :, :], psT[:, 0, :].rearrange("p (c n) -> p c n", c=4), ACT.Copy).then_inc(qT_copied, 1)

            def exps(t, r, w):
                p = r % 2
                halves(act, bias_done, t, w + 1)
                for c in range(4):
                    n = 4 * w + c
                    i = act.activation(prob[:, p, w, c, :], psS[:, w, c * P:(c + 1) * P], ACT.Exp,
                                       bias=bias[:, p, n:n + 1], scale=QK_SCALE, accum_out=den[:, p, n:n + 1])
                i.then_inc(exp_done, 1)

            def copy_pT(t, r):
                at_least(act, pT_done[0], base, t, 1)
                halves(act, av_done, t, -1)
                act.activation(pT[:, 0, :, :], psT[:, 0, :].rearrange("p (b n) -> p b n", b=4), ACT.Copy).then_inc(pT_copied[0], 1)

            def copy_oT(t, r):
                halves(act, av_done, t, 2)
                at_least(act, y_done, base, t, 0)
                act.activation(oT[:, :, :], psO[:, :].rearrange("p (c n) -> p c n", c=4), ACT.Copy).then_inc(oT_copied, 1)

            def slot(s, r, whole):
                def runs(t):
                    return whole or 0 <= t < NT
                r2, r3 = (r - 2) % 4, (r - 3) % 4
                if runs(s):
                    copy_raw(s, r)
                if runs(s - 2):
                    copy_qT(s - 2, r2)
                if runs(s):
                    squares(s, r)
                    copy_v(s, r)
                if runs(s - 3):
                    copy_pT(s - 3, r3)
                if runs(s - 2):
                    exps(s - 2, r2, 0)
                if runs(s + 2):
                    copy_hT(s + 2, (r + 2) % 4)
                if runs(s - 3):
                    copy_oT(s - 3, r3)
                if runs(s - 2):
                    exps(s - 2, r2, 1)

            act.wait_ge(zeroed, layer * 3 + 3)
            copy_hT(0, 0)
            copy_hT(1, 1)
            slots(act, slot)

        @block.gpsimd
        def _(pool):
            def rotate(t, r):
                at_least(pool, raw_done, base, t, 1)
                at_least(pool, rot_done, base, t, 0)
                out, src = (x.rearrange("p (w h u d) -> p w h u d", w=2, h=HEADS, u=2) for x in (t2[:, :], raw[:, r % 2, :]))
                for half in range(2):
                    for w in range(2):
                        tab = sin[:, t % TB, w, half * 32:half * 32 + 32].unsqueeze(1).broadcast_to((P, HEADS, 32))
                        i = pool.tensor_tensor(out[:, w, :, half, :], src[:, w, :, 1 - half, :], tab, ALU.mult)
                i.then_inc(t2_done, 1)
                at_least(pool, t1_done, base, t, 1)
                at_least(pool, t2_done, base, t, 1)
                at_least(pool, qkT_done, base, t, -1)
                pool.tensor_tensor(rot[:, r % 2, :], t1[:, :], t2[:, :], ALU.add).then_inc(rot_done, 1)

            def norms(t, r):
                p = r % 2
                at_least(pool, ssm_done, base, t, 1)
                at_least(pool, unit_done, base, t, -1)
                pool.tensor_tensor(rn[:, p, :], ssm[:, p, :], sb["mhalf"][:, 0:16], ALU.pow).then_inc(rn_done, 1)

            pool.wait_ge(tables, layer * 6 + 6)
            pipelined(pool, NT, 4, [(0, rotate), (0, norms)])

        @block.vector
        def _(dve):
            dve.memset(hT[WIN:P, 1, P:P + 1], 0.0).then_inc(zeroed, 1)
            dve.memset(kT[:, 1, :, :], 0.0).then_inc(zeroed, 1)
            dve.memset(vb[0][WIN:P, :], 0.0).then_inc(zeroed, 1)
            dve.wait_ge(w_in, WINDOW_LOADS)
            for w in range(2):
                sc = sb["scales"][:, bass.ds(layer, 1), w, :].broadcast_to((P, TB, DH))
                dve.tensor_tensor(cos[:, :, w, :], sb["cos"][:, :, w, :], sc, ALU.mult).then_inc(tables, 1)
                for half in range(2):
                    sc = sb["scales"][:, bass.ds(layer, 1), w, 32 - 32 * half:64 - 32 * half].broadcast_to((P, TB, 32))
                    part = slice(32 * half, 32 * half + 32)
                    dve.tensor_tensor(sin[:, :, w, part], sb["sin"][:, :, w, part], sc, ALU.mult).then_inc(tables, 1)
            dve.wait_ge(zeroed, layer * 3 + 3)
            dve.wait_ge(tables, layer * 6 + 6)

            def carry(t, r):
                p = r % 2
                at_least(dve, hT_copied, base, t, 0)
                at_least(dve, v_done, base, t, -1)
                dve.tensor_scalar(hT[WIN:P, p, 0:1], hT[WIN:P, 1 - p, P:P + 1], sb["carry"][WIN:P, bass.ds(t % TB, 1)], None,
                                  ALU.mult).then_inc(carried, 1)

            def sums(t, r):
                at_least(dve, sq_done, base, t, 1)
                dve.tensor_reduce(ss[:, r % 2, :], sq[:, :].rearrange("p (h d) -> p h d", d=DH), AX.X, ALU.add).then_inc(ss_done, 1)
                at_least(dve, ss_done, base, t, 1)
                at_least(dve, rn_done, base, t, -1)
                dve.tensor_scalar(ssm[:, r % 2, :], ss[:, r % 2, :], 1e-24, None, ALU.max).then_inc(ssm_done, 1)

            def cosines(t, r):
                at_least(dve, raw_done, base, t, 1)
                at_least(dve, rot_done, base, t, 0)
                dve.tensor_tensor(t1[:, :].rearrange("p (w h d) -> p w h d", w=2, d=DH), raw[:, r % 2, :].rearrange("p (w h d) -> p w h d", w=2, d=DH),
                                  cos[:, t % TB, :, :].unsqueeze(2).broadcast_to((P, 2, HEADS, DH)), ALU.mult).then_inc(t1_done, 1)

            def normalise(t, r):
                p = r % 2
                at_least(dve, rn_done, base, t, 1)
                at_least(dve, rot_done, base, t, 1)
                both = rot[:, p, :].rearrange("p (h d) -> p h d", d=DH)
                dve.tensor_tensor(both, both, rn[:, p, :].unsqueeze(2).broadcast_to((P, 16, DH)), ALU.mult).then_inc(unit_done, 1)

            def copy_kT(t, r):
                p = r % 2
                at_least(dve, qkT_done, base, t, 1)
                at_least(dve, prev_copied, base, t, 0)
                dve.tensor_copy(kT[:, p, :, 0:P], psT[:, 1, :].rearrange("p (c n) -> p c n", c=4)).then_inc(kT_copied, 1)
                halves(dve, s_done, t, -2)
                dve.tensor_copy(kT[:, p, :, P:KEYS], kT[:, 1 - p, :, WIN:P]).then_inc(prev_copied, 1)

            def maxima(t, r, w):
                p = r % 2
                halves(dve, s_done, t, w + 1)
                ns = slice(4 * w, 4 * w + 4)
                dve.tensor_reduce(nmx[:, p, ns], psS[:, w, :].rearrange("p (c k) -> p c k", c=4), AX.X, ALU.max).then_inc(max_done, 1)
                halves(dve, max_done, t, w + 1)
                halves(dve, exp_done, t, w - 3)
                dve.tensor_scalar(bias[:, p, ns], nmx[:, p, ns], -QK_SCALE, None, ALU.mult).then_inc(bias_done, 1)

            def copy_pT(t, r):
                at_least(dve, pT_done[1], base, t, 1)
                halves(dve, av_done, t, 0)
                dve.tensor_copy(pT[:, 1, :, :], psT[:, 1, :].rearrange("p (b n) -> p b n", b=4)).then_inc(pT_copied[1], 1)

            def divide(t, r):
                p = r % 2
                halves(dve, exp_done, t, 2)
                dve.reciprocal(rden[:, p, :], den[:, p, :]).then_inc(rden_done, 1)
                at_least(dve, rden_done, base, t, 1)
                pr = prob[:, p, :, :, :].rearrange("p w c k -> p (w c) k")
                dve.tensor_tensor(pr, pr, rden[:, p, :].unsqueeze(2).broadcast_to((P, HEADS, P)), ALU.mult).then_inc(prob_done, 1)

            def residual(t, r):
                at_least(dve, y_done, base, t, 1)
                dve.tensor_tensor(sb["xf"][:, t, :], sb["xf"][:, t, :], psO[:, 0:P], ALU.add).then_inc(xf_done, 1)

            def slot(s, r, whole):
                def runs(t):
                    return whole or 0 <= t < NT
                r2, r3 = (r - 2) % 4, (r - 3) % 4
                if runs(s - 2):
                    copy_kT(s - 2, r2)
                if runs(s - 3):
                    divide(s - 3, r3)
                if runs(s - 4):
                    residual(s - 4, r)
                if runs(s):
                    cosines(s, r)
                if runs(s - 2):
                    maxima(s - 2, r2, 0)
                if runs(s + 2):
                    carry(s + 2, (r + 2) % 4)
                if runs(s - 3):
                    copy_pT(s - 3, r3)
                if runs(s - 1):
                    normalise(s - 1, (r - 1) % 4)
                if runs(s - 2):
                    maxima(s - 2, r2, 1)
                if runs(s):
                    sums(s, r)

            carry(0, 0)
            carry(1, 1)
            slots(dve, slot)


def mlp(nc, io, sb, layer):
    base = layer * NCH
    with ExitStack() as ctx:
        def tile(name, shape, dt=F32):
            return ctx.enter_context(nc.sbuf_tensor(name, shape, dt))

        def sem(name):
            return ctx.enter_context(nc.semaphore("f_" + name))

        w1, w2, b1, b2, lg, lb, shift, carry = (sb[x] for x in ("w1", "w2", "b1", "b2", "lg", "lb", "shift", "carry_m"))
        stats, mv = tile("f_stats", [P, 2, 4, 2, 6]), tile("f_mv", [P, 2, 4, 2])
        ve, rstd = tile("f_ve", [P, 2, 4]), tile("f_rstd", [P, 2, 4])
        hn, hT = tile("f_hn", [P, 2, 4, D]), tile("f_hT", [P, 2, 512])
        gate, act_t = tile("f_gate", [HC, 3, 512]), tile("f_act", [HC, 2, 3, 512])
        last = tile("f_last", [P, NCH + 1, WIN])
        psH = ctx.enter_context(nc.psum_tensor("f_psH", [P, 2, 512], F32))
        psT = ctx.enter_context(nc.psum_tensor("f_psT", [P, 512], F32))
        psU = ctx.enter_context(nc.psum_tensor("f_psU", [P, 3, 512], F32))
        psY = ctx.enter_context(nc.psum_tensor("f_psY", [P, 2, 512], F32))

        w_in, last_set = sb["f_in"], sem("last_set")
        shifted, stats_done, mean_done, var_done, rstd_done = (sem(x) for x in ("shifted", "stats_done", "mean_done", "var_done", "rstd_done"))
        hn_done, hnT_done, hT_done, u_done, gate_done, act_done = (sem(x) for x in ("hn_done", "hnT_done", "hT_done", "u_done", "gate_done", "act_done"))
        y_done, y_added, xf_done = sem("y_done"), sem("y_added"), sem("xf_done")
        block = ctx.enter_context(nc.Block())
        def units(eng, s, c, k, per=3):
            if isinstance(c, int) and per * c + k <= 0:
                return
            eng.wait_ge(s, base * per + c * per + k)

        LOADS = 16 * 14

        @block.tensor
        def _(pe):
            def shift_half(c, r):
                p = r % 2
                at_least(pe, hn_done, base, c, -1)
                out = psH[:, p, 0:4 * WIN].rearrange("p (t d) -> p t d", t=4)
                pe.matmul(out, shift[:, :], sb["xf"][:, bass.ts(c, 4), WIN:D], start=True, stop=False, skip_group_check=True)
                pe.matmul(out[:, 0, :], carry[:, :], last[:, c, :], start=False, stop=False, skip_group_check=True)
                pe.matmul(out[:, 1:4, :], carry[:, :], sb["xf"][:, bass.ds(c * 4, 3), WIN:D], start=False, stop=True, skip_group_check=True).then_inc(shifted, 1)

            def turn(c, r):
                at_least(pe, hn_done, base, c, 1)
                at_least(pe, hT_done, base, c, 0)
                for t in range(4):
                    i = pe.transpose(psT[:, t * P:(t + 1) * P], hn[:, r % 2, t, :], sb["ident"])
                i.then_inc(hnT_done, 1)

            def up(c, r):
                at_least(pe, hT_done, base, c, 1)
                n = 0
                for m in range(3):
                    for w in (1, 0):
                        units(pe, gate_done if (n - 3) % 2 == 0 else act_done, c, (n - 3) // 2 + 1)
                        M = HCS[m]
                        pe.matmul(psU[0:M, n % 3, :], w1[:, w * HID + m * HC:w * HID + m * HC + M], hT[:, r % 2, :],
                                  start=True, stop=True).then_inc(u_done, 1)
                        n += 1

            def down(c, r):
                p = r % 2
                units(pe, act_done, c, 3)
                at_least(pe, y_added, base, c, -1)
                for t in range(4):
                    for m in range(3):
                        M = HCS[m]
                        i = pe.matmul(psY[:, p, t * P:(t + 1) * P], act_t[0:M, p, m, t * P:(t + 1) * P], w2[0:M, m, :],
                                      start=(m == 0), stop=(m == 2))
                i.then_inc(y_done, 1)

            pe.wait_ge(w_in, (layer + 1) * LOADS)
            pe.wait_ge(last_set, (layer + 1) * 3)
            pipelined(pe, NCH, 2, [(0, shift_half), (3, down), (1, turn), (2, up)])

        @block.gpsimd
        def _(pool):
            def powers(c, r):
                p = r % 2
                at_least(pool, mean_done, base, c, 1)
                pool.tensor_tensor(ve[:, p, :], mv[:, p, :, 1], sb["eps"][:, 0:4], ALU.add).then_inc(var_done, 1)
                at_least(pool, var_done, base, c, 1)
                pool.tensor_tensor(rstd[:, p, :], ve[:, p, :], sb["mhalf"][:, 0:4], ALU.pow).then_inc(rstd_done, 1)

            pipelined(pool, NCH, 2, [(0, powers)])

        @block.scalar
        def _(act):
            act.wait_ge(w_in, (layer + 1) * LOADS)

            def affine(c, r):
                at_least(act, hnT_done, base, c, 1)
                units(act, u_done, c, -6, 6)
                act.activation(hT[:, r % 2, :], psT[:, :], ACT.Identity, scale=lg[:, 0:1], bias=lb[:, 0:1]).then_inc(hT_done, 1)

            def gelu(c, r):
                for m in range(3):
                    M = HCS[m]
                    units(act, u_done, c, 2 * m + 1, 6)
                    units(act, act_done, c, m - 2)
                    act.activation(gate[0:M, m, :], psU[0:M, (2 * m) % 3, :], ACT.Gelu, bias=b1[0:M, 1, m:m + 1]).then_inc(gate_done, 1)

            pipelined(act, NCH, 2, [(1, affine), (2, gelu)])

        @block.vector
        def _(dve):
            def statistics(c, r):
                p = r % 2
                at_least(dve, shifted, base, c, 1)
                for t in range(4):
                    dve.bn_stats(stats[:, p, t, 0, :], sb["xf"][:, c * 4 + t, 0:WIN])
                    i = dve.bn_stats(stats[:, p, t, 1, :], psH[:, p, t * WIN:(t + 1) * WIN])
                i.then_inc(stats_done, 1)
                at_least(dve, stats_done, base, c, 1)
                carry_wait(dve, sb)
                for t in range(4):
                    i = dve.bn_aggr(mv[:, p, t, :], stats[:, p, t, :, :].rearrange("p a b -> p (a b)"))
                i.then_inc(mean_done, 1)

            def norm(c, r):
                p = r % 2
                at_least(dve, rstd_done, base, c, 1)
                at_least(dve, hnT_done, base, c, -1)
                for t in range(4):
                    dve.tensor_scalar(hn[:, p, t, 0:WIN], sb["xf"][:, c * 4 + t, 0:WIN], mv[:, p, t, 0:1], rstd[:, p, t:t + 1], ALU.subtract, ALU.mult)
                    i = dve.tensor_scalar(hn[:, p, t, WIN:D], psH[:, p, t * WIN:(t + 1) * WIN], mv[:, p, t, 0:1], rstd[:, p, t:t + 1], ALU.subtract, ALU.mult)
                i.then_inc(hn_done, 1)

            def gated(c, r):
                p = r % 2
                for m in range(3):
                    M = HCS[m]
                    units(dve, u_done, c, 2 * m + 2, 6)
                    units(dve, gate_done, c, m + 1)
                    if m == 0:
                        at_least(dve, y_done, base, c, -1)
                    dve.scalar_tensor_tensor(out=act_t[0:M, p, m, :], in0=psU[0:M, (2 * m + 1) % 3, :], scalar=b1[0:M, 0, m:m + 1],
                                             in1=gate[0:M, m, :], op0=ALU.add, op1=ALU.mult).then_inc(act_done, 1)

            def residual(c, r):
                xs = sb["xf"][:, bass.ts(c, 4), :]
                at_least(dve, y_done, base, c, 1)
                dve.tensor_tensor(xs, xs, psY[:, r % 2, :].rearrange("p (t n) -> p t n", t=4), ALU.add).then_inc(y_added, 1)
                at_least(dve, y_added, base, c, 1)
                dve.tensor_tensor(xs, xs, b2[:, :].unsqueeze(1).broadcast_to((P, 4, D)), ALU.add).then_inc(xf_done, 1)

            dve.memset(last[:, :, :], 0.0).then_inc(last_set, 1)
            dve.wait_ge(last_set, layer * 3 + 1)
            src = sb["xf"].rearrange("p (b u t) n -> p b u t n", b=B, u=2)[:, :, 0, 3, WIN:D]
            dst = last[:, 0:NCH, :].rearrange("p (b u) n -> p b u n", u=2)[:, :, 1, :]
            dve.tensor_copy(dst, src).then_inc(last_set, 2)
            dve.wait_ge(w_in, (layer + 1) * LOADS)
            pipelined(dve, NCH, 2, [(3, residual), (0, statistics), (2, gated), (0, norm)])


def last_norm(nc, io, sb):
    with ExitStack() as ctx:
        def tile(name, shape, dt=F32):
            return ctx.enter_context(nc.sbuf_tensor(name, shape, dt))

        def sem(name):
            return ctx.enter_context(nc.semaphore("l_" + name))

        stats, mv = tile("l_stats", [P, 2, 4, 6]), tile("l_mv", [P, 2, 4, 2])
        ve, rstd = tile("l_ve", [P, 2, 4]), tile("l_rstd", [P, 2, 4])
        yn, y = tile("l_yn", [P, 2, 4, D]), tile("l_y", [P, 2, 4, D])
        stats_done, mean_done, var_done, rstd_done, yn_done, y_done = (sem(x) for x in ("stats_done", "mean_done", "var_done", "rstd_done", "yn_done", "y_done"))
        y_out = [sem("y_out0"), sem("y_out1")]
        block = ctx.enter_context(nc.Block())
        out_v = io["out"].rearrange("b (t p) c -> p (b t) c", p=P)

        @block.sync
        def _(sp):
            with sp.Fori(0, NCH // 2) as pair:
                for p in range(2):
                    c = pair * 2 + p
                    sp.wait_ge(y_done, c + 1)
                    sp.dma_start(out_v[:, bass.ts(c, 4), :], y[:, p, :, :]).then_inc(y_out[p], 16)
            for p in range(2):
                sp.wait_ge(y_out[p], 16 * (NCH // 2))

        @block.gpsimd
        def _(pool):
            def powers(c, r):
                p = r % 2
                at_least(pool, mean_done, 0, c, 1)
                pool.tensor_tensor(ve[:, p, :], mv[:, p, :, 1], sb["eps"][:, 0:4], ALU.add).then_inc(var_done, 1)
                at_least(pool, var_done, 0, c, 1)
                pool.tensor_tensor(rstd[:, p, :], ve[:, p, :], sb["mhalf"][:, 0:4], ALU.pow).then_inc(rstd_done, 1)

            pipelined(pool, NCH, 2, [(0, powers)])

        @block.vector
        def _(dve):
            def moments(c, r):
                p = r % 2
                for t in range(4):
                    i = dve.bn_stats(stats[:, p, t, :], sb["xf"][:, c * 4 + t, :])
                i.then_inc(stats_done, 1)
                at_least(dve, stats_done, 0, c, 1)
                carry_wait(dve, sb)
                for t in range(4):
                    i = dve.bn_aggr(mv[:, p, t, :], stats[:, p, t, :])
                i.then_inc(mean_done, 1)

            def finish(c, r):
                p = r % 2
                at_least(dve, rstd_done, 0, c, 1)
                for t in range(4):
                    i = dve.tensor_scalar(yn[:, p, t, :], sb["xf"][:, c * 4 + t, :], mv[:, p, t, 0:1], rstd[:, p, t:t + 1], ALU.subtract, ALU.mult)
                i.then_inc(yn_done, 1)
                at_least(dve, yn_done, 0, c, 1)
                if not isinstance(c, int) or c >= 2:
                    dve.wait_ge(y_out[p], (c - p) * 8)
                dve.tensor_tensor(y[:, p, :, :], yn[:, p, :, :], sb["x"][:, bass.ts(c, 4), :], ALU.add).then_inc(y_done, 1)

            pipelined(dve, NCH, 2, [(0, moments), (1, finish)])


def latent_attention_and_window_layers(nc, io):
    io["q_parts"] = nc.dram_tensor("q_parts", (B, NG, 3, DK, HG, S), BF16).ap()
    io["k_parts"] = nc.dram_tensor("k_parts", (B, NG, DK, 3, HG, S), BF16).ap()
    with ExitStack() as ctx:
        def tile(name, shape, dt=F32):
            return ctx.enter_context(nc.sbuf_tensor(name, shape, dt))

        sb = {
            "x": tile("x_sb", [P, NT, D])[:, :, :],
            "ident": tile("ident", [P, P])[:, :],
            "ident_b": tile("ident_b", [P, P], BF16)[:, :],
            "mhalf": tile("mhalf", [P, 16])[:, :],
            "eps": tile("eps", [P, 16])[:, :],
            "spare": tile("spare", [P, 1])[:, :],
            "carry": tile("carry", [P, TB])[:, :],
            "xf": tile("xf_sb", [P, NT, D])[:, :, :],
            "o_tok": tile("o_tok", [P, NT, D])[:, :, :],
            "w_o": tile("w_o", [P, D])[:, :],
        }
        with ExitStack() as first:
            def early(name, shape, dt=F32):
                return first.enter_context(nc.sbuf_tensor(name, shape, dt))[:]

            sb["mask_q"] = early("mask_q", [P, P], BF16)
            sb["mask_k"] = early("mask_k", [P, P], BF16)
            sb["w_down"] = early("w_down", [P, 2 * DC])
            sb["w_uq"] = early("w_uq", [DC, D])
            sb["w_ukv"] = early("w_ukv", [2 * DC, 2 * D])
            sb["v_all"] = early("v_all", [P, NG, NT, HG * VA])
            sb["qs"] = early("a_qs", [KROWS, NG, HG, S], BF16)
            sb["ks"] = early("a_ks", [KROWS, NG, HG, S], BF16)
            sb["vs"] = [early(f"a_vs{g}", [P, TB * HG * VA + VPAD]) for g in range(NG)]
            sb["const_in"] = ctx.enter_context(nc.semaphore("const_in"))
            sb["parts"] = early("p_parts", [P, 2, 2, 3, 512], BF16)
            sb["parts_out"] = [ctx.enter_context(nc.semaphore(f"parts_out{par}")) for par in range(2)]
            sb["stack_in"] = [ctx.enter_context(nc.semaphore(f"stack_in{g}")) for g in range(NG)]
            project(nc, io, sb)
            attend(nc, io, sb)
        sb["mask_w"] = tile("mask_w", [P, TB, P], BF16)[:, :, :]
        sb["wqkv"], sb["wo"] = tile("w_wqkv", [P, DEPTH * 3 * INNER])[:, :], tile("w_wo", [P, DEPTH * 4 * D])[:, :]
        sb["scales"] = tile("w_scales", [P, DEPTH, 2, DH])[:, :, :, :]
        sb["cos"], sb["sin"] = tile("cos_given", [P, TB, 2, DH])[:, :, :, :], tile("sin_given", [P, TB, 2, DH])[:, :, :, :]
        sb["w_in"], sb["f_in"] = ctx.enter_context(nc.semaphore("w_w_in")), ctx.enter_context(nc.semaphore("f_w_in"))
        sb["w1"], sb["w2"] = tile("f_w1", [P, 2 * HID])[:, :], tile("f_w2", [HC, 3, D])[:, :, :]
        sb["b1"], sb["b2"] = tile("f_b1", [HC, 2, 3])[:, :, :], tile("f_b2", [P, D])[:, :]
        sb["lg"], sb["lb"] = tile("f_lg", [P, 1])[:, :], tile("f_lb", [P, 1])[:, :]
        sb["shift"], sb["carry_m"] = tile("f_shift", [P, P])[:, :], tile("f_carry", [P, P])[:, :]
        mix(nc, io, sb)
        with nc.Fori(0, DEPTH) as layer:
            window(nc, io, sb, layer)
            mlp(nc, io, sb, layer)
        last_norm(nc, io, sb)


def constants():
    bf, f = mybir.dt.np(BF16), np.float32
    c = {"c_ident": np.eye(P, dtype=f), "c_ident_b": np.eye(P).astype(bf)}
    i, j = np.arange(P)[:, None], np.arange(P)[None, :]
    c["c_mask_q"] = np.where(j > i, NEG, 0.0).astype(bf)
    c["c_mask_k"] = np.where(i > j, NEG, 0.0).astype(bf)
    c["c_zero"] = np.zeros((KROWS - ROWS, HG, S), bf)
    sel = np.zeros((KROWS - ROWS, NG, HG, S), bf)
    for h in range(HG):
        sel[3 * h:3 * h + 3, :, h, :] = 1
    c["c_sel"] = sel
    key = np.where((j >= WIN) & (i < WIN), j - 2 * WIN, j)
    ok = (key <= i) & (i <= key + WIN)
    mask = np.broadcast_to(ok[:, None, :], (P, TB, P)).copy()
    mask[:WIN, 0, WIN:] = False
    c["c_mask_w"] = np.where(mask, 0.0, NEG).astype(bf)
    c["c_carry"] = np.broadcast_to((np.arange(TB) > 0).astype(f), (P, TB)).copy()
    c["c_shift"] = np.eye(P, k=1, dtype=f)
    c["c_carry_m"] = np.zeros((P, P), f)
    c["c_carry_m"][P - 1, 0] = 1
    half = np.arange(0, DH, 2, dtype=f)
    inv = (f(1.0) / np.power(f(10000.0), half / f(DH))).astype(f)
    t = np.arange(S, dtype=f)
    freqs = (t[:, None] * inv[None, :]).astype(f)
    base = ((half + f(0.4 * DH)) / f(1.4 * DH)).astype(f)
    power = ((t - f(S // 2)) / f(WIN // 2)).astype(f)
    scale = np.power(base[None, :], power[:, None]).astype(f)
    cos, sin = np.cos(freqs).astype(f), np.sin(freqs).astype(f)
    two = lambda a, b: np.concatenate([a, b], axis=-1)
    cosines = np.stack([two(cos * scale, cos * scale), two(cos / scale, cos / scale)], 1)
    sines = np.stack([two(-sin * scale, sin * scale), two(-sin / scale, sin / scale)], 1)
    for name, x in (("c_cos", cosines), ("c_sin", sines)):
        c[name] = np.ascontiguousarray(x.reshape(TB, P, 2, DH).transpose(1, 0, 2, 3).astype(f))
    return c


_INS = {"x": "L0_attn_x", "W_dq": "L0_attn_W_dq", "W_uq": "L0_attn_W_uq", "W_dkv": "L0_attn_W_dkv",
        "W_uk": "L0_attn_W_uk", "W_uv": "L0_attn_W_uv", "W_o": "L0_attn_W_o", "wqkv": "L0_ffn_wqkv",
        "q_scale": "L0_ffn_q_scale", "k_scale": "L0_ffn_k_scale", "wo": "L0_ffn_wo", "ln_g": "L0_ffn_ln_g",
        "ln_b": "L0_ffn_ln_b", "w1": "L0_ffn_w1", "b1": "L0_ffn_b1", "w2": "L0_ffn_w2", "b2": "L0_ffn_b2"}


def kernel(**inputs):
    import concourse.bacc as bacc
    from concourse.bass_utils import run_bass_kernel_spmd as run

    nc = bacc.Bacc("TRN2", target_bir_lowering=False, num_devices=1)
    nc.disable_value_cache = True
    arrays, io = {}, {}
    given = {short: np.ascontiguousarray(inputs[name]) for short, name in _INS.items()}
    for short, a in {**given, **constants()}.items():
        arrays["in_" + short] = a
        io[short] = nc.dram_tensor("in_" + short, a.shape, mybir.dt.from_np(a.dtype), kind="ExternalInput").ap()
    io["out"] = nc.dram_tensor("out_x", (B, S, D), F32, kind="ExternalOutput").ap()
    latent_attention_and_window_layers(nc, io)
    return run(nc, [arrays], core_ids=[0]).results[0]["out_x"]
```
